# Optimizing a Trainium2 kernel written in Bass

```python
import numpy as np
import jax
import jax.numpy as jnp

def _softmax(x, axis=-1):
    return jax.nn.softmax(x, axis=axis)

def _gelu(x):
    return jax.nn.gelu(x, approximate=True)

def _silu(x):
    return jax.nn.silu(x)

def _sigmoid(x):
    return jax.nn.sigmoid(x)

def _layernorm(x, axis=-1, eps=1e-05):
    m = jnp.mean(x, axis=axis, keepdims=True)
    v = jnp.var(x, axis=axis, keepdims=True)
    return (x - m) / jnp.sqrt(v + eps)

def _scatter_add(tgt, idx, src, axis=0):
    return tgt.at[idx].add(src)

def _segment_sum(src, seg, n):
    return jax.ops.segment_sum(src, seg, n)
kernel_name = 'mk_flamingo_gated_d2_seqx_r4_3dfaa7'

def setup_inputs(seed: int=0):
    np.random.seed(seed)
    _w = jnp.asarray

    def _rec_inputs():
        import jax
        import jax.numpy as jnp
        _rk = jax.random.key(seed)
        x = -0.0003929 + 0.9999 * jax.random.normal(jax.random.fold_in(_rk, 1), (16, 256, 256), jnp.float32)
        _lenS = 256 - jax.random.randint(jax.random.fold_in(_rk, 7), (16,), 0, max(1, 256 // 4) + 1, jnp.int32)
        _lenS2 = 256 - jax.random.randint(jax.random.fold_in(_rk, 8), (16,), 0, max(1, 256 // 4) + 1, jnp.int32)
        _ctx_1024P = jax.random.normal(jax.random.fold_in(_rk, 11), (16, 16, 256), jnp.float32)
        _ctx_1024c = jax.random.dirichlet(jax.random.fold_in(_rk, 511), 0.3 * jnp.ones((16,), jnp.float32), (16, 256))
        _ctx_1024t = jnp.einsum('bsk,bkd->bsd', _ctx_1024c, _ctx_1024P)
        _ctx_1024t = _ctx_1024t * jax.lax.rsqrt(jnp.mean(jnp.square(_ctx_1024t)) + 1e-12) * 0.953939
        ctx_1024 = 2.81802e-05 + 1.00001 * (_ctx_1024t + 0.3 * jax.random.normal(jax.random.fold_in(_rk, 611), (16, 256, 256), jnp.float32))
        _g = jax.random.normal(jax.random.fold_in(_rk, 9001), (2, 2), jnp.float32)
        _g = jnp.sign(_g) * jnp.maximum(jnp.abs(_g), 1.0) + (_g == 0) * 1.0
        g_xattn = _g[0]
        g_ffn = _g[1]
        return (x, ctx_1024, g_xattn, g_ffn)
    x, ctx_1024, g_xattn, g_ffn = _rec_inputs()

    def _L0_xattn_setup():
        import math
        import jax, jax.numpy as jnp
        import numpy as np
        D_MODEL = 256
        N_HEADS = 16
        D_K = D_MODEL // N_HEADS

        def _autocorr_forward(queries, keys, values, Wq, bq, Wk, bk, Wv, bv, Wo, bo):
            B, L, D = queries.shape
            H, dk = (N_HEADS, D_K)
            q = (queries @ Wq.T + bq).reshape(B, L, H, dk)
            k = (keys @ Wk.T + bk).reshape(B, L, H, dk)
            v = (values @ Wv.T + bv).reshape(B, L, H, dk)
            qf = jnp.fft.rfft(q, axis=1)
            kf = jnp.fft.rfft(k, axis=1)
            corr = jnp.fft.irfft(qf * jnp.conj(kf), n=L, axis=1).mean(axis=-1)
            corr = corr.transpose(0, 2, 1)
            topk = min(max(1, int(math.log(L))), L)
            weights, delays = jax.lax.top_k(corr, topk)
            w = jax.nn.softmax(weights, axis=-1)
            idx = (jnp.arange(L)[None, None, None, :] - delays[..., None]) % L
            v_h = v.transpose(0, 2, 1, 3)
            gathered = jnp.take_along_axis(v_h[:, :, None], idx[..., None], axis=3)
            out = (w[..., None, None] * gathered).sum(axis=2)
            out = out.transpose(0, 2, 1, 3).reshape(B, L, D)
            return out @ Wo.T + bo
        key = jax.random.key(seed)
        ks = jax.random.split(key, 12)
        B, L, D = (8, 512, D_MODEL)
        scale = 1.0 / math.sqrt(D)
        inp = {'queries': jax.random.normal(ks[0], (B, L, D), jnp.float32), 'keys': jax.random.normal(ks[1], (B, L, D), jnp.float32), 'values': jax.random.normal(ks[2], (B, L, D), jnp.float32), 'Wq': jax.random.normal(ks[3], (D, D), jnp.float32) * scale, 'bq': jnp.zeros((D,), jnp.float32), 'Wk': jax.random.normal(ks[4], (D, D), jnp.float32) * scale, 'bk': jnp.zeros((D,), jnp.float32), 'Wv': jax.random.normal(ks[5], (D, D), jnp.float32) * scale, 'bv': jnp.zeros((D,), jnp.float32), 'Wo': jax.random.normal(ks[6], (D, D), jnp.float32) * scale, 'bo': jnp.zeros((D,), jnp.float32)}
        return inp
    _L0_xattn_all = _L0_xattn_setup()
    _L0_xattn_in = {k: v for k, v in _L0_xattn_all.items() if k in ('Wq', 'bq', 'Wk', 'bk', 'Wv', 'bv', 'Wo', 'bo')}
    del _L0_xattn_all

    def _L0_ffn_setup():
        import jax, jax.numpy as jnp
        import numpy as np
        B, S, H, DFF, E, K = (2, 512, 256, 512, 8, 2)

        def _moe(x, Wg, W1, b1, W2, b2, W3, b3):
            Bm, Sm, Hm = x.shape
            xt = x.reshape(-1, Hm)
            gout = xt @ Wg.T
            topv, topi = jax.lax.top_k(gout, K)
            w = jax.nn.softmax(topv, axis=-1)
            comb = jnp.einsum('tke,tk->te', jax.nn.one_hot(topi, E, dtype=x.dtype), w)
            g = jnp.einsum('th,efh->etf', xt, W1) + b1[:, None, :]
            v = jnp.einsum('th,efh->etf', xt, W2) + b2[:, None, :]
            h = jax.nn.silu(g) * v
            eo = jnp.einsum('etf,ehf->eth', h, W3) + b3[:, None, :]
            out = jnp.einsum('eth,te->th', eo, comb)
            return out.reshape(Bm, Sm, Hm)
        key = jax.random.key(seed)
        ks = jax.random.split(key, 8)
        sc_h = 1.0 / np.sqrt(H)
        sc_f = 1.0 / np.sqrt(DFF)
        x = jax.random.normal(ks[0], (B, S, H), dtype=jnp.float32)
        Wg = jax.random.uniform(ks[1], (E, H), jnp.float32, -sc_h, sc_h)
        W1 = jax.random.uniform(ks[2], (E, DFF, H), jnp.float32, -sc_h, sc_h)
        b1 = jax.random.uniform(ks[3], (E, DFF), jnp.float32, -sc_h, sc_h)
        W2 = jax.random.uniform(ks[4], (E, DFF, H), jnp.float32, -sc_h, sc_h)
        b2 = jax.random.uniform(ks[5], (E, DFF), jnp.float32, -sc_h, sc_h)
        W3 = jax.random.uniform(ks[6], (E, H, DFF), jnp.float32, -sc_f, sc_f)
        b3 = jax.random.uniform(ks[7], (E, H), jnp.float32, -sc_f, sc_f)
        return {'x': x, 'Wg': Wg, 'W1': W1, 'b1': b1, 'W2': W2, 'b2': b2, 'W3': W3, 'b3': b3}
    _L0_ffn_all = _L0_ffn_setup()
    _L0_ffn_in = {k: v for k, v in _L0_ffn_all.items() if k in ('Wg', 'W1', 'b1', 'W2', 'b2', 'W3', 'b3')}
    del _L0_ffn_all

    def _L1_xattn_setup():
        import jax, jax.numpy as jnp
        import numpy as np
        B, N, L, D, H = (8, 128, 1024, 256, 16)
        key = jax.random.key(seed)
        ks = jax.random.split(key, 7)
        s = 1.0 / np.sqrt(D)
        return {'q': jax.random.normal(ks[0], (B, N, D), dtype=jnp.float32), 'k': jax.random.normal(ks[1], (B, L, D), dtype=jnp.float32), 'v': jax.random.normal(ks[2], (B, L, D), dtype=jnp.float32), 'Wq': jax.random.normal(ks[3], (D, D), dtype=jnp.float32) * s, 'Wk': jax.random.normal(ks[4], (D, D), dtype=jnp.float32) * s, 'Wv': jax.random.normal(ks[5], (D, D), dtype=jnp.float32) * s, 'Wo': jax.random.normal(ks[6], (D, D), dtype=jnp.float32) * s}
    _L1_xattn_all = _L1_xattn_setup()
    _L1_xattn_in = {k: v for k, v in _L1_xattn_all.items() if k in ('Wq', 'Wk', 'Wv', 'Wo')}
    del _L1_xattn_all

    def _L1_ffn_setup():
        import jax, jax.numpy as jnp
        import numpy as np
        DIM = 256
        HID = 2 * DIM
        NUM_EXPERTS = 8
        TOP_K = 2
        BATCH, SEQ = (2, 512)

        def _gelu(x):
            return jax.nn.gelu(x, approximate=False)
        key = jax.random.key(seed)
        ks = jax.random.split(key, 8)
        s = 0.02
        return {'x': jax.random.normal(ks[0], (BATCH, SEQ, DIM), jnp.float32), 'router_w': jax.random.normal(ks[1], (DIM, NUM_EXPERTS), jnp.float32) * s, 'router_b': jnp.zeros((NUM_EXPERTS,), jnp.float32), 'sw1': jax.random.normal(ks[2], (DIM, HID), jnp.float32) * s, 'sb1': jnp.zeros((HID,), jnp.float32), 'sw2': jax.random.normal(ks[3], (HID, DIM), jnp.float32) * s, 'sb2': jnp.zeros((DIM,), jnp.float32), 'ew1': jax.random.normal(ks[4], (NUM_EXPERTS, DIM, HID), jnp.float32) * s, 'eb1': jnp.zeros((NUM_EXPERTS, HID), jnp.float32), 'ew2': jax.random.normal(ks[5], (NUM_EXPERTS, HID, DIM), jnp.float32) * s, 'eb2': jnp.zeros((NUM_EXPERTS, DIM), jnp.float32)}
    _L1_ffn_all = _L1_ffn_setup()
    _L1_ffn_in = {k: v for k, v in _L1_ffn_all.items() if k in ('router_w', 'router_b', 'sw1', 'sb1', 'sw2', 'sb2', 'ew1', 'eb1', 'ew2', 'eb2')}
    del _L1_ffn_all
    return {'x': x, 'ctx_1024': ctx_1024, 'g_xattn': g_xattn, 'g_ffn': g_ffn, 'L0_xattn_Wq': _L0_xattn_in['Wq'], 'L0_xattn_bq': _L0_xattn_in['bq'], 'L0_xattn_Wk': _L0_xattn_in['Wk'], 'L0_xattn_bk': _L0_xattn_in['bk'], 'L0_xattn_Wv': _L0_xattn_in['Wv'], 'L0_xattn_bv': _L0_xattn_in['bv'], 'L0_xattn_Wo': _L0_xattn_in['Wo'], 'L0_xattn_bo': _L0_xattn_in['bo'], 'L0_ffn_Wg': _L0_ffn_in['Wg'], 'L0_ffn_W1': _L0_ffn_in['W1'], 'L0_ffn_b1': _L0_ffn_in['b1'], 'L0_ffn_W2': _L0_ffn_in['W2'], 'L0_ffn_b2': _L0_ffn_in['b2'], 'L0_ffn_W3': _L0_ffn_in['W3'], 'L0_ffn_b3': _L0_ffn_in['b3'], 'L1_xattn_Wq': _L1_xattn_in['Wq'], 'L1_xattn_Wk': _L1_xattn_in['Wk'], 'L1_xattn_Wv': _L1_xattn_in['Wv'], 'L1_xattn_Wo': _L1_xattn_in['Wo'], 'L1_ffn_router_w': _L1_ffn_in['router_w'], 'L1_ffn_router_b': _L1_ffn_in['router_b'], 'L1_ffn_sw1': _L1_ffn_in['sw1'], 'L1_ffn_sb1': _L1_ffn_in['sb1'], 'L1_ffn_sw2': _L1_ffn_in['sw2'], 'L1_ffn_sb2': _L1_ffn_in['sb2'], 'L1_ffn_ew1': _L1_ffn_in['ew1'], 'L1_ffn_eb1': _L1_ffn_in['eb1'], 'L1_ffn_ew2': _L1_ffn_in['ew2'], 'L1_ffn_eb2': _L1_ffn_in['eb2']}

def reference(x, ctx_1024, g_xattn, g_ffn, L0_xattn_Wq, L0_xattn_bq, L0_xattn_Wk, L0_xattn_bk, L0_xattn_Wv, L0_xattn_bv, L0_xattn_Wo, L0_xattn_bo, L0_ffn_Wg, L0_ffn_W1, L0_ffn_b1, L0_ffn_W2, L0_ffn_b2, L0_ffn_W3, L0_ffn_b3, L1_xattn_Wq, L1_xattn_Wk, L1_xattn_Wv, L1_xattn_Wo, L1_ffn_router_w, L1_ffn_router_b, L1_ffn_sw1, L1_ffn_sb1, L1_ffn_sw2, L1_ffn_sb2, L1_ffn_ew1, L1_ffn_eb1, L1_ffn_ew2, L1_ffn_eb2):
    import jax
    import jax.numpy as jnp

    def _L0_xattn_ref(queries, keys, values, Wq, bq, Wk, bk, Wv, bv, Wo, bo):
        import math
        import jax, jax.numpy as jnp
        import numpy as np
        D_MODEL = 256
        N_HEADS = 16
        D_K = D_MODEL // N_HEADS

        def _autocorr_forward(queries, keys, values, Wq, bq, Wk, bk, Wv, bv, Wo, bo):
            B, L, D = queries.shape
            H, dk = (N_HEADS, D_K)
            q = (queries @ Wq.T + bq).reshape(B, L, H, dk)
            k = (keys @ Wk.T + bk).reshape(B, L, H, dk)
            v = (values @ Wv.T + bv).reshape(B, L, H, dk)
            qf = jnp.fft.rfft(q, axis=1)
            kf = jnp.fft.rfft(k, axis=1)
            corr = jnp.fft.irfft(qf * jnp.conj(kf), n=L, axis=1).mean(axis=-1)
            corr = corr.transpose(0, 2, 1)
            topk = min(max(1, int(math.log(L))), L)
            weights, delays = jax.lax.top_k(corr, topk)
            w = jax.nn.softmax(weights, axis=-1)
            idx = (jnp.arange(L)[None, None, None, :] - delays[..., None]) % L
            v_h = v.transpose(0, 2, 1, 3)
            gathered = jnp.take_along_axis(v_h[:, :, None], idx[..., None], axis=3)
            out = (w[..., None, None] * gathered).sum(axis=2)
            out = out.transpose(0, 2, 1, 3).reshape(B, L, D)
            return out @ Wo.T + bo
        return _autocorr_forward(queries, keys, values, Wq, bq, Wk, bk, Wv, bv, Wo, bo)

    def _L0_ffn_ref(x, Wg, W1, b1, W2, b2, W3, b3):
        import jax, jax.numpy as jnp
        import numpy as np
        B, S, H, DFF, E, K = (2, 512, 256, 512, 8, 2)

        def _moe(x, Wg, W1, b1, W2, b2, W3, b3):
            Bm, Sm, Hm = x.shape
            xt = x.reshape(-1, Hm)
            gout = xt @ Wg.T
            topv, topi = jax.lax.top_k(gout, K)
            w = jax.nn.softmax(topv, axis=-1)
            comb = jnp.einsum('tke,tk->te', jax.nn.one_hot(topi, E, dtype=x.dtype), w)
            g = jnp.einsum('th,efh->etf', xt, W1) + b1[:, None, :]
            v = jnp.einsum('th,efh->etf', xt, W2) + b2[:, None, :]
            h = jax.nn.silu(g) * v
            eo = jnp.einsum('etf,ehf->eth', h, W3) + b3[:, None, :]
            out = jnp.einsum('eth,te->th', eo, comb)
            return out.reshape(Bm, Sm, Hm)
        return _moe(x, Wg, W1, b1, W2, b2, W3, b3)

    def _L1_xattn_ref(q, k, v, Wq, Wk, Wv, Wo):
        import jax, jax.numpy as jnp
        import numpy as np
        B, N, L, D, H = (8, 128, 1024, 256, 16)
        Bq, Nq, Dm = q.shape
        Lk = k.shape[1]
        Hh = H
        Dh = Dm // Hh
        scale = Dm ** (-0.5)
        qh = (q @ Wq.T).reshape(Bq, Nq, Hh, Dh).transpose(0, 2, 1, 3)
        kh = (k @ Wk.T).reshape(Bq, Lk, Hh, Dh).transpose(0, 2, 1, 3)
        vh = (v @ Wv.T).reshape(Bq, Lk, Hh, Dh).transpose(0, 2, 1, 3)
        attn = jnp.einsum('bhnc,bhlc->bhnl', qh * scale, kh)
        attn = jax.nn.softmax(attn, axis=2)
        attn = attn / jnp.sum(attn, axis=-1, keepdims=True)
        out = jnp.einsum('bhnl,bhlc->bhnc', attn, vh)
        out = out.transpose(0, 2, 1, 3).reshape(Bq, Nq, Dm)
        return out @ Wo.T

    def _L1_ffn_ref(x, router_w, router_b, sw1, sb1, sw2, sb2, ew1, eb1, ew2, eb2):
        import jax, jax.numpy as jnp
        import numpy as np
        DIM = 256
        HID = 2 * DIM
        NUM_EXPERTS = 8
        TOP_K = 2
        BATCH, SEQ = (2, 512)

        def _gelu(x):
            return jax.nn.gelu(x, approximate=False)
        B, S, D = x.shape
        flat = x.reshape(-1, D)
        T = flat.shape[0]
        probs = jax.nn.softmax(flat @ router_w + router_b, axis=-1)
        top_w, top_i = jax.lax.top_k(probs, TOP_K)
        top_w = top_w / jnp.sum(top_w, axis=-1, keepdims=True)
        comb = jnp.zeros_like(probs).at[jnp.arange(T)[:, None], top_i].set(top_w)
        shared = _gelu(flat @ sw1 + sb1) @ sw2 + sb2
        h = _gelu(jnp.einsum('td,edh->eth', flat, ew1) + eb1[:, None, :])
        eo = jnp.einsum('eth,ehd->etd', h, ew2) + eb2[:, None, :]
        moe = jnp.einsum('te,etd->td', comb, eo)
        return (shared + moe).reshape(B, S, D)
    x = x + jnp.tanh(g_xattn[0]) * _L0_xattn_ref(_layernorm(x, axis=-1), ctx_1024, ctx_1024, L0_xattn_Wq, L0_xattn_bq, L0_xattn_Wk, L0_xattn_bk, L0_xattn_Wv, L0_xattn_bv, L0_xattn_Wo, L0_xattn_bo)
    x = x + jnp.tanh(g_ffn[0]) * _L0_ffn_ref(_layernorm(x, axis=-1), L0_ffn_Wg, L0_ffn_W1, L0_ffn_b1, L0_ffn_W2, L0_ffn_b2, L0_ffn_W3, L0_ffn_b3)
    x = x + jnp.tanh(g_xattn[1]) * _L1_xattn_ref(_layernorm(x, axis=-1), ctx_1024, ctx_1024, L1_xattn_Wq, L1_xattn_Wk, L1_xattn_Wv, L1_xattn_Wo)
    x = x + jnp.tanh(g_ffn[1]) * _L1_ffn_ref(_layernorm(x, axis=-1), L1_ffn_router_w, L1_ffn_router_b, L1_ffn_sw1, L1_ffn_sb1, L1_ffn_sw2, L1_ffn_sb2, L1_ffn_ew1, L1_ffn_eb1, L1_ffn_ew2, L1_ffn_eb2)
    return x

_drawn_inputs = setup_inputs


def setup_inputs(seed=0):
    import zlib

    import numpy as np

    out = dict(_drawn_inputs(seed))
    spreads = {'g_ffn': (-1.0, 0.6),
     'L0_xattn_bq': (0.0, 0.8),
     'L0_xattn_bk': (0.0, 0.8),
     'L0_xattn_bv': (0.0, 0.1),
     'L0_xattn_bo': (0.0, 0.1),
     'L1_ffn_router_b': (0.0, 0.1),
     'L1_ffn_sb1': (0.0, 0.445),
     'L1_ffn_sb2': (0.0, 0.1),
     'L1_ffn_eb1': (0.0, 0.63),
     'L1_ffn_eb2': (0.0, 0.1)}
    factors = {'L0_ffn_b1': 8.0, 'L0_ffn_b2': 8.0, 'L0_ffn_b3': 3.943}
    for name, (base, spread) in spreads.items():
        noise = np.random.default_rng([zlib.crc32(name.encode()), seed]).standard_normal(out[name].shape)
        drawn = base * np.exp(spread * noise) if base else spread * noise
        out[name] = jnp.asarray(drawn.astype(out[name].dtype))
    for name, factor in factors.items():
        out[name] = (out[name] * factor).astype(out[name].dtype)
    return out
```

```python
from contextlib import ExitStack

import numpy as np
import concourse.bass as bass
from concourse import mybir

P = 128
B, S, D = 16, 256, 256
H, C = 16, 16
KD = D // P
TOK = B * S
NTT = TOK // P
E, F = 8, 512
KF = F // P
TOPK, LAGS = 2, 5
NT = 2 * TOK // P + E
REGION = TOK + P
EPS = 1e-5
GROUP = P // H
HALF = TOK // P // 2
LOWEST, TAKEN = -3.0e38, -3.2e38

f32 = mybir.dt.float32
bf16 = mybir.dt.bfloat16
i32 = mybir.dt.int32
u32 = mybir.dt.uint32
ALU = mybir.AluOpType
ACT = mybir.ActivationFunctionType
AX = mybir.AxisListType.X
ds = bass.ds


class Memory:

    def __init__(self, nc):
        self.nc, self.stack = nc, ExitStack()

    def __enter__(self):
        return self

    def __exit__(self, *_):
        self.stack.close()

    def sb(self, name, shape, dt=f32):
        return self.stack.enter_context(self.nc.sbuf_tensor("sb_" + name, shape, dt))

    def bank(self, name, shape=(P, 512), dt=f32):
        return self.stack.enter_context(self.nc.psum_tensor(name, list(shape), dt))

    def sem(self, name):
        return self.stack.enter_context(self.nc.semaphore(name))


def rows(ap):
    return ap.rearrange("(k p) n -> p k n", p=P)


def over_partitions(ap, n):
    return ap.rearrange("(a n) -> a n", a=1).broadcast_to([P, n])


def flat(t):
    return t[:].rearrange("p a b -> p (a b)")


def wait_past_zero(engine, sem, value):
    if not isinstance(value, int) or value > 0:
        engine.wait_ge(sem, value)


def bc(ap, axis, n):
    shape = list(ap.shape)
    shape[axis] = n
    return ap.broadcast_to(shape)


def load_expert0(sp, io, g, e):
    for n, name in enumerate(("L0_ffn_W1", "L0_ffn_W2")):
        sp.dma_start(g.ffn[:, e, n * KD * F:(n + 1) * KD * F].rearrange("p (k n) -> p k n", k=KD),
                     rows(io[name][e])).then_inc(g.ffn_in, 16)
    sp.dma_start(g.ffn[:, e, 2 * KD * F:].rearrange("p (k n) -> p k n", k=KF),
                 rows(io["L0_ffn_W3"][e])).then_inc(g.ffn_in, 16)


def spectra(nc, io, g):
    with Memory(nc) as m:
        ctx_in = [m.sb(f"ctx_in{p}", [P, KD, D]) for p in range(2)]
        xn = [m.sb(f"xn{p}", [P, KD, D]) for p in range(2)]
        stats = m.sb("ln0_stats", [P, KD, 6])
        moments = m.sb("ln0_moments", [P, 2, KD, 2])
        rstd = m.sb("ln0_rstd", [P, 2, KD])
        spare = g.ffn[:, E - 1, :]
        wq = spare[:, 0:KD * D].rearrange("p (k n) -> p k n", k=KD)
        wkv = spare[:, KD * D:3 * KD * D].rearrange("p (k n) -> p k n", k=KD)
        bias0 = spare[:, 3 * KD * D:3 * KD * D + 3 * D]
        xf = [m.sb(f"xf{p}", [P, KD, S]) for p in range(2)]
        cf = [m.sb(f"cf{p}", [P, KD, S]) for p in range(2)]
        qs = m.sb("q_spec", [P, 2, D])
        ks = m.sb("k_spec", [P, 2, D])
        prod = m.sb("prod", [P, 4, D])
        summed = m.sb("prod_sum", [P, 4, H])
        edge = m.sb("edge", [P, 2, H])
        xf_ps, cf_ps = m.bank("xf_ps"), m.bank("cf_ps")
        q_ps = [m.bank(f"q_ps{t}") for t in range(2)]
        kv_ps = [m.bank(f"kv_ps{t}") for t in range(2)]

        consts_in = m.sem("a_consts_in")
        zeroed = m.sem("a_zeroed")
        in_loaded = [m.sem(f"a_in_loaded{p}") for p in range(2)]
        moments_ready, rstd_ready = m.sem("a_moments_ready"), m.sem("a_rstd_ready")
        xn_ready = m.sem("a_xn_ready")
        xf_done, cf_done = m.sem("a_xf_done"), m.sem("a_cf_done")
        xf_copied, cf_copied = m.sem("a_xf_copied"), m.sem("a_cf_copied")
        q_done, kv_done = m.sem("a_q_done"), m.sem("a_kv_done")
        act_copied, dve_copied = m.sem("a_sin_copied"), m.sem("a_cos_copied")
        spec_used = m.sem("a_spec_used")
        bias_ready = m.sem("a_bias_ready")
        block = m.stack.enter_context(nc.Block())

        @block.sync
        def _(sp):
            sp.dma_start(g.dft[:], rows(io["dft"])).then_inc(consts_in, 16)
            sp.dma_start(wq[:], rows(io["L0_xattn_Wq"])).then_inc(consts_in, 16)
            sp.dma_start(wkv[:, :, 0:D], rows(io["L0_xattn_Wk"])).then_inc(consts_in, 16)
            sp.dma_start(wkv[:, :, D:2 * D], rows(io["L0_xattn_Wv"])).then_inc(consts_in, 16)
            sp.wait_ge(zeroed, 1)
            for n, name in enumerate(("L0_xattn_bq", "L0_xattn_bk", "L0_xattn_bv")):
                sp.dma_start(bias0[0:1, n * D:(n + 1) * D],
                             io[name].rearrange("(a n) -> a n", a=1)).then_inc(consts_in, 16)
            with sp.Fori(0, B // 2) as j:
                for p in range(2):
                    b = j * 2 + p
                    sp.wait_ge(cf_done, b + 1)
                    sp.dma_start(ctx_in[p][:], io["ctx"][:, ds(b * KD, KD), :]).then_inc(in_loaded[p], 16)
                    sp.dma_start(g.x[:, ds(b * KD, KD), :], io["x"][:, ds(b * KD, KD), :])\
                        .then_inc(in_loaded[p], 16)
            sp.dma_start(g.icorr[:], rows(io["icorr"])).then_inc(g.later_in, 16)
            sp.dma_start(g.iout[:], rows(io["iout"])).then_inc(g.later_in, 16)
            sp.dma_start(g.wo0[:], rows(io["L0_xattn_Wo"])).then_inc(g.later_in, 16)
            sp.dma_start(g.router0[:], rows(io["L0_ffn_Wg"])).then_inc(g.later_in, 16)
            sp.dma_start(g.bo[:], over_partitions(io["L0_xattn_bo"], D)).then_inc(g.later_in, 16)
            sp.dma_start(g.gates[:, 0:2], over_partitions(io["g_xattn"], 2)).then_inc(g.later_in, 16)
            sp.dma_start(g.gates[:, 2:4], over_partitions(io["g_ffn"], 2)).then_inc(g.later_in, 16)
            for e in range(E - 1):
                load_expert0(sp, io, g, e)

        @block.gpsimd
        def _(pool):
            nc.gpsimd.memset(bias0, 0.0).then_inc(zeroed, 1)
            nc.gpsimd.memset(g.neg_half[:], -0.5)
            nc.gpsimd.memset(g.eps[:], EPS)
            nc.gpsimd.memset(g.zero_i[:], 0)
            nc.gpsimd.memset(g.ones[:], 1.0)
            nc.gpsimd.memset(g.before[:], 1.0)
            nc.gpsimd.memset(g.ident[:], 0.0)
            nc.gpsimd.memset(g.not_dc[:], 1.0)
            nc.gpsimd.memset(g.only_dc[:], 0.0)
            nc.gpsimd.memset(g.parity[:], 0.0)
            nc.gpsimd.memset(g.zeros[:], 0.0)
            nc.gpsimd.iota(g.expert_of[:], pattern=[[1, E]], base=0, channel_multiplier=0, allow_small_or_imprecise_dtypes=True)
            nc.gpsimd.iota(g.region_of[:], pattern=[[REGION, E]], base=0, channel_multiplier=0, allow_small_or_imprecise_dtypes=True)
            nc.gpsimd.iota(g.tile_no[:], pattern=[[1, NT]], base=0, channel_multiplier=0, allow_small_or_imprecise_dtypes=True)
            pool.drain()
            nc.gpsimd.memset(g.not_dc[0:1, :], 0.0)
            nc.gpsimd.memset(g.only_dc[0:1, :], 1.0)
            nc.gpsimd.affine_select(out=g.before[:], in_=g.before[:], compare_op=ALU.is_gt, fill=0.0,
                                    base=0, pattern=[[1, P]], channel_multiplier=-1)
            nc.gpsimd.affine_select(out=g.ident[:], in_=g.ident[:], compare_op=ALU.not_equal, fill=1.0,
                                    base=0, pattern=[[-1, P]], channel_multiplier=1)
            for par in range(2):
                v = g.parity_rows[:, par, :]
                nc.gpsimd.memset(v, 1.0)
            pool.drain()
            for par in range(2):
                v = g.parity_rows[:, par, :]
                nc.gpsimd.affine_select(out=v, in_=v, compare_op=ALU.is_ge, fill=0.0, base=-16 * par,
                                        pattern=[[-32, 4]], channel_multiplier=1)
            pool.drain()
            for par in range(2):
                v = g.parity_rows[:, par, :]
                nc.gpsimd.affine_select(out=v, in_=v, compare_op=ALU.is_ge, fill=0.0, base=16 * par + 15,
                                        pattern=[[32, 4]], channel_multiplier=-1)\
                    .then_inc(g.consts_made, 1)

            def scale_of_rows(b, p):
                pool.wait_ge(moments_ready, b + 1)
                nc.gpsimd.tensor_tensor(rstd[:, p, :], moments[:, p, :, 1], bc(g.eps[:], 1, KD), ALU.add)
                pool.drain()
                nc.gpsimd.tensor_tensor(rstd[:, p, :], rstd[:, p, :], bc(g.neg_half[:], 1, KD), ALU.pow)\
                    .then_inc(rstd_ready, 1)

            pool.drain()
            with pool.Fori(0, B // 2) as j:
                for p in range(2):
                    scale_of_rows(j * 2 + p, p)

        @block.scalar
        def _(act):
            act.sem_inc(xf_copied, 1)
            act.sem_inc(cf_copied, 1)
            act.wait_ge(zeroed, 1)
            act.wait_ge(consts_in, 16 * 7)
            nc.scalar.mul(bias0, bias0, float(S)).then_inc(bias_ready, 1)

            def spectra_in(b, p):
                act.wait_ge(xf_done, b + 3)
                nc.scalar.copy(flat(xf[p]), xf_ps[:]).then_inc(xf_copied, 1)
                act.wait_ge(cf_done, b + 3)
                nc.scalar.copy(flat(cf[p]), cf_ps[:]).then_inc(cf_copied, 1)

            def sines(b, p):
                act.wait_ge(q_done, b + 1)
                act.wait_ge(spec_used, b + 1)
                nc.scalar.copy(qs[:, 1, :], q_ps[1][:, 0:D])
                act.wait_ge(kv_done, b * 2 + 2)
                nc.scalar.copy(ks[:, 1, :], kv_ps[1][:, 0:D])
                nc.scalar.copy(g.v_spec[:, ds(b, 1), 1, :], kv_ps[1][:, D:2 * D]).then_inc(act_copied, 1)

            spectra_in(0, 0)
            with act.Fori(0, B // 2 - 1) as j:
                for p in range(2):
                    spectra_in(j * 2 + p + 1, 1 - p)
                    sines(j * 2 + p, p)
            spectra_in(B - 1, 1)
            sines(B - 2, 0)
            sines(B - 1, 1)

        @block.vector
        def _(dve):
            dve.sem_inc(spec_used, 1)

            def normalise(b, p):
                dve.wait_ge(in_loaded[p], b * 16 + (32 - 16 * p))
                for t in range(KD):
                    nc.vector.bn_stats(stats[:, t, :], g.x[:, ds(b * KD + t, 1), :])
                dve.drain()
                for t in range(KD):
                    k = nc.vector.bn_aggr(moments[:, p, t, :], stats[:, t, :])
                k.then_inc(moments_ready, 1)
                dve.drain()
                dve.wait_ge(rstd_ready, b + 1)
                dve.wait_ge(xf_done, b + 1)
                for t in range(KD):
                    k = nc.vector.tensor_scalar(xn[p][:, t, :], g.x[:, ds(b * KD + t, 1), :],
                                                moments[:, p, t, 0:1], rstd[:, p, t:t + 1],
                                                ALU.subtract, ALU.mult)
                k.then_inc(xn_ready, 1)

            def cross_spectrum(b, p):
                dve.wait_ge(q_done, b + 1)
                nc.vector.tensor_tensor(qs[:, 0, :], q_ps[0][:, 0:D], bias0[:, 0:D], ALU.add)
                dve.wait_ge(kv_done, b * 2 + 1)
                nc.vector.tensor_tensor(ks[:, 0, :], kv_ps[0][:, 0:D], bias0[:, D:2 * D], ALU.add)
                nc.vector.tensor_tensor(g.v_spec[:, ds(b, 1), 0, :], kv_ps[0][:, D:2 * D],
                                        bias0[:, 2 * D:3 * D], ALU.add).then_inc(dve_copied, 1)
                dve.drain()
                dve.wait_ge(act_copied, b + 1)
                nc.vector.tensor_tensor(prod[:, 0:2, :], qs[:], ks[:], ALU.mult)
                nc.vector.tensor_tensor(prod[:, 2, :], qs[:, 0, :], ks[:, 1, :], ALU.mult)
                nc.vector.tensor_tensor(prod[:, 3, :], qs[:, 1, :], ks[:, 0, :], ALU.mult)\
                    .then_inc(spec_used, 1)
                dve.drain()
                nc.vector.tensor_reduce(summed[:], prod[:].rearrange("p a (h c) -> p a h c", c=C), AX, ALU.add)
                dve.drain()
                nc.vector.scalar_tensor_tensor(g.cross[:, 0, ds(b * H, H)], summed[:, 1, :], g.not_dc[:],
                                               summed[:, 0, :], ALU.mult, ALU.add)
                nc.vector.tensor_tensor(edge[:, 0, :], summed[:, 2, :], summed[:, 3, :], ALU.subtract)
                nc.vector.tensor_scalar(edge[:, 1, :], summed[:, 1, :], g.only_dc[:], None, ALU.mult)
                dve.drain()
                nc.vector.scalar_tensor_tensor(g.cross[:, 1, ds(b * H, H)], edge[:, 0, :], g.not_dc[:],
                                               edge[:, 1, :], ALU.mult, ALU.add)

            normalise(0, 0)
            dve.wait_ge(bias_ready, 1)
            dve.wait_ge(g.consts_made, 2)
            nc.vector.tensor_reduce(g.parity[:], g.parity_rows[:], AX, ALU.add)
            with dve.Fori(0, B // 2 - 1) as j:
                for p in range(2):
                    b = j * 2 + p
                    normalise(b + 1, 1 - p)
                    cross_spectrum(b, p)
            normalise(B - 1, 1)
            cross_spectrum(B - 2, 0)
            cross_spectrum(B - 1, 1)

        @block.tensor
        def _(pe):
            pe.sem_inc(xf_done, 2)
            pe.sem_inc(cf_done, 2)

            def forward(b, p):
                pe.wait_ge(xn_ready, b + 1)
                pe.wait_ge(xf_copied, b + 1)
                for c in range(KD):
                    for t in range(KD):
                        k = nc.tensor.matmul(xf_ps[:, c * S:(c + 1) * S], xn[p][:, t, c * P:(c + 1) * P],
                                             g.dft[:, t, :], start=t == 0, stop=t == KD - 1)
                k.then_inc(xf_done, 1)
                pe.wait_ge(in_loaded[p], b * 16 + (32 - 16 * p))
                pe.wait_ge(cf_copied, b + 1)
                for c in range(KD):
                    for t in range(KD):
                        k = nc.tensor.matmul(cf_ps[:, c * S:(c + 1) * S], ctx_in[p][:, t, c * P:(c + 1) * P],
                                             g.dft[:, t, :], start=t == 0, stop=t == KD - 1)
                k.then_inc(cf_done, 1)

            def project(b, p):
                pe.wait_ge(xf_copied, b + 2)
                wait_past_zero(pe, act_copied, b)
                wait_past_zero(pe, dve_copied, b)
                for f in range(2):
                    for c in range(KD):
                        k = nc.tensor.matmul(q_ps[f][:, 0:D], xf[p][:, c, f * P:(f + 1) * P],
                                             wq[:, c, :], start=c == 0, stop=c == KD - 1)
                k.then_inc(q_done, 1)
                pe.wait_ge(cf_copied, b + 2)
                for f in range(2):
                    for c in range(KD):
                        k = nc.tensor.matmul(kv_ps[f][:], cf[p][:, c, f * P:(f + 1) * P],
                                             wkv[:, c, :], start=c == 0, stop=c == KD - 1)
                    k.then_inc(kv_done, 1)

            pe.wait_ge(consts_in, 16 * 7)
            forward(0, 0)
            forward(1, 1)
            project(0, 0)
            with pe.Fori(1, B // 2) as j:
                for p in range(2):
                    b = j * 2 + p
                    forward(b, p)
                    project(b - 1, 1 - p)
            project(B - 1, 1)


def lags(nc, io, g):
    G2 = B // GROUP
    with Memory(nc) as m:
        corr = m.sb("corr", [P, G2, S + 8])
        left = m.sb("corr_left", [P, G2, S + 8])
        top8 = m.sb("top8", [P, G2, 8])
        best = m.sb("best", [P, G2, 8])
        neg_max = m.sb("neg_max", [P, G2])
        expd = m.sb("lag_exp", [P, G2, S])
        weight = m.sb("lag_weight", [P, G2, S])
        total = m.sb("lag_total", [P, G2])
        weight_t = m.sb("lag_weight_t", [P, KD, G2 * P])
        corr_ps = [m.bank(f"corr_ps{i}") for i in range(G2)]
        wt_ps, ws_ps = m.bank("wt_ps"), m.bank("ws_ps")
        corr_done, exp_in, exp_done = m.sem("b_corr_done"), m.sem("b_exp_in"), m.sem("b_exp_done")
        weight_ready, wt_done, wt_copied = m.sem("b_weight_ready"), m.sem("b_wt_done"), m.sem("b_wt_copied")
        ws_done = m.sem("b_ws_done")
        block = m.stack.enter_context(nc.Block())

        @block.sync
        def _(sp):
            load_expert0(sp, io, g, E - 1)

        @block.tensor
        def _(pe):
            pe.wait_ge(g.later_in, 16 * 7)
            for i in range(G2):
                for f in range(2):
                    k = nc.tensor.matmul(corr_ps[i][:, 0:S], g.cross[:, f, i * P:(i + 1) * P],
                                         g.icorr[:, f, :], start=f == 0, stop=f == 1)
                k.then_inc(corr_done, 1)
            for i in range(G2):
                pe.wait_ge(weight_ready, i + 1)
                for t in range(KD):
                    k = nc.tensor.transpose(wt_ps[:, t * G2 * P + i * P:t * G2 * P + (i + 1) * P],
                                            weight[:, i, t * P:(t + 1) * P], g.ident[:])
            k.then_inc(wt_done, 1)
            pe.wait_ge(wt_copied, 1)
            for f in range(2):
                for t in range(KD):
                    k = nc.tensor.matmul(ws_ps[:, f * B * H:(f + 1) * B * H], g.dft[:, t, f * P:(f + 1) * P],
                                         weight_t[:, t, :], start=t == 0, stop=t == KD - 1)
            k.then_inc(ws_done, 1)

        @block.scalar
        def _(act):
            act.wait_ge(g.later_in, 16 * 7)
            nc.scalar.activation(g.gates[:], g.gates[:], ACT.Tanh).then_inc(g.gates_ready, 1)
            for i in range(G2):
                act.wait_ge(exp_in, i + 1)
                nc.scalar.activation(expd[:, i, :], corr[:, i, 0:S], ACT.Exp, bias=neg_max[:, i:i + 1])\
                    .then_inc(exp_done, 1)
            act.wait_ge(wt_done, 1)
            nc.scalar.copy(flat(weight_t), wt_ps[:]).then_inc(wt_copied, 1)

        @block.vector
        def _(dve):
            nc.vector.memset(corr[:], LOWEST)
            nc.vector.memset(best[:], LOWEST)
            dve.drain()
            for i in range(G2):
                dve.wait_ge(corr_done, i + 1)
                nc.vector.tensor_copy(corr[:, i, 0:S], corr_ps[i][:, 0:S])
                dve.drain()
                nc.vector.max(top8[:, i, :], corr[:, i, 0:S])
                dve.drain()
                nc.vector.tensor_scalar(neg_max[:, i:i + 1], top8[:, i, 0:1], -1.0, None, ALU.mult)\
                    .then_inc(exp_in, 1)
                nc.vector.tensor_copy(best[:, i, 0:LAGS], top8[:, i, 0:LAGS])
                dve.drain()
                nc.vector.match_replace(left[:, i, :], best[:, i, :], corr[:, i, :], TAKEN)
            dve.drain()
            for i in range(G2):
                dve.wait_ge(exp_done, i + 1)
                nc.vector.scalar_tensor_tensor(weight[:, i, :], left[:, i, 0:S], (LOWEST + TAKEN) / 2,
                                               expd[:, i, :], ALU.is_lt, ALU.mult,
                                               accum_out=total[:, i:i + 1])
                dve.drain()
                nc.vector.reciprocal(total[:, i:i + 1], total[:, i:i + 1])
                dve.drain()
                nc.vector.tensor_scalar(weight[:, i, :], weight[:, i, :], total[:, i:i + 1], None, ALU.mult)\
                    .then_inc(weight_ready, 1)
            dve.wait_ge(ws_done, 1)
            nc.vector.tensor_copy(g.w_same[:, 0, :], ws_ps[:, 0:B * H])
            nc.vector.tensor_scalar(g.w_other[:, 1, :], ws_ps[:, B * H:2 * B * H], g.not_dc[:], None, ALU.mult)
            nc.vector.tensor_scalar(g.w_other[:, 0, :], ws_ps[:, B * H:2 * B * H], g.not_dc[:], -1.0,
                                    ALU.mult, ALU.mult)
            nc.vector.tensor_scalar(g.w_same[:, 1, :], ws_ps[:, B * H:2 * B * H], g.only_dc[:], None, ALU.mult)
            dve.drain()
            nc.vector.scalar_tensor_tensor(g.w_same[:, 1, :], g.w_same[:, 0, :], g.not_dc[:],
                                           g.w_same[:, 1, :], ALU.mult, ALU.add)


class Routing:

    def __init__(self, m, g, layer, xr_ps, small_ps):
        self.g, self.layer, self.xr_ps, self.small_ps = g, layer, xr_ps, small_ps
        n = f"r{layer}_"
        self.stats = m.sb(n + "stats", [P, KD, 6])
        self.moments = m.sb(n + "moments", [P, KD, 2])
        self.rstd = m.sb(n + "rstd", [P, KD])
        self.xr = [m.sb(n + f"xr{p}", [P, KD, D]) for p in range(2)]
        self.xrt = m.sb(n + "xrt", [P, KD, S])
        self.logits = m.sb(n + "logits", [P, KD, E])
        self.top_v = m.sb(n + "top_v", [P, KD, 8])
        self.top_f = m.sb(n + "top_f", [P, KD, TOPK])
        self.top_i = m.sb(n + "top_i", [P, KD, 8], u32)
        self.onehot = m.sb(n + "onehot", [P, KD, TOPK, E])
        self.mask = m.sb(n + "mask", [P, KD, E], bf16)
        self.rank = m.sb(n + "rank", [P, KD, E])
        self.pos_f = m.sb(n + "pos_f", [P, KD, TOPK, E])
        self.to = [m.sb(n + f"to{p}", [P, KD * TOPK], i32) for p in range(2)]
        self.pos_i = [m.sb(n + f"pos_i{p}", [P, KD * TOPK], i32) for p in range(2)]
        (self.moments_ready, self.rstd_ready, self.xr_ready, self.xrt_done, self.xrt_copied,
         self.logits_done, self.mask_ready, self.rank_done, self.pos_ready, self.seen_ready) = (
            m.sem(n + s) for s in ("moments_ready", "rstd_ready", "xr_ready", "xrt_done", "xrt_copied",
                                   "logits_done", "mask_ready", "rank_done", "pos_ready", "seen_ready"))
        self.scattered = [m.sem(n + f"scattered{p}") for p in range(2)]
        self.per_batch = 16 * (KD * TOPK + (1 if layer else 0))

    def vector(self, nc, dve, j, p, b):
        g = self.g
        for t in range(KD):
            nc.vector.bn_stats(self.stats[:, t, :], g.x[:, ds(b * KD + t, 1), :])
        dve.drain()
        for t in range(KD):
            k = nc.vector.bn_aggr(self.moments[:, t, :], self.stats[:, t, :])
        k.then_inc(self.moments_ready, 1)
        dve.drain()
        dve.wait_ge(self.rstd_ready, b + 1)
        wait_past_zero(dve, self.scattered[p], self.per_batch * j)
        for t in range(KD):
            k = nc.vector.tensor_scalar(self.xr[p][:, t, :], g.x[:, ds(b * KD + t, 1), :],
                                        self.moments[:, t, 0:1], self.rstd[:, t:t + 1],
                                        ALU.subtract, ALU.mult)
        k.then_inc(self.xr_ready, 1)
        dve.wait_ge(self.logits_done, b + 1)
        logits_ps = self.small_ps[:, 0:KD * E].rearrange("p (t e) -> p t e", e=E)
        if self.layer:
            nc.vector.tensor_tensor(self.logits[:], logits_ps, bc(g.router_b[:], 1, KD), ALU.add)
        else:
            nc.vector.tensor_copy(self.logits[:], logits_ps)
        dve.drain()
        for t in range(KD):
            nc.vector.max(self.top_v[:, t, :], self.logits[:, t, :])
        dve.drain()
        for t in range(KD):
            nc.vector.max_index(self.top_i[:, t, :], self.top_v[:, t, :], self.logits[:, t, :])
        nc.vector.tensor_copy(g.top_v[:, ds(b * KD, KD), :], self.top_v[:, :, 0:TOPK])
        dve.drain()
        nc.vector.tensor_copy(self.top_f[:], self.top_i[:, :, 0:TOPK])
        dve.drain()
        nc.vector.tensor_copy(g.top_f[:, ds(b * KD, KD), :], self.top_f[:])
        nc.vector.tensor_tensor(self.onehot[:].rearrange("p t k e -> p (t k) e"),
                                bc(g.expert_of[:].rearrange("p (a e) -> p a e", a=1), 1, KD * TOPK),
                                bc(self.top_f[:].rearrange("p t (k c) -> p (t k) c", c=1), 2, E), ALU.is_equal)
        dve.drain()
        nc.vector.tensor_tensor(self.mask[:], self.onehot[:, :, 0, :], self.onehot[:, :, 1, :], ALU.add)\
            .then_inc(self.mask_ready, 1)
        dve.wait_ge(self.rank_done, b + 1)
        rank_ps = self.small_ps[:, 32:32 + KD * E].rearrange("p (t e) -> p t e", e=E)
        nc.vector.tensor_tensor(self.rank[:], rank_ps, bc(g.region_of[:].rearrange("p (a e) -> p a e", a=1), 1, KD),
                                ALU.add)
        nc.vector.tensor_tensor(g.seen[:], g.seen[:], self.mask[:, 0, :], ALU.add)
        dve.drain()
        nc.vector.tensor_tensor(g.seen[:], g.seen[:], self.mask[:, 1, :], ALU.add).then_inc(self.seen_ready, 1)
        for t in range(KD):
            nc.vector.tensor_tensor(self.pos_f[:, t, :, :], self.onehot[:, t, :, :],
                                    bc(self.rank[:, t:t + 1, :], 1, TOPK), ALU.mult)
        dve.drain()
        pos = g.pos[:, ds(b * KD, KD), :]
        nc.vector.tensor_reduce(pos, self.pos_f[:], AX, ALU.add)
        dve.drain()
        nc.vector.tensor_copy(self.pos_i[p][:].rearrange("p (t k) -> p t k", k=TOPK), pos)\
            .then_inc(self.pos_ready, 1)

    def gpsimd_rstd(self, nc, pool, b):
        pool.wait_ge(self.moments_ready, b + 1)
        nc.gpsimd.tensor_tensor(self.rstd[:], self.moments[:, :, 1], bc(self.g.eps[:], 1, KD), ALU.add)
        pool.drain()
        nc.gpsimd.tensor_tensor(self.rstd[:], self.rstd[:], bc(self.g.neg_half[:], 1, KD), ALU.pow)\
            .then_inc(self.rstd_ready, 1)

    def gpsimd_scatter(self, nc, pool, j, p, b):
        pool.wait_ge(self.pos_ready, b + 1)
        nc.gpsimd.tensor_tensor(self.to[p][:], self.pos_i[p][:], self.g.zero_i[:], ALU.add)
        pool.drain()
        for t in range(KD):
            for k in range(TOPK):
                at = t * TOPK + k
                pool.indirect_dma_start(
                    self.g.routed, bass.IndirectOffsetOnAxis(ap=self.to[p][:, at:at + 1], axis=0),
                    self.xr[p][:, t, :], None).then_inc(self.scattered[p], 16)
        if self.layer:
            pool.dma_start(
                self.g.routed[ds(b * S + E * REGION, S), :].rearrange("(t p) d -> p t d", p=P),
                self.xr[p][:]).then_inc(self.scattered[p], 16)

    def scalar(self, nc, act, b):
        act.wait_ge(self.xrt_done, b + 1)
        nc.scalar.copy(flat(self.xrt), self.xr_ps[:]).then_inc(self.xrt_copied, 1)

    def tensor(self, nc, pe, p, b):
        g = self.g
        pe.wait_ge(self.xr_ready, b + 1)
        for t in range(KD):
            for c in range(KD):
                k = nc.tensor.transpose(self.xr_ps[:, c * S + t * P:c * S + (t + 1) * P],
                                        self.xr[p][:, t, c * P:(c + 1) * P], g.ident[:])
        k.then_inc(self.xrt_done, 1)
        pe.wait_ge(self.xrt_copied, b + 1)
        router = g.router1 if self.layer else g.router0
        for t in range(KD):
            for c in range(KD):
                k = nc.tensor.matmul(self.small_ps[:, t * E:(t + 1) * E], self.xrt[:, c, t * P:(t + 1) * P],
                                     router[:, c, :], start=c == 0, stop=c == KD - 1)
        k.then_inc(self.logits_done, 1)
        pe.wait_ge(self.mask_ready, b + 1)
        pe.wait_ge(self.seen_ready, b + 1)
        for t in range(KD):
            out = self.small_ps[:, 32 + t * E:32 + (t + 1) * E]
            nc.tensor.matmul(out, g.before[:], self.mask[:, t, :], start=True, stop=False)
            if t:
                nc.tensor.matmul(out, g.ones[:], self.mask[:, 0, :], start=False, stop=False)
            k = nc.tensor.matmul(out, g.ones[:], g.seen[:], start=False, stop=True)
        k.then_inc(self.rank_done, 1)


def mix(nc, io, g):
    with Memory(nc) as m:
        same = m.sb("same", [P, 2, D])
        other = m.sb("other", [P, 2, D])
        spec = [m.sb(f"out_spec{p}", [P, 2, D]) for p in range(2)]
        ot = m.sb("ot", [P, KD, S])
        x_bo = m.sb("x_bo", [P, KD, D])
        gbo = m.sb("gbo", [P, 1, D])
        ot_ps, y_ps, xr_ps, small_ps = m.bank("ot_ps"), m.bank("y_ps"), m.bank("xr_ps"), m.bank("small_ps")
        r = Routing(m, g, 0, xr_ps, small_ps)
        other_ready = m.sem("c_other_ready")
        spec_ready, ot_done, ot_copied = m.sem("c_spec_ready"), m.sem("c_ot_done"), m.sem("c_ot_copied")
        y_done, x_done, xbo_ready = m.sem("c_y_done"), m.sem("c_x_done"), m.sem("c_xbo_ready")
        block = m.stack.enter_context(nc.Block())

        def heads(ap):
            return ap.rearrange("p a (h c) -> p a h c", c=C)

        def per_head(w, b, a):
            return bc(w[:, a, ds(b * H, H)].rearrange("p (h c) -> p h c", c=1), 2, C)

        @block.gpsimd
        def _(pool):
            pool.wait_ge(g.gates_ready, 1)
            nc.gpsimd.tensor_scalar(gbo[:, 0, :], g.bo[:], g.gates[:, 0:1], None, ALU.mult)
            pool.drain()

            def values(b):
                pool.wait_ge(spec_ready, b + 1)
                for a in range(2):
                    k = nc.gpsimd.tensor_tensor(
                        other[:, a, :].rearrange("p (h c) -> p h c", c=C),
                        g.v_spec[:, ds(b, 1), 1 - a, :].rearrange("p a (h c) -> p (a h) c", c=C),
                        per_head(g.w_other, b, a), ALU.mult)
                k.then_inc(other_ready, 1)
                pool.wait_ge(x_done, b + 1)
                nc.gpsimd.tensor_tensor(x_bo[:], g.x[:, ds(b * KD, KD), :], bc(gbo[:], 1, KD), ALU.add)\
                    .then_inc(xbo_ready, 1)

            with pool.Fori(0, B // 2) as j:
                for p in range(2):
                    b = j * 2 + p
                    values(b)
                    r.gpsimd_rstd(nc, pool, b)
                    r.gpsimd_scatter(nc, pool, j, p, b)
            for p in range(2):
                pool.wait_ge(r.scattered[p], r.per_batch * (B // 2))

        @block.scalar
        def _(act):
            with act.Fori(0, B // 2) as j:
                for p in range(2):
                    b = j * 2 + p
                    act.wait_ge(ot_done, b + 1)
                    nc.scalar.copy(flat(ot), ot_ps[:]).then_inc(ot_copied, 1)
                    r.scalar(nc, act, b)

        @block.vector
        def _(dve):
            dve.sem_inc(spec_ready, 1)
            dve.sem_inc(x_done, 1)
            nc.vector.memset(g.seen[:], 0.0).then_inc(r.seen_ready, 1)
            def batch(j, p):
                b = j * 2 + p
                for a in range(2):
                    nc.vector.tensor_tensor(
                        same[:, a, :].rearrange("p (h c) -> p h c", c=C),
                        g.v_spec[:, ds(b, 1), a, :].rearrange("p a (h c) -> p (a h) c", c=C),
                        per_head(g.w_same, b, a), ALU.mult)
                dve.drain()
                dve.wait_ge(other_ready, b + 1)
                nc.vector.tensor_tensor(spec[p][:], same[:], other[:], ALU.add).then_inc(spec_ready, 1)
                dve.wait_ge(y_done, b + 1)
                dve.wait_ge(xbo_ready, b + 1)
                nc.vector.scalar_tensor_tensor(g.x[:, ds(b * KD, KD), :], y_ps[:].rearrange("p (t d) -> p t d", d=D),
                                               g.gates[:, 0:1], x_bo[:], ALU.mult, ALU.add)\
                    .then_inc(x_done, 1)
                dve.drain()
                r.vector(nc, dve, j, p, b)

            for p in range(2):
                batch(0, p)
            with dve.Fori(1, B // 2) as j:
                for p in range(2):
                    batch(j, p)

        @block.tensor
        def _(pe):
            with pe.Fori(0, B // 2) as j:
                for p in range(2):
                    b = j * 2 + p
                    pe.wait_ge(spec_ready, b + 2)
                    for c in range(KD):
                        for f in range(2):
                            k = nc.tensor.matmul(ot_ps[:, c * S:(c + 1) * S], spec[p][:, f, c * P:(c + 1) * P],
                                                 g.iout[:, f, :], start=f == 0, stop=f == 1)
                    k.then_inc(ot_done, 1)
                    pe.wait_ge(ot_copied, b + 1)
                    for t in range(KD):
                        for c in range(KD):
                            k = nc.tensor.matmul(y_ps[:, t * D:(t + 1) * D], ot[:, c, t * P:(t + 1) * P],
                                                 g.wo0[:, c, :], start=c == 0, stop=c == KD - 1)
                    k.then_inc(y_done, 1)
                    r.tensor(nc, pe, p, b)


def plan(nc, io, g, layer):
    with Memory(nc) as m:
        n = f"p{layer}_"
        count = m.sb(n + "count", [P, E])
        tiles_i = m.sb(n + "tiles_i", [P, E], i32)
        tiles = m.sb(n + "tiles", [P, E])
        ends = m.sb(n + "ends", [P, E])
        shift = m.sb(n + "shift", [P, E])
        one = m.sb(n + "one", [P, E])
        over = m.sb(n + "over", [P, NT, E])
        work = m.sb(n + "work", [P, NT, E])
        plan_f = m.sb(n + "plan_f", [P, 4, NT])
        count_i = m.sb(n + "count_i", [P, E], i32)
        pick = m.sb(n + "pick", [P, NTT * TOPK, E])
        packed = m.sb(n + "packed", [P, NTT * TOPK])
        expd = m.sb(n + "expd", [P, NTT])
        count_ps = m.bank(n + "count_ps")
        counted, counts_ready, done = m.sem(n + "counted"), m.sem(n + "counts_ready"), m.sem(n + "done")
        diff_ready, exp_done = m.sem(n + "diff_ready"), m.sem(n + "exp_done")
        block = m.stack.enter_context(nc.Block())

        @block.tensor
        def _(pe):
            nc.tensor.matmul(count_ps[:, 0:E], g.ones[:], g.seen[:], start=True, stop=True).then_inc(counted, 1)

        @block.gpsimd
        def _(pool):
            shared = NTT if layer else 0
            nc.gpsimd.memset(g.plan[:, 0, NT:NT + shared + 2], E if layer else E - 1)
            if layer:
                nc.gpsimd.iota(g.plan[:, 1, NT:NT + NTT], pattern=[[P, NTT]], base=E * REGION,
                               channel_multiplier=0)
            nc.gpsimd.memset(g.plan[:, 1, NT + shared:NT + shared + 2], (E if layer else E - 1) * REGION)

        @block.scalar
        def _(act):
            act.wait_ge(diff_ready, 1)
            nc.scalar.activation(expd[:], expd[:], ACT.Exp).then_inc(exp_done, 1)

        @block.sync
        def _(sp):
            sp.wait_ge(counts_ready, 1)
            for e in range(E):
                c = sp.value_load(count_i[0:1, e:e + 1], min_val=0, max_val=TOK)
                sp.dma_start(g.routed[ds(c + e * REGION, P), :], g.zeros[:]).then_inc(done, 16)
            sp.wait_ge(done, 16 * E)

        @block.vector
        def _(dve):
            v = nc.vector
            v.memset(one[:], 1.0)
            v.tensor_tensor(expd[:], g.top_v[:, :, 1], g.top_v[:, :, 0], ALU.subtract).then_inc(diff_ready, 1)
            dve.wait_ge(counted, 1)
            v.tensor_copy(count[:], count_ps[:, 0:E])
            dve.drain()
            v.tensor_copy(count_i[:], count[:]).then_inc(counts_ready, 1)
            v.tensor_scalar(tiles_i[:], count[:], float(P - 1), None, ALU.add)
            dve.drain()
            v.tensor_scalar(tiles_i[:], tiles_i[:], 7, None, ALU.arith_shift_right)
            dve.drain()
            v.tensor_copy(tiles[:], tiles_i[:])
            dve.drain()
            v.tensor_tensor_scan(ends[:], one[:], tiles[:], 0.0, ALU.mult, ALU.add)
            dve.drain()
            v.tensor_tensor(over[:], bc(g.tile_no[:].rearrange("p (n a) -> p n a", a=1), 2, E),
                            bc(ends[:].rearrange("p (a e) -> p a e", a=1), 1, NT), ALU.is_ge)
            v.tensor_tensor(shift[:], ends[:], tiles[:], ALU.subtract)
            dve.drain()
            v.tensor_reduce(plan_f[:, 0, :], over[:], AX, ALU.add)
            v.tensor_tensor(work[:], over[:], bc(tiles[:].rearrange("p (a e) -> p a e", a=1), 1, NT), ALU.mult)
            v.scalar_tensor_tensor(shift[:], shift[:], float(P), g.region_of[:], ALU.mult, ALU.subtract)
            dve.drain()
            v.tensor_reduce(plan_f[:, 1, :], work[:], AX, ALU.add)
            v.tensor_scalar(plan_f[:, 2, :], plan_f[:, 0, :], float(E), None, ALU.is_lt)
            v.tensor_scalar(plan_f[:, 3, :], plan_f[:, 0, :], float(E - 1), None, ALU.min)
            dve.drain()
            v.tensor_tensor(plan_f[:, 1, :], g.tile_no[:], plan_f[:, 1, :], ALU.subtract)
            dve.drain()
            v.scalar_tensor_tensor(plan_f[:, 1, :], plan_f[:, 1, :], float(P), plan_f[:, 2, :], ALU.mult, ALU.mult)
            dve.drain()
            v.scalar_tensor_tensor(plan_f[:, 1, :], plan_f[:, 3, :], float(REGION), plan_f[:, 1, :],
                                   ALU.mult, ALU.add)
            v.tensor_copy(g.plan[:, 0, 0:NT], plan_f[:, 3, :])
            dve.drain()
            v.tensor_copy(g.plan[:, 1, 0:NT], plan_f[:, 1, :])
            v.tensor_tensor(pick[:], bc(g.top_f[:].rearrange("p t (k a) -> p (t k) a", a=1), 2, E),
                            bc(g.expert_of[:].rearrange("p (a e) -> p a e", a=1), 1, NTT * TOPK), ALU.is_equal)
            dve.drain()
            v.tensor_tensor(pick[:], pick[:], bc(shift[:].rearrange("p (a e) -> p a e", a=1), 1, NTT * TOPK),
                            ALU.mult)
            dve.drain()
            v.tensor_reduce(packed[:], pick[:], AX, ALU.add)
            dve.drain()
            v.tensor_tensor(g.packed_i[:], packed[:], g.pos[:].rearrange("p t k -> p (t k)"), ALU.add)
            dve.drain()
            dve.wait_ge(exp_done, 1)
            v.tensor_scalar(packed[:, 0:NTT], expd[:], 1.0, None, ALU.add)
            dve.drain()
            v.reciprocal(packed[:, 0:NTT], packed[:, 0:NTT])
            dve.drain()
            v.tensor_scalar(g.share[:, 0, :], packed[:, 0:NTT], g.gates[:, 2 + layer:3 + layer], None, ALU.mult)
            dve.drain()
            v.tensor_tensor(g.share[:, 1, :], g.share[:, 0, :], expd[:], ALU.mult)


def experts(nc, io, g, layer):
    tiles = NT + (NTT if layer else 0)
    ups = 1 if layer else 2
    slots = E + layer
    width = (ups * KD * F) + KF * D
    w = g.ffn_flat[:, 0:slots * width].rearrange("p (e n) -> p e n", n=width)
    up_bias = g.v_flat[:, 0:slots * ups * F].rearrange("p (e n) -> p e n", n=ups * F)
    with Memory(nc) as m:
        n = f"e{layer}_"
        xg = [m.sb(n + f"xg{p}", [P, D]) for p in range(2)]
        xt = [m.sb(n + f"xt{p}", [P, KD, P]) for p in range(2)]
        pre = m.sb(n + "pre", [P, F])
        lin = m.sb(n + "lin", [P, F])
        act_out = m.sb(n + "act_out", [P, F])
        h = act_out if layer else m.sb(n + "h", [P, F])
        ht = m.sb(n + "ht", [P, KF, P])
        out = [m.sb(n + f"out{p}", [P, D]) for p in range(2)]
        down_bias = m.sb(n + "down_bias", [P, slots, D])
        up_ps = [[m.bank(n + f"up_ps{u}{p}") for p in range(2)] for u in range(ups)]
        xt_ps = [m.bank(n + f"xt_ps{p}") for p in range(2)]
        ht_ps, out_ps = m.bank(n + "ht_ps"), m.bank(n + "out_ps")
        bias_in = m.sem(n + "bias_in")
        xg_loaded = [m.sem(n + f"xg_loaded{p}") for p in range(2)]
        stored = [m.sem(n + f"stored{p}") for p in range(2)]
        (xt_done, xt_copied, up_done, pre_ready, lin_ready, act_done, h_ready, ht_done, ht_copied, out_done,
         out_ready) = (
            m.sem(n + s) for s in ("xt_done", "xt_copied", "up_done", "pre_ready", "lin_ready", "act_done",
                                   "h_ready", "ht_done", "ht_copied", "out_done", "out_ready"))
        block = m.stack.enter_context(nc.Block())

        @block.sync
        def _(sp):
            if layer:
                for e in range(E):
                    sp.dma_start(up_bias[:, e, :], over_partitions(io["L1_ffn_eb1"][e], F)).then_inc(bias_in, 16)
                    sp.dma_start(down_bias[:, e, :], over_partitions(io["L1_ffn_eb2"][e], D)).then_inc(bias_in, 16)
                sp.dma_start(up_bias[:, E, :], over_partitions(io["L1_ffn_sb1"], F)).then_inc(bias_in, 16)
                sp.dma_start(down_bias[:, E, :], over_partitions(io["L1_ffn_sb2"], D)).then_inc(bias_in, 16)
            else:
                for e in range(E):
                    sp.dma_start(up_bias[:, e, 0:F], over_partitions(io["L0_ffn_b1"][e], F)).then_inc(bias_in, 16)
                    sp.dma_start(up_bias[:, e, F:2 * F], over_partitions(io["L0_ffn_b2"][e], F)).then_inc(bias_in, 16)
                    sp.dma_start(down_bias[:, e, :], over_partitions(io["L0_ffn_b3"][e], D)).then_inc(bias_in, 16)
            with sp.Fori(0, tiles // 2 + 1) as j:
                for p in range(2):
                    i = j * 2 + p
                    row = sp.value_load(g.plan[0:1, 1, ds(i, 1)], min_val=0, max_val=(E + 1) * REGION - P)
                    sp.wait_ge(xt_done, i + 1)
                    sp.dma_start(xg[p][:], g.routed[ds(row, P), :]).then_inc(xg_loaded[p], 16)

        @block.gpsimd
        def _(pool):
            with pool.Fori(0, tiles // 2) as j:
                for p in range(2):
                    i = j * 2 + p
                    pool.wait_ge(out_ready, i + 1)
                    pool.dma_start(g.expert_out[layer][ds(i * P, P), :], out[p][:]).then_inc(stored[p], 16)
            for p in range(2):
                pool.wait_ge(stored[p], 16 * (tiles // 2))

        @block.scalar
        def _(act):
            def turned(i, p):
                act.wait_ge(xt_done, i + 3)
                nc.scalar.copy(flat(xt[p]), xt_ps[p][:, 0:D]).then_inc(xt_copied, 1)

            turned(0, 0)
            with act.Fori(0, tiles // 2) as j:
                for p in range(2):
                    i = j * 2 + p
                    turned(i + 1, 1 - p)
                    act.wait_ge(pre_ready, i + 1)
                    if layer:
                        act.wait_ge(ht_done, i + 1)
                        nc.scalar.activation(h[:], pre[:], ACT.Gelu).then_inc(act_done, 1)
                    else:
                        act.wait_ge(h_ready, i + 1)
                        nc.scalar.activation(act_out[:], pre[:], ACT.Silu).then_inc(act_done, 1)
                    act.wait_ge(ht_done, i + 2)
                    nc.scalar.copy(flat(ht), ht_ps[:]).then_inc(ht_copied, 1)

        @block.vector
        def _(dve):
            dve.sem_inc(h_ready, 1)
            dve.wait_ge(bias_in, 16 * (2 * slots if layer else 3 * slots))
            def tile(j, p):
                i = j * 2 + p
                e = dve.value_load(g.plan[0:1, 0, ds(i, 1)], min_val=0, max_val=slots - 1)
                dve.wait_ge(up_done, i * ups + 1)
                nc.vector.tensor_tensor(pre[:], up_ps[0][p][:], up_bias[:, ds(e, 1), 0:F], ALU.add)\
                    .then_inc(pre_ready, 1)
                if not layer:
                    dve.wait_ge(up_done, i * ups + 2)
                    nc.vector.tensor_tensor(lin[:], up_ps[1][p][:], up_bias[:, ds(e, 1), F:2 * F], ALU.add)
                if not layer:
                    dve.drain()
                dve.wait_ge(act_done, i + 1)
                if not layer:
                    dve.wait_ge(ht_done, i + 1)
                    nc.vector.tensor_tensor(h[:], act_out[:], lin[:], ALU.mult).then_inc(h_ready, 1)
                dve.wait_ge(out_done, i + 1)
                wait_past_zero(dve, stored[p], j * 16)
                nc.vector.tensor_tensor(out[p][:], out_ps[:, 0:D], down_bias[:, ds(e, 1), :], ALU.add)\
                    .then_inc(out_ready, 1)

            for p in range(2):
                tile(0, p)
            with dve.Fori(1, tiles // 2) as j:
                for p in range(2):
                    tile(j, p)

        @block.tensor
        def _(pe):
            pe.sem_inc(xt_done, 2)
            pe.sem_inc(ht_done, 1)
            pe.wait_ge(g.ffn_in if not layer else g.ffn1_in, 16 * (E * 3 if not layer else 2 * slots))

            def turn(i, p):
                pe.wait_ge(xg_loaded[p], i * 8 + (16 - 8 * p))
                wait_past_zero(pe, xt_copied, i - 1)
                for c in range(KD):
                    k = nc.tensor.transpose(xt_ps[p][:, c * P:(c + 1) * P], xg[p][:, c * P:(c + 1) * P], g.ident[:])
                k.then_inc(xt_done, 1)

            def up(i, p):
                e = pe.value_load(g.plan[0:1, 0, ds(i, 1)], min_val=0, max_val=slots - 1)
                pe.wait_ge(xt_copied, i + 1)
                for u in range(ups):
                    for c in range(KD):
                        at = (u * KD + c) * F
                        k = nc.tensor.matmul(up_ps[u][p][:], xt[p][:, c, :], w[:, ds(e, 1), at:at + F],
                                             start=c == 0, stop=c == KD - 1)
                    k.then_inc(up_done, 1)
                return e

            def down(i, p, e):
                pe.wait_ge(act_done if layer else h_ready, i + 1 + (0 if layer else 1))
                wait_past_zero(pe, ht_copied, i)
                for f in range(KF):
                    k = nc.tensor.transpose(ht_ps[:, f * P:(f + 1) * P], h[:, f * P:(f + 1) * P], g.ident[:])
                k.then_inc(ht_done, 1)
                turn(i + 2, p)
                pe.wait_ge(ht_copied, i + 1)
                wait_past_zero(pe, out_ready, i)
                for f in range(KF):
                    at = ups * KD * F + f * D
                    k = nc.tensor.matmul(out_ps[:, 0:D], ht[:, f, :], w[:, ds(e, 1), at:at + D],
                                         start=f == 0, stop=f == KF - 1)
                k.then_inc(out_done, 1)

            def expert(i):
                return pe.value_load(g.plan[0:1, 0, ds(i, 1)], min_val=0, max_val=slots - 1)

            turn(0, 0)
            turn(1, 1)
            up(0, 0)
            up(1, 1)
            down(0, 0, expert(0))
            with pe.Fori(1, tiles // 2) as j:
                up(j * 2, 0)
                down(j * 2 - 1, 1, expert(j * 2 - 1))
                up(j * 2 + 1, 1)
                down(j * 2, 0, expert(j * 2))
            down(tiles - 1, 1, expert(tiles - 1))


def attention(nc, io, g):
    CV = C + 1
    QUAD = 4
    SB = 3
    with Memory(nc) as m:
        ctx_in = [m.sb(f"d_ctx_in{p}", [P, KD, D]) for p in range(2)]
        idx = [m.sb(f"d_idx{p}", [P, KD * TOPK], i32) for p in range(2)]
        eo = [g.v_flat[:, (2 * QUAD * KD + p * KD * TOPK) * D:(2 * QUAD * KD + (p + 1) * KD * TOPK) * D]
              .rearrange("p (t d) -> p t d", d=D) for p in range(2)]
        stats = m.sb("d_stats", [P, KD, 6])
        moments = m.sb("d_moments", [P, KD, 2])
        rstd = m.sb("d_rstd", [P, KD])
        xn = m.sb("d_xn", [P, KD, D])
        xnt = m.sb("d_xnt", [P, KD, S])
        ctxt = m.sb("d_ctxt", [P, KD, S])
        qt = m.sb("d_qt", [P, KD, S])
        kt = [m.sb(f"d_kt{par}", [P, KD, S]) for par in range(2)]
        v = m.sb("d_v", [P, KD, D])
        exps = [g.v_flat[:, s * KD * S:(s + 1) * KD * S].rearrange("p (t n) -> p t n", n=S)
                for s in range(2 * QUAD)]
        neg_max = m.sb("d_neg_max", [P, 2 * QUAD, KD])
        sums = m.sb("d_sums", [P, 2, KD, QUAD])
        vp = [m.sb(f"d_vp{q}", [P, KD, QUAD, CV]) for q in range(2)]
        rden = m.sb("d_rden", [P, KD, H])
        on = m.sb("d_on", [P, KD, D])
        ont = m.sb("d_ont", [P, KD, S])
        t_ps = [m.bank(f"d_t_ps{i}") for i in range(2)]
        s_ps = [m.bank(f"d_s_ps{i}") for i in range(SB)]
        o_ps = [m.bank(f"d_o_ps{i}") for i in range(KD)]
        small_ps = m.bank("d_small_ps")
        r = Routing(m, g, 1, t_ps[0], small_ps)
        names = ("moments_ready", "rstd_ready", "xn_ready", "gather_used", "t_done", "t_copied",
                 "scores_done", "max_ready", "exp_done", "vp_ready", "av_done", "on_ready", "x_done")
        (moments_ready, rstd_ready, xn_ready, gather_used, t_done, t_copied, scores_done, max_ready,
         exp_done, vp_ready, av_done, on_ready, x_done) = (m.sem("d_" + s) for s in names)
        ctx_loaded = [m.sem(f"d_ctx_loaded{p}") for p in range(2)]
        gathered = [m.sem(f"d_gathered{p}") for p in range(2)]
        T = 7

        block = m.stack.enter_context(nc.Block())

        @block.sync
        def _(sp):
            with sp.Fori(0, B // 2) as j:
                for p in range(2):
                    b = j * 2 + p
                    sp.wait_ge(x_done, b + 1)
                    sp.dma_start(ctx_in[p][:], io["ctx"][:, ds(b * KD, KD), :]).then_inc(ctx_loaded[p], 16)

        @block.gpsimd
        def _(pool):

            def gather(b, p):
                pool.wait_ge(gather_used, b + 1)
                nc.gpsimd.tensor_copy(idx[p][:], g.packed_i[:, ds(b * KD * TOPK, KD * TOPK)])
                pool.drain()
                for at in range(KD * TOPK):
                    pool.indirect_dma_start(
                        eo[p][:, at, :], None, g.expert_out[0],
                        bass.IndirectOffsetOnAxis(ap=idx[p][:, at:at + 1], axis=0)).then_inc(gathered[p], 16)

            def rest(j, p):
                b = j * 2 + p
                pool.wait_ge(moments_ready, b + 1)
                nc.gpsimd.tensor_tensor(rstd[:], moments[:, :, 1], bc(g.eps[:], 1, KD), ALU.add)
                pool.drain()
                nc.gpsimd.tensor_tensor(rstd[:], rstd[:], bc(g.neg_half[:], 1, KD), ALU.pow)\
                    .then_inc(rstd_ready, 1)
                r.gpsimd_rstd(nc, pool, b)
                r.gpsimd_scatter(nc, pool, j, p, b)

            gather(0, 0)
            with pool.Fori(0, B // 2 - 1) as j:
                for p in range(2):
                    gather(j * 2 + p + 1, 1 - p)
                    rest(j, p)
            gather(B - 1, 1)
            for p in range(2):
                rest(B // 2 - 1, p)
            for p in range(2):
                pool.wait_ge(r.scattered[p], r.per_batch * (B // 2))

        @block.scalar
        def _(act):
            with act.Fori(0, B // 2) as j:
                for p in range(2):
                    b = j * 2 + p
                    act.wait_ge(t_done, b * T + 1)
                    nc.scalar.copy(flat(xnt), t_ps[0][:]).then_inc(t_copied, 1)
                    act.wait_ge(t_done, b * T + 2)
                    nc.scalar.copy(flat(ctxt), t_ps[1][:]).then_inc(t_copied, 1)
                    act.wait_ge(t_done, b * T + 3)
                    nc.scalar.mul(flat(qt), t_ps[0][:], float(D) ** -0.5).then_inc(t_copied, 1)
                    act.wait_ge(t_done, b * T + 4)
                    for par in range(2):
                        k = nc.scalar.mul(flat(kt[par]), t_ps[1][:], g.parity[:, par:par + 1])
                    k.then_inc(t_copied, 1)
                    act.wait_ge(t_done, b * T + 5)
                    nc.scalar.copy(flat(v), t_ps[0][:]).then_inc(t_copied, 1)
                    for h in range(H):
                        s, q = h % (2 * QUAD), h // QUAD % 2
                        act.wait_ge(max_ready, b * H + h + 1)
                        act.wait_ge(av_done, b * H + h + 1)
                        for t in range(KD):
                            k = nc.scalar.activation(exps[s][:, t, :], s_ps[h % SB][:, t * S:(t + 1) * S], ACT.Exp,
                                                     bias=neg_max[:, s, t:t + 1],
                                                     accum_out=sums[:, q, t, h % QUAD:h % QUAD + 1])
                        k.then_inc(exp_done, 1)
                    act.wait_ge(t_done, b * T + 6)
                    nc.scalar.copy(flat(ont), t_ps[1][:]).then_inc(t_copied, 1)
                    r.scalar(nc, act, b)

        @block.vector
        def _(dve):
            dve.sem_inc(gather_used, 2)
            dve.sem_inc(x_done, 2)
            nc.vector.memset(g.seen[:], 0.0).then_inc(r.seen_ready, 1)
            def batch(j, p):
                b = j * 2 + p
                dve.wait_ge(gathered[p], (j + 1) * (16 * KD * TOPK))
                for k in range(TOPK):
                    for t in range(KD):
                        xb = g.x[:, ds(b * KD + t, 1), :]
                        last = nc.vector.scalar_tensor_tensor(
                            xb, eo[p][:, t * TOPK + k, :], g.share[:, k, ds(b * KD + t, 1)], xb,
                            ALU.mult, ALU.add)
                    if k == TOPK - 1:
                        last.then_inc(gather_used, 1)
                    dve.drain()
                for t in range(KD):
                    nc.vector.bn_stats(stats[:, t, :], g.x[:, ds(b * KD + t, 1), :])
                dve.drain()
                for t in range(KD):
                    k = nc.vector.bn_aggr(moments[:, t, :], stats[:, t, :])
                k.then_inc(moments_ready, 1)
                dve.drain()
                dve.wait_ge(rstd_ready, b + 1)
                for t in range(KD):
                    k = nc.vector.tensor_scalar(xn[:, t, :], g.x[:, ds(b * KD + t, 1), :],
                                                moments[:, t, 0:1], rstd[:, t:t + 1],
                                                ALU.subtract, ALU.mult)
                k.then_inc(xn_ready, 1)

                def scale_values(quad):
                    q = quad % 2
                    dve.drain()
                    dve.wait_ge(exp_done, b * H + (quad + 1) * QUAD)
                    nc.vector.reciprocal(sums[:, q, :, :], sums[:, q, :, :])
                    dve.drain()
                    by = sums[:, q, :, :].rearrange("p t (h a) -> p t h a", a=1)
                    nc.vector.tensor_tensor(
                        vp[q][:, :, :, 0:C],
                        v[:, :, quad * QUAD * C:(quad + 1) * QUAD * C].rearrange("p t (h c) -> p t h c", c=C),
                        bc(by, 3, C), ALU.mult)
                    nc.vector.tensor_copy(vp[q][:, :, :, C:CV], by).then_inc(vp_ready, 1)

                for h in range(H):
                    dve.wait_ge(scores_done, b * H + h + 1)
                    if h == 0:
                        dve.wait_ge(t_copied, b * (T - 1) + 5)
                    nc.vector.tensor_reduce(neg_max[:, h % (2 * QUAD), :],
                                            s_ps[h % SB][:].rearrange("p (t n) -> p t n", n=S),
                                            AX, ALU.max, negate=True).then_inc(max_ready, 1)
                    if h % QUAD == 1 and h > QUAD:
                        scale_values(h // QUAD - 1)
                scale_values(H // QUAD - 1)
                dve.wait_ge(av_done, b * H + H + 8)
                for t in range(KD):
                    o = o_ps[t][:, 0:H * CV].rearrange("p (h c) -> p h c", c=CV)
                    nc.vector.reciprocal(rden[:, t, :], o[:, :, C])
                dve.drain()
                for t in range(KD):
                    o = o_ps[t][:, 0:H * CV].rearrange("p (h c) -> p h c", c=CV)
                    k = nc.vector.tensor_tensor(on[:, t, :].rearrange("p (h c) -> p h c", c=C), o[:, :, 0:C],
                                                bc(rden[:, t, :].rearrange("p (h a) -> p h a", a=1), 2, C),
                                                ALU.mult)
                k.then_inc(on_ready, 1)
                dve.wait_ge(t_done, b * T + 7)
                xb = g.x[:, ds(b * KD, KD), :]
                nc.vector.scalar_tensor_tensor(xb, t_ps[1][:].rearrange("p (t d) -> p t d", d=D),
                                               g.gates[:, 1:2], xb, ALU.mult, ALU.add).then_inc(x_done, 1)
                dve.drain()
                r.vector(nc, dve, j, p, b)

            for p in range(2):
                batch(0, p)
            with dve.Fori(1, B // 2) as j:
                for p in range(2):
                    batch(j, p)

        @block.tensor
        def _(pe):
            pe.sem_inc(av_done, 8)
            pe.wait_ge(g.attn1_in, 16 * 6)
            with pe.Fori(0, B // 2) as j:
                for p in range(2):
                    b = j * 2 + p

                    def product(turn, out, lhs, rhs):
                        for i in range(KD):
                            for c in range(KD):
                                k = nc.tensor.matmul(out[:, i * 256:(i + 1) * 256],
                                                     lhs[:, c, i * P:(i + 1) * P], rhs[:, c, :],
                                                     start=c == 0, stop=c == KD - 1)
                        k.then_inc(t_done, 1)

                    def turn_over(out, src):
                        for t in range(KD):
                            for c in range(KD):
                                k = nc.tensor.transpose(out[:, c * S + t * P:c * S + (t + 1) * P],
                                                        src[:, t, c * P:(c + 1) * P], g.ident[:])
                        k.then_inc(t_done, 1)

                    pe.wait_ge(xn_ready, b + 1)
                    turn_over(t_ps[0], xn)
                    pe.wait_ge(ctx_loaded[p], (j + 1) * 16)
                    turn_over(t_ps[1], ctx_in[p])
                    pe.wait_ge(t_copied, b * (T - 1) + 1)
                    product(2, t_ps[0], g.wq1, xnt)
                    pe.wait_ge(t_copied, b * (T - 1) + 2)
                    product(3, t_ps[1], g.wk1, ctxt)
                    pe.wait_ge(t_copied, b * (T - 1) + 3)
                    product(4, t_ps[0], ctxt, g.wv1)

                    def scores(h):
                        r0 = h % 8 // 2 * 32
                        if h == 0:
                            pe.wait_ge(t_copied, b * (T - 1) + 4)
                        if h >= SB:
                            pe.wait_ge(exp_done, b * H + h - SB + 1)
                        for t in range(KD):
                            k = nc.tensor.matmul(s_ps[h % SB][:, t * S:(t + 1) * S],
                                                 kt[h % 2][r0:r0 + 32, h // 8, t * P:(t + 1) * P],
                                                 qt[r0:r0 + 32, h // 8, :], start=True, stop=True)
                        k.then_inc(scores_done, 1)

                    def weigh(h):
                        q = h // QUAD
                        if h % QUAD == 0:
                            pe.wait_ge(vp_ready, b * (H // QUAD) + q + 1)
                        for n in range(KD):
                            for t in range(KD):
                                k = nc.tensor.matmul(o_ps[n][:, h * CV:(h + 1) * CV],
                                                     exps[h % (2 * QUAD)][:, t, n * P:(n + 1) * P],
                                                     vp[q % 2][:, t, h % QUAD, :], start=t == 0, stop=t == KD - 1)
                        k.then_inc(av_done, 1)

                    for h in range(H + QUAD + 1):
                        if h < H:
                            scores(h)
                        if h > QUAD:
                            weigh(h - QUAD - 1)
                    pe.wait_ge(on_ready, b + 1)
                    turn_over(t_ps[1], on)
                    pe.wait_ge(t_copied, b * (T - 1) + 6)
                    product(6, t_ps[1], ont, g.wo1)
                    r.tensor(nc, pe, p, b)


def finish(nc, io, g):
    with Memory(nc) as m:
        idx = [m.sb(f"f_idx{p}", [P, KD * TOPK], i32) for p in range(2)]
        eo = [m.sb(f"f_eo{p}", [P, KD * TOPK, D]) for p in range(2)]
        shared = [m.sb(f"f_shared{p}", [P, KD, D]) for p in range(2)]
        rows_used = m.sem("f_rows_used")
        gathered = [m.sem(f"f_gathered{p}") for p in range(2)]
        shared_in = [m.sem(f"f_shared_in{p}") for p in range(2)]
        ready, stored = m.sem("f_ready"), m.sem("f_stored")
        block = m.stack.enter_context(nc.Block())

        @block.gpsimd
        def _(pool):
            with pool.Fori(0, B // 2) as j:
                for p in range(2):
                    b = j * 2 + p
                    pool.wait_ge(rows_used, b + 1)
                    nc.gpsimd.tensor_copy(idx[p][:], g.packed_i[:, ds(b * KD * TOPK, KD * TOPK)])
                    pool.drain()
                    for at in range(KD * TOPK):
                        pool.indirect_dma_start(
                            eo[p][:, at, :], None, g.expert_out[1],
                            bass.IndirectOffsetOnAxis(ap=idx[p][:, at:at + 1], axis=0)).then_inc(gathered[p], 16)

        @block.sync
        def _(sp):
            with sp.Fori(0, B // 2) as j:
                for p in range(2):
                    b = j * 2 + p
                    sp.wait_ge(rows_used, b + 1)
                    sp.dma_start(shared[p][:], g.expert_out[1][ds(b * S + NT * P, S), :]
                                 .rearrange("(t p) d -> p t d", p=P)).then_inc(shared_in[p], 16)

        @block.scalar
        def _(act):
            with act.Fori(0, B) as b:
                act.wait_ge(ready, b + 1)
                act.dma_start(io["out"][:, ds(b * KD, KD), :], g.x[:, ds(b * KD, KD), :]).then_inc(stored, 16)
            act.wait_ge(stored, 16 * B)

        @block.vector
        def _(dve):
            dve.sem_inc(rows_used, 2)
            with dve.Fori(0, B // 2) as j:
                for p in range(2):
                    b = j * 2 + p
                    dve.wait_ge(shared_in[p], (j + 1) * 16)
                    xb = g.x[:, ds(b * KD, KD), :]
                    nc.vector.scalar_tensor_tensor(xb, shared[p][:], g.gates[:, 3:4], xb, ALU.mult, ALU.add)
                    dve.drain()
                    dve.wait_ge(gathered[p], (j + 1) * (16 * KD * TOPK))
                    for k in range(TOPK):
                        for t in range(KD):
                            xb = g.x[:, ds(b * KD + t, 1), :]
                            last = nc.vector.scalar_tensor_tensor(
                                xb, eo[p][:, t * TOPK + k, :], g.share[:, k, ds(b * KD + t, 1)], xb,
                                ALU.mult, ALU.add)
                        dve.drain()
                    dve.sem_inc(rows_used, 1)
                    dve.sem_inc(ready, 1)


def build(nc, io, upto=99):
    with Memory(nc) as g:
        g.routed = nc.dram_tensor("routed_rows", [(E + 1) * REGION, D], f32, kind="Internal").ap()
        g.expert_out = [nc.dram_tensor(f"expert_rows{n}", [(NT + n * NTT) * P, D], f32, kind="Internal").ap()
                        for n in range(2)]
        g.x = g.sb("x", [P, NTT, D])
        g.ffn = g.sb("ffn", [P, E, 2 * KD * F + KF * D])
        g.ffn_flat = g.ffn[:].rearrange("p e n -> p (e n)")
        g.v_spec = g.sb("v_spec", [P, B, 2, D])
        g.v_flat = g.v_spec[:].rearrange("p b a d -> p (b a d)")
        g.ident = g.sb("ident", [P, P])
        g.ones = g.sb("ones", [P, P], bf16)
        g.before = g.sb("before", [P, P], bf16)
        g.zeros = g.sb("zeros", [P, D])
        g.neg_half, g.eps = g.sb("neg_half", [P, 1]), g.sb("eps", [P, 1])
        g.zero_i = g.sb("zero_i", [P, KD * TOPK], i32)
        g.not_dc, g.only_dc = g.sb("not_dc", [P, 1]), g.sb("only_dc", [P, 1])
        g.parity = g.sb("parity", [P, 2])
        g.parity_rows = g.sb("parity_rows", [P, 2, 4])
        g.expert_of, g.region_of = g.sb("expert_of", [P, E]), g.sb("region_of", [P, E])
        g.tile_no = g.sb("tile_no", [P, NT])
        g.gates = g.sb("gates", [P, 4])
        g.bo = g.sb("bo", [P, D])
        g.router0, g.router1 = g.sb("router0", [P, KD, E]), g.sb("router1", [P, KD, E])
        g.router_b = g.sb("router_b", [P, 1, E])
        g.seen = g.sb("seen", [P, E], bf16)
        g.top_v, g.top_f = g.sb("top_v", [P, NTT, TOPK]), g.sb("top_f", [P, NTT, TOPK])
        g.pos = g.sb("pos", [P, NTT, TOPK])
        g.packed_i = g.sb("packed_i", [P, NTT * TOPK], i32)
        g.share = g.sb("share", [P, TOPK, NTT])
        g.plan = g.sb("plan", [P, 2, NT + NTT + 2], i32)
        g.consts_made, g.later_in, g.ffn_in = g.sem("consts_made"), g.sem("later_in"), g.sem("ffn_in")
        g.gates_ready, g.attn1_in, g.ffn1_in = g.sem("gates_ready"), g.sem("attn1_in"), g.sem("ffn1_in")

        with Memory(nc) as m0:
            g.dft, g.icorr = m0.sb("dft", [P, KD, S]), m0.sb("icorr", [P, 2, S])
            g.iout, g.wo0 = m0.sb("iout", [P, 2, S]), m0.sb("wo0", [P, KD, D])
            g.cross = m0.sb("cross", [P, 2, B * H])
            g.w_same, g.w_other = m0.sb("w_same", [P, 2, B * H]), m0.sb("w_other", [P, 2, B * H])
            spectra(nc, io, g)
            if upto > 1: lags(nc, io, g)
            if upto > 2: mix(nc, io, g)
        if upto > 3: plan(nc, io, g, 0)
        if upto > 4: experts(nc, io, g, 0)
        with Memory(nc) as m1:
            g.wq1, g.wk1 = m1.sb("wq1", [P, KD, D]), m1.sb("wk1", [P, KD, D])
            g.wv1, g.wo1 = m1.sb("wv1", [P, KD, D]), m1.sb("wo1", [P, KD, D])
            if upto > 5: load_layer1(nc, io, g)
            if upto > 5: attention(nc, io, g)
        if upto > 6: plan(nc, io, g, 1)
        if upto > 7: experts(nc, io, g, 1)
        if upto > 8: finish(nc, io, g)


def load_layer1(nc, io, g):
    width = KD * F + KF * D
    w = g.ffn_flat[:, 0:(E + 1) * width].rearrange("p (e n) -> p e n", n=width)
    with nc.Block() as block:
        @block.sync
        def _(sp):
            for dst, name in ((g.wq1, "L1_xattn_Wq"), (g.wk1, "L1_xattn_Wk"), (g.wv1, "L1_xattn_Wv"),
                              (g.wo1, "L1_xattn_Wo")):
                sp.dma_start(dst[:], rows(io[name])).then_inc(g.attn1_in, 16)
            sp.dma_start(g.router1[:], rows(io["L1_ffn_router_w"])).then_inc(g.attn1_in, 16)
            sp.dma_start(g.router_b[:, 0, :], over_partitions(io["L1_ffn_router_b"], E)).then_inc(g.attn1_in, 16)
            for e in range(E + 1):
                up = io["L1_ffn_ew1"][e] if e < E else io["L1_ffn_sw1"]
                down = io["L1_ffn_ew2"][e] if e < E else io["L1_ffn_sw2"]
                sp.dma_start(w[:, e, 0:KD * F].rearrange("p (k n) -> p k n", k=KD), rows(up)).then_inc(g.ffn1_in, 16)
                sp.dma_start(w[:, e, KD * F:].rearrange("p (k n) -> p k n", k=KF), rows(down)).then_inc(g.ffn1_in, 16)


TRANSPOSED = ("L0_xattn_Wq", "L0_xattn_Wk", "L0_xattn_Wv", "L0_xattn_Wo", "L0_ffn_Wg", "L0_ffn_W1", "L0_ffn_W2",
              "L0_ffn_W3", "L1_xattn_Wq", "L1_xattn_Wk", "L1_xattn_Wv", "L1_xattn_Wo")


def transforms():
    t = np.arange(S)
    w = 2 * np.pi * np.outer(t, np.arange(S // 2)) / S
    cos, sin = np.cos(w), np.sin(w)
    sin[:, 0] = np.cos(np.pi * t)
    two = np.full(S // 2, 2.0 / S)
    two[0] = 1.0 / S
    sign = np.full(S // 2, -1.0)
    sign[0] = 1.0
    forward = np.concatenate([cos, sin], 1)
    from_cross = np.concatenate([cos * two, sin * two * sign], 1).T / C
    from_spectrum = np.concatenate([cos * two, sin * two], 1).T
    return {n: np.ascontiguousarray(a, np.float32)
            for n, a in (("dft", forward), ("icorr", from_cross), ("iout", from_spectrum))}


def kernel(**inputs):
    import concourse.bacc as bacc
    from concourse.bass_utils import run_bass_kernel_spmd

    nc = bacc.Bacc("TRN2", target_bir_lowering=False, num_devices=1)
    arrays = {}
    for name, a in inputs.items():
        a = np.asarray(a)
        arrays[name] = np.ascontiguousarray(np.swapaxes(a, -1, -2) if name in TRANSPOSED else a)
    arrays.update(transforms())
    io = {n: nc.dram_tensor(n, a.shape, mybir.dt.from_np(a.dtype), kind="ExternalInput").ap()
          for n, a in arrays.items()}
    out = nc.dram_tensor("out", (B, S, D), f32, kind="ExternalOutput").ap()
    by_tile = "b (t p) d -> p (b t) d"
    io["x"] = io["x"].rearrange(by_tile, p=P)
    io["ctx"] = io["ctx_1024"].rearrange(by_tile, p=P)
    io["out"] = out.rearrange(by_tile, p=P)
    build(nc, io)
    r = run_bass_kernel_spmd(nc, [arrays], core_ids=[0])
    return r.results[0]["out"]
```

```python
from contextlib import ExitStack

import numpy as np
import concourse.bass as bass
from concourse import mybir

P = 128
B, S, D = 16, 256, 256
H, C = 16, 16
KD = D // P
TOK = B * S
NTT = TOK // P
E, F = 8, 512
KF = F // P
TOPK, LAGS = 2, 5
NT = 2 * TOK // P + E
REGION = TOK + P
EPS = 1e-5
GROUP = P // H
HALF = TOK // P // 2
LOWEST, TAKEN = -3.0e38, -3.2e38

f32 = mybir.dt.float32
bf16 = mybir.dt.bfloat16
i32 = mybir.dt.int32
u32 = mybir.dt.uint32
ALU = mybir.AluOpType
ACT = mybir.ActivationFunctionType
AX = mybir.AxisListType.X
ds = bass.ds


class Memory:

    def __init__(self, nc):
        self.nc, self.stack = nc, ExitStack()

    def __enter__(self):
        return self

    def __exit__(self, *_):
        self.stack.close()

    def sb(self, name, shape, dt=f32):
        return self.stack.enter_context(self.nc.sbuf_tensor("sb_" + name, shape, dt))

    def bank(self, name, shape=(P, 512), dt=f32):
        return self.stack.enter_context(self.nc.psum_tensor(name, list(shape), dt))

    def sem(self, name):
        return self.stack.enter_context(self.nc.semaphore(name))


class Carved:

    def __init__(self, flat_ap, start):
        self.ap, self.at = flat_ap, start

    def take(self, a, b):
        self.at += a * b
        assert self.at <= self.ap.shape[1]
        return self.ap[:, self.at - a * b:self.at].rearrange("p (a b) -> p a b", a=a)


def rows(ap):
    return ap.rearrange("(k p) n -> p k n", p=P)


def over_partitions(ap, n):
    return ap.rearrange("(a n) -> a n", a=1).broadcast_to([P, n])


def flat(t):
    return t[:].rearrange("p a b -> p (a b)")


def wait_past_zero(engine, sem, value):
    if not isinstance(value, int) or value > 0:
        engine.wait_ge(sem, value)


def active(step, stage, count=B):
    return not isinstance(step, int) or 0 <= step - stage < count


def skewed(engine, depth, body, count=B):
    first = depth + depth % 2
    for step in range(first):
        body(step, step % 2)
    with engine.Fori(first // 2, count // 2) as j:
        for p in range(2):
            body(j * 2 + p, p)
    for step in range(count, count + depth):
        body(step, step % 2)


def filled(n, parity, inc):
    return n * (inc // 2) + inc - parity * (inc // 2)


def bc(ap, axis, n):
    shape = list(ap.shape)
    shape[axis] = n
    return ap.broadcast_to(shape)


def load_expert0(sp, io, g, e):
    for n, name in enumerate(("L0_ffn_W1", "L0_ffn_W2")):
        sp.dma_start(g.ffn[:, e, n * KD * F:(n + 1) * KD * F].rearrange("p (k n) -> p k n", k=KD),
                     rows(io[name][e])).then_inc(g.ffn_in, 16)
    sp.dma_start(g.ffn[:, e, 2 * KD * F:].rearrange("p (k n) -> p k n", k=KF),
                 rows(io["L0_ffn_W3"][e])).then_inc(g.ffn_in, 16)


def spectra(nc, io, g):
    with Memory(nc) as m:
        ctx_in = [m.sb(f"ctx_in{p}", [P, KD, D]) for p in range(2)]
        xn = [m.sb(f"xn{p}", [P, KD, D]) for p in range(2)]
        stats = m.sb("ln0_stats", [P, KD, 6])
        moments = m.sb("ln0_moments", [P, 2, KD, 2])
        rstd = m.sb("ln0_rstd", [P, 2, KD])
        spare = g.ffn[:, E - 1, :]
        wq = spare[:, 0:KD * D].rearrange("p (k n) -> p k n", k=KD)
        wkv = spare[:, KD * D:3 * KD * D].rearrange("p (k n) -> p k n", k=KD)
        bias0 = spare[:, 3 * KD * D:3 * KD * D + 3 * D]
        xf = [m.sb(f"xf{p}", [P, KD, S]) for p in range(2)]
        cf = [m.sb(f"cf{p}", [P, KD, S]) for p in range(2)]
        qs = m.sb("q_spec", [P, 2, D])
        ks = m.sb("k_spec", [P, 2, D])
        prod = m.sb("prod", [P, 4, D])
        summed = m.sb("prod_sum", [P, 4, H])
        edge = m.sb("edge", [P, 2, H])
        xf_ps, cf_ps = m.bank("xf_ps"), m.bank("cf_ps")
        q_ps = [m.bank(f"q_ps{t}") for t in range(2)]
        kv_ps = [m.bank(f"kv_ps{t}") for t in range(2)]

        consts_in = m.sem("a_consts_in")
        zeroed = m.sem("a_zeroed")
        in_loaded = [m.sem(f"a_in_loaded{p}") for p in range(2)]
        moments_ready, rstd_ready = m.sem("a_moments_ready"), m.sem("a_rstd_ready")
        xn_ready = m.sem("a_xn_ready")
        xf_done, cf_done = m.sem("a_xf_done"), m.sem("a_cf_done")
        xf_copied, cf_copied = m.sem("a_xf_copied"), m.sem("a_cf_copied")
        q_done, kv_done = m.sem("a_q_done"), m.sem("a_kv_done")
        act_copied, dve_copied = m.sem("a_sin_copied"), m.sem("a_cos_copied")
        spec_used = m.sem("a_spec_used")
        bias_ready = m.sem("a_bias_ready")
        block = m.stack.enter_context(nc.Block())

        @block.sync
        def _(sp):
            sp.dma_start(g.dft[:], rows(io["dft"])).then_inc(consts_in, 16)
            sp.dma_start(wq[:], rows(io["L0_xattn_Wq"])).then_inc(consts_in, 16)
            sp.dma_start(wkv[:, :, 0:D], rows(io["L0_xattn_Wk"])).then_inc(consts_in, 16)
            sp.dma_start(wkv[:, :, D:2 * D], rows(io["L0_xattn_Wv"])).then_inc(consts_in, 16)
            sp.wait_ge(zeroed, 1)
            for n, name in enumerate(("L0_xattn_bq", "L0_xattn_bk", "L0_xattn_bv")):
                sp.dma_start(bias0[0:1, n * D:(n + 1) * D],
                             io[name].rearrange("(a n) -> a n", a=1)).then_inc(consts_in, 16)
            with sp.Fori(0, B // 2) as j:
                for p in range(2):
                    b = j * 2 + p
                    sp.wait_ge(cf_done, b + 1)
                    sp.dma_start(ctx_in[p][:], io["ctx"][:, ds(b * KD, KD), :]).then_inc(in_loaded[p], 16)
                    sp.dma_start(g.x[:, ds(b * KD, KD), :], io["x"][:, ds(b * KD, KD), :])\
                        .then_inc(in_loaded[p], 16)
            sp.dma_start(g.icorr[:], rows(io["icorr"])).then_inc(g.later_in, 16)
            sp.dma_start(g.iout[:], rows(io["iout"])).then_inc(g.later_in, 16)
            sp.dma_start(g.wo0[:], rows(io["L0_xattn_Wo"])).then_inc(g.later_in, 16)
            sp.dma_start(g.router0[:], rows(io["L0_ffn_Wg"])).then_inc(g.later_in, 16)
            sp.dma_start(g.bo[:], over_partitions(io["L0_xattn_bo"], D)).then_inc(g.later_in, 16)
            sp.dma_start(g.gates[:, 0:2], over_partitions(io["g_xattn"], 2)).then_inc(g.later_in, 16)
            sp.dma_start(g.gates[:, 2:4], over_partitions(io["g_ffn"], 2)).then_inc(g.later_in, 16)
            for e in range(E - 1):
                load_expert0(sp, io, g, e)

        @block.gpsimd
        def _(pool):
            nc.gpsimd.memset(bias0, 0.0).then_inc(zeroed, 1)
            nc.gpsimd.memset(g.neg_half[:], -0.5)
            nc.gpsimd.memset(g.eps[:], EPS)
            nc.gpsimd.memset(g.zero_i[:], 0)
            nc.gpsimd.memset(g.ones[:], 1.0)
            nc.gpsimd.memset(g.before[:], 1.0)
            nc.gpsimd.memset(g.ident[:], 0.0)
            nc.gpsimd.memset(g.not_dc[:], 1.0)
            nc.gpsimd.memset(g.only_dc[:], 0.0)
            nc.gpsimd.memset(g.parity[:], 0.0)
            nc.gpsimd.memset(g.zeros[:], 0.0)
            nc.gpsimd.iota(g.expert_of[:], pattern=[[1, E]], base=0, channel_multiplier=0, allow_small_or_imprecise_dtypes=True)
            nc.gpsimd.iota(g.region_of[:], pattern=[[REGION, E]], base=0, channel_multiplier=0, allow_small_or_imprecise_dtypes=True)
            nc.gpsimd.iota(g.tile_no[:], pattern=[[1, NT]], base=0, channel_multiplier=0, allow_small_or_imprecise_dtypes=True)
            pool.drain()
            nc.gpsimd.memset(g.not_dc[0:1, :], 0.0)
            nc.gpsimd.memset(g.only_dc[0:1, :], 1.0)
            nc.gpsimd.affine_select(out=g.before[:], in_=g.before[:], compare_op=ALU.is_gt, fill=0.0,
                                    base=0, pattern=[[1, P]], channel_multiplier=-1)
            nc.gpsimd.affine_select(out=g.ident[:], in_=g.ident[:], compare_op=ALU.not_equal, fill=1.0,
                                    base=0, pattern=[[-1, P]], channel_multiplier=1)
            for par in range(2):
                v = g.parity_rows[:, par, :]
                nc.gpsimd.memset(v, 1.0)
            pool.drain()
            for par in range(2):
                v = g.parity_rows[:, par, :]
                nc.gpsimd.affine_select(out=v, in_=v, compare_op=ALU.is_ge, fill=0.0, base=-16 * par,
                                        pattern=[[-32, 4]], channel_multiplier=1)
            pool.drain()
            for par in range(2):
                v = g.parity_rows[:, par, :]
                nc.gpsimd.affine_select(out=v, in_=v, compare_op=ALU.is_ge, fill=0.0, base=16 * par + 15,
                                        pattern=[[32, 4]], channel_multiplier=-1)\
                    .then_inc(g.consts_made, 1)

            def scale_of_rows(b, p):
                pool.wait_ge(moments_ready, b + 1)
                nc.gpsimd.tensor_tensor(rstd[:, p, :], moments[:, p, :, 1], bc(g.eps[:], 1, KD), ALU.add)
                pool.drain()
                nc.gpsimd.tensor_tensor(rstd[:, p, :], rstd[:, p, :], bc(g.neg_half[:], 1, KD), ALU.pow)\
                    .then_inc(rstd_ready, 1)

            pool.drain()
            with pool.Fori(0, B // 2) as j:
                for p in range(2):
                    scale_of_rows(j * 2 + p, p)

        @block.scalar
        def _(act):
            act.sem_inc(xf_copied, 1)
            act.sem_inc(cf_copied, 1)
            act.wait_ge(zeroed, 1)
            act.wait_ge(consts_in, 16 * 7)
            nc.scalar.mul(bias0, bias0, float(S)).then_inc(bias_ready, 1)

            def spectra_in(b, p):
                act.wait_ge(xf_done, b + 3)
                nc.scalar.copy(flat(xf[p]), xf_ps[:]).then_inc(xf_copied, 1)
                act.wait_ge(cf_done, b + 3)
                nc.scalar.copy(flat(cf[p]), cf_ps[:]).then_inc(cf_copied, 1)

            def sines(b, p):
                act.wait_ge(q_done, b + 1)
                act.wait_ge(spec_used, b + 1)
                nc.scalar.copy(qs[:, 1, :], q_ps[1][:, 0:D])
                act.wait_ge(kv_done, b * 2 + 2)
                nc.scalar.copy(ks[:, 1, :], kv_ps[1][:, 0:D])
                nc.scalar.copy(g.v_spec[:, ds(b, 1), 1, :], kv_ps[1][:, D:2 * D]).then_inc(act_copied, 1)

            spectra_in(0, 0)
            with act.Fori(0, B // 2 - 1) as j:
                for p in range(2):
                    spectra_in(j * 2 + p + 1, 1 - p)
                    sines(j * 2 + p, p)
            spectra_in(B - 1, 1)
            sines(B - 2, 0)
            sines(B - 1, 1)

        @block.vector
        def _(dve):
            dve.sem_inc(spec_used, 1)

            def normalise(b, p):
                dve.wait_ge(in_loaded[p], b * 16 + (32 - 16 * p))
                for t in range(KD):
                    nc.vector.bn_stats(stats[:, t, :], g.x[:, ds(b * KD + t, 1), :])
                dve.drain()
                for t in range(KD):
                    k = nc.vector.bn_aggr(moments[:, p, t, :], stats[:, t, :])
                k.then_inc(moments_ready, 1)
                dve.drain()
                dve.wait_ge(rstd_ready, b + 1)
                dve.wait_ge(xf_done, b + 1)
                for t in range(KD):
                    k = nc.vector.tensor_scalar(xn[p][:, t, :], g.x[:, ds(b * KD + t, 1), :],
                                                moments[:, p, t, 0:1], rstd[:, p, t:t + 1],
                                                ALU.subtract, ALU.mult)
                k.then_inc(xn_ready, 1)

            def cross_spectrum(b, p):
                dve.wait_ge(q_done, b + 1)
                nc.vector.tensor_tensor(qs[:, 0, :], q_ps[0][:, 0:D], bias0[:, 0:D], ALU.add)
                dve.wait_ge(kv_done, b * 2 + 1)
                nc.vector.tensor_tensor(ks[:, 0, :], kv_ps[0][:, 0:D], bias0[:, D:2 * D], ALU.add)
                nc.vector.tensor_tensor(g.v_spec[:, ds(b, 1), 0, :], kv_ps[0][:, D:2 * D],
                                        bias0[:, 2 * D:3 * D], ALU.add).then_inc(dve_copied, 1)
                dve.drain()
                dve.wait_ge(act_copied, b + 1)
                nc.vector.tensor_tensor(prod[:, 0:2, :], qs[:], ks[:], ALU.mult)
                nc.vector.tensor_tensor(prod[:, 2, :], qs[:, 0, :], ks[:, 1, :], ALU.mult)
                nc.vector.tensor_tensor(prod[:, 3, :], qs[:, 1, :], ks[:, 0, :], ALU.mult)\
                    .then_inc(spec_used, 1)
                dve.drain()
                nc.vector.tensor_reduce(summed[:], prod[:].rearrange("p a (h c) -> p a h c", c=C), AX, ALU.add)
                dve.drain()
                nc.vector.scalar_tensor_tensor(g.cross[:, 0, ds(b * H, H)], summed[:, 1, :], g.not_dc[:],
                                               summed[:, 0, :], ALU.mult, ALU.add)
                nc.vector.tensor_tensor(edge[:, 0, :], summed[:, 2, :], summed[:, 3, :], ALU.subtract)
                nc.vector.tensor_scalar(edge[:, 1, :], summed[:, 1, :], g.only_dc[:], None, ALU.mult)
                dve.drain()
                nc.vector.scalar_tensor_tensor(g.cross[:, 1, ds(b * H, H)], edge[:, 0, :], g.not_dc[:],
                                               edge[:, 1, :], ALU.mult, ALU.add)

            normalise(0, 0)
            normalise(1, 1)
            dve.wait_ge(bias_ready, 1)
            dve.wait_ge(g.consts_made, 2)
            nc.vector.tensor_reduce(g.parity[:], g.parity_rows[:], AX, ALU.add)
            with dve.Fori(0, B // 2 - 1) as j:
                for p in range(2):
                    b = j * 2 + p
                    normalise(b + 2, p)
                    cross_spectrum(b, p)
            cross_spectrum(B - 2, 0)
            cross_spectrum(B - 1, 1)

        @block.tensor
        def _(pe):
            pe.sem_inc(xf_done, 2)
            pe.sem_inc(cf_done, 2)

            def forward(b, p):
                pe.wait_ge(xn_ready, b + 1)
                pe.wait_ge(xf_copied, b + 1)
                for c in range(KD):
                    for t in range(KD):
                        k = nc.tensor.matmul(xf_ps[:, c * S:(c + 1) * S], xn[p][:, t, c * P:(c + 1) * P],
                                             g.dft[:, t, :], start=t == 0, stop=t == KD - 1)
                k.then_inc(xf_done, 1)
                pe.wait_ge(in_loaded[p], b * 16 + (32 - 16 * p))
                pe.wait_ge(cf_copied, b + 1)
                for c in range(KD):
                    for t in range(KD):
                        k = nc.tensor.matmul(cf_ps[:, c * S:(c + 1) * S], ctx_in[p][:, t, c * P:(c + 1) * P],
                                             g.dft[:, t, :], start=t == 0, stop=t == KD - 1)
                k.then_inc(cf_done, 1)

            def project(b, p):
                pe.wait_ge(xf_copied, b + 2)
                wait_past_zero(pe, act_copied, b)
                wait_past_zero(pe, dve_copied, b)
                for f in range(2):
                    for c in range(KD):
                        k = nc.tensor.matmul(q_ps[f][:, 0:D], xf[p][:, c, f * P:(f + 1) * P],
                                             wq[:, c, :], start=c == 0, stop=c == KD - 1)
                k.then_inc(q_done, 1)
                pe.wait_ge(cf_copied, b + 2)
                for f in range(2):
                    for c in range(KD):
                        k = nc.tensor.matmul(kv_ps[f][:], cf[p][:, c, f * P:(f + 1) * P],
                                             wkv[:, c, :], start=c == 0, stop=c == KD - 1)
                    k.then_inc(kv_done, 1)

            pe.wait_ge(consts_in, 16 * 7)
            forward(0, 0)
            forward(1, 1)
            project(0, 0)
            with pe.Fori(1, B // 2) as j:
                for p in range(2):
                    b = j * 2 + p
                    forward(b, p)
                    project(b - 1, 1 - p)
            project(B - 1, 1)


def lags(nc, io, g):
    G2 = B // GROUP
    with Memory(nc) as m:
        corr = m.sb("corr", [P, G2, S + 8])
        left = m.sb("corr_left", [P, G2, S + 8])
        top8 = m.sb("top8", [P, G2, 8])
        best = m.sb("best", [P, G2, 8])
        neg_max = m.sb("neg_max", [P, G2])
        expd = m.sb("lag_exp", [P, G2, S])
        weight = m.sb("lag_weight", [P, G2, S])
        total = m.sb("lag_total", [P, G2])
        weight_t = m.sb("lag_weight_t", [P, KD, G2 * P])
        corr_ps = [m.bank(f"corr_ps{i}") for i in range(G2)]
        wt_ps, ws_ps = m.bank("wt_ps"), m.bank("ws_ps")
        corr_done, exp_in, exp_done = m.sem("b_corr_done"), m.sem("b_exp_in"), m.sem("b_exp_done")
        weight_ready, wt_done, wt_copied = m.sem("b_weight_ready"), m.sem("b_wt_done"), m.sem("b_wt_copied")
        ws_done = m.sem("b_ws_done")
        block = m.stack.enter_context(nc.Block())

        @block.sync
        def _(sp):
            load_expert0(sp, io, g, E - 1)

        @block.tensor
        def _(pe):
            pe.wait_ge(g.later_in, 16 * 7)
            for i in range(G2):
                for f in range(2):
                    k = nc.tensor.matmul(corr_ps[i][:, 0:S], g.cross[:, f, i * P:(i + 1) * P],
                                         g.icorr[:, f, :], start=f == 0, stop=f == 1)
                k.then_inc(corr_done, 1)
            for i in range(G2):
                pe.wait_ge(weight_ready, i + 1)
                for t in range(KD):
                    k = nc.tensor.transpose(wt_ps[:, t * G2 * P + i * P:t * G2 * P + (i + 1) * P],
                                            weight[:, i, t * P:(t + 1) * P], g.ident[:])
            k.then_inc(wt_done, 1)
            pe.wait_ge(wt_copied, 1)
            for f in range(2):
                for t in range(KD):
                    k = nc.tensor.matmul(ws_ps[:, f * B * H:(f + 1) * B * H], g.dft[:, t, f * P:(f + 1) * P],
                                         weight_t[:, t, :], start=t == 0, stop=t == KD - 1)
            k.then_inc(ws_done, 1)

        @block.scalar
        def _(act):
            act.wait_ge(g.later_in, 16 * 7)
            nc.scalar.activation(g.gates[:], g.gates[:], ACT.Tanh).then_inc(g.gates_ready, 1)
            for i in range(G2):
                act.wait_ge(exp_in, i + 1)
                nc.scalar.activation(expd[:, i, :], corr[:, i, 0:S], ACT.Exp, bias=neg_max[:, i:i + 1])\
                    .then_inc(exp_done, 1)
            act.wait_ge(wt_done, 1)
            nc.scalar.copy(flat(weight_t), wt_ps[:]).then_inc(wt_copied, 1)

        @block.vector
        def _(dve):
            nc.vector.memset(corr[:], LOWEST)
            nc.vector.memset(best[:], LOWEST)
            dve.drain()
            for i in range(G2):
                dve.wait_ge(corr_done, i + 1)
                nc.vector.tensor_copy(corr[:, i, 0:S], corr_ps[i][:, 0:S])
                dve.drain()
                nc.vector.max(top8[:, i, :], corr[:, i, 0:S])
                dve.drain()
                nc.vector.tensor_scalar(neg_max[:, i:i + 1], top8[:, i, 0:1], -1.0, None, ALU.mult)\
                    .then_inc(exp_in, 1)
                nc.vector.tensor_copy(best[:, i, 0:LAGS], top8[:, i, 0:LAGS])
                dve.drain()
                nc.vector.match_replace(left[:, i, :], best[:, i, :], corr[:, i, :], TAKEN)
            dve.drain()
            for i in range(G2):
                dve.wait_ge(exp_done, i + 1)
                nc.vector.scalar_tensor_tensor(weight[:, i, :], left[:, i, 0:S], (LOWEST + TAKEN) / 2,
                                               expd[:, i, :], ALU.is_lt, ALU.mult,
                                               accum_out=total[:, i:i + 1])
                dve.drain()
                nc.vector.reciprocal(total[:, i:i + 1], total[:, i:i + 1])
                dve.drain()
                nc.vector.tensor_scalar(weight[:, i, :], weight[:, i, :], total[:, i:i + 1], None, ALU.mult)\
                    .then_inc(weight_ready, 1)
            dve.wait_ge(ws_done, 1)
            nc.vector.tensor_copy(g.w_same[:, 0, :], ws_ps[:, 0:B * H])
            nc.vector.tensor_scalar(g.w_other[:, 1, :], ws_ps[:, B * H:2 * B * H], g.not_dc[:], None, ALU.mult)
            nc.vector.tensor_scalar(g.w_other[:, 0, :], ws_ps[:, B * H:2 * B * H], g.not_dc[:], -1.0,
                                    ALU.mult, ALU.mult)
            nc.vector.tensor_scalar(g.w_same[:, 1, :], ws_ps[:, B * H:2 * B * H], g.only_dc[:], None, ALU.mult)
            dve.drain()
            nc.vector.scalar_tensor_tensor(g.w_same[:, 1, :], g.w_same[:, 0, :], g.not_dc[:],
                                           g.w_same[:, 1, :], ALU.mult, ALU.add)


class Routing:

    def __init__(self, m, g, layer, xr_ps, small_ps):
        self.g, self.layer, self.xr_ps, self.small_ps = g, layer, xr_ps, small_ps
        n = f"r{layer}_"
        self.stats = m.sb(n + "stats", [P, KD, 6])
        self.moments = m.sb(n + "moments", [P, KD, 2])
        self.rstd = m.sb(n + "rstd", [P, KD])
        self.xr = [m.sb(n + f"xr{p}", [P, KD, D]) for p in range(2)]
        self.xrt = m.sb(n + "xrt", [P, KD, S])
        self.logits = m.sb(n + "logits", [P, KD, E])
        self.top_v = m.sb(n + "top_v", [P, KD, 8])
        self.top_f = m.sb(n + "top_f", [P, KD, TOPK])
        self.top_i = m.sb(n + "top_i", [P, KD, 8], u32)
        self.onehot = m.sb(n + "onehot", [P, KD, TOPK, E])
        self.mask = m.sb(n + "mask", [P, KD, E], bf16)
        self.rank = m.sb(n + "rank", [P, KD, E])
        self.pos_f = m.sb(n + "pos_f", [P, KD, TOPK, E])
        self.to = [m.sb(n + f"to{p}", [P, KD * TOPK], i32) for p in range(2)]
        self.pos_i = [m.sb(n + f"pos_i{p}", [P, KD * TOPK], i32) for p in range(2)]
        (self.moments_ready, self.rstd_ready, self.xr_ready, self.xrt_done, self.xrt_copied,
         self.logits_done, self.mask_ready, self.rank_done, self.pos_ready, self.seen_ready) = (
            m.sem(n + s) for s in ("moments_ready", "rstd_ready", "xr_ready", "xrt_done", "xrt_copied",
                                   "logits_done", "mask_ready", "rank_done", "pos_ready", "seen_ready"))
        self.scattered = [m.sem(n + f"scattered{p}") for p in range(2)]
        self.per_batch = 16 * (KD * TOPK + (1 if layer else 0))

    def vector_norm(self, nc, dve, b):
        for t in range(KD):
            nc.vector.bn_stats(self.stats[:, t, :], self.g.x[:, ds(b * KD + t, 1), :])
        dve.drain()
        for t in range(KD):
            k = nc.vector.bn_aggr(self.moments[:, t, :], self.stats[:, t, :])
        k.then_inc(self.moments_ready, 1)

    def vector_rows(self, nc, dve, b, p):
        dve.wait_ge(self.rstd_ready, b + 1)
        if not self.layer:
            nc.vector.reciprocal(self.rstd[:], self.rstd[:])
            dve.drain()
        if not isinstance(b, int) or b >= 2:
            dve.wait_ge(self.scattered[p], filled(b - 2, p, self.per_batch))
        for t in range(KD):
            k = nc.vector.tensor_scalar(self.xr[p][:, t, :], self.g.x[:, ds(b * KD + t, 1), :],
                                        self.moments[:, t, 0:1], self.rstd[:, t:t + 1],
                                        ALU.subtract, ALU.mult)
        k.then_inc(self.xr_ready, 1)

    def vector_pick(self, nc, dve, b):
        g = self.g
        dve.wait_ge(self.logits_done, b + 1)
        logits_ps = self.small_ps[:, 0:KD * E].rearrange("p (t e) -> p t e", e=E)
        if self.layer:
            nc.vector.tensor_tensor(self.logits[:], logits_ps, bc(g.router_b[:], 1, KD), ALU.add)
        else:
            nc.vector.tensor_copy(self.logits[:], logits_ps)
        dve.drain()
        for t in range(KD):
            nc.vector.max(self.top_v[:, t, :], self.logits[:, t, :])
        dve.drain()
        for t in range(KD):
            nc.vector.max_index(self.top_i[:, t, :], self.top_v[:, t, :], self.logits[:, t, :])
        nc.vector.tensor_copy(g.top_v[:, ds(b * KD, KD), :], self.top_v[:, :, 0:TOPK])
        dve.drain()
        nc.vector.tensor_copy(self.top_f[:], self.top_i[:, :, 0:TOPK])
        dve.drain()
        nc.vector.tensor_copy(g.top_f[:, ds(b * KD, KD), :], self.top_f[:])
        nc.vector.tensor_tensor(self.onehot[:].rearrange("p t k e -> p (t k) e"),
                                bc(g.expert_of[:].rearrange("p (a e) -> p a e", a=1), 1, KD * TOPK),
                                bc(self.top_f[:].rearrange("p t (k c) -> p (t k) c", c=1), 2, E), ALU.is_equal)
        dve.drain()
        nc.vector.tensor_tensor(self.mask[:], self.onehot[:, :, 0, :], self.onehot[:, :, 1, :], ALU.add)\
            .then_inc(self.mask_ready, 1)

    def vector_place(self, nc, dve, b, p):
        g = self.g
        dve.wait_ge(self.rank_done, b + 1)
        rank_ps = self.small_ps[:, 32:32 + KD * E].rearrange("p (t e) -> p t e", e=E)
        nc.vector.tensor_tensor(self.rank[:], rank_ps, bc(g.region_of[:].rearrange("p (a e) -> p a e", a=1), 1, KD),
                                ALU.add)
        nc.vector.tensor_tensor(g.seen[:], g.seen[:], self.mask[:, 0, :], ALU.add)
        dve.drain()
        nc.vector.tensor_tensor(g.seen[:], g.seen[:], self.mask[:, 1, :], ALU.add).then_inc(self.seen_ready, 1)
        for t in range(KD):
            nc.vector.tensor_tensor(self.pos_f[:, t, :, :], self.onehot[:, t, :, :],
                                    bc(self.rank[:, t:t + 1, :], 1, TOPK), ALU.mult)
        dve.drain()
        pos = g.pos[:, ds(b * KD, KD), :]
        nc.vector.tensor_reduce(pos, self.pos_f[:], AX, ALU.add)
        dve.drain()
        nc.vector.tensor_copy(self.pos_i[p][:].rearrange("p (t k) -> p t k", k=TOPK), pos)\
            .then_inc(self.pos_ready, 1)

    def gpsimd_rstd(self, nc, pool, b):
        pool.wait_ge(self.moments_ready, b + 1)
        nc.gpsimd.tensor_tensor(self.rstd[:], self.moments[:, :, 1], bc(self.g.eps[:], 1, KD), ALU.add)
        pool.drain()
        nc.gpsimd.tensor_tensor(self.rstd[:], self.rstd[:], bc(self.g.neg_half[:], 1, KD), ALU.pow)\
            .then_inc(self.rstd_ready, 1)

    def scalar_deviation(self, nc, act, b):
        act.wait_ge(self.moments_ready, b + 1)
        nc.scalar.activation(self.rstd[:], self.moments[:, :, 1], ACT.Sqrt, bias=self.g.eps[:])\
            .then_inc(self.rstd_ready, 1)

    def gpsimd_scatter(self, nc, pool, b, p):
        pool.wait_ge(self.pos_ready, b + 1)
        nc.gpsimd.tensor_tensor(self.to[p][:], self.pos_i[p][:], self.g.zero_i[:], ALU.add)
        pool.drain()
        for t in range(KD):
            for k in range(TOPK):
                at = t * TOPK + k
                pool.indirect_dma_start(
                    self.g.routed, bass.IndirectOffsetOnAxis(ap=self.to[p][:, at:at + 1], axis=0),
                    self.xr[p][:, t, :], None).then_inc(self.scattered[p], 16)
        if self.layer:
            pool.dma_start(
                self.g.routed[ds(b * S + E * REGION, S), :].rearrange("(t p) d -> p t d", p=P),
                self.xr[p][:]).then_inc(self.scattered[p], 16)

    def scalar(self, nc, act, b):
        act.wait_ge(self.xrt_done, b + 1)
        nc.scalar.copy(flat(self.xrt), self.xr_ps[:]).then_inc(self.xrt_copied, 1)

    def tensor_turn(self, nc, pe, b, p):
        g = self.g
        pe.wait_ge(self.xr_ready, b + 1)
        for t in range(KD):
            for c in range(KD):
                k = nc.tensor.transpose(self.xr_ps[:, c * S + t * P:c * S + (t + 1) * P],
                                        self.xr[p][:, t, c * P:(c + 1) * P], g.ident[:])
        k.then_inc(self.xrt_done, 1)

    def tensor_logits(self, nc, pe, b):
        g = self.g
        pe.wait_ge(self.xrt_copied, b + 1)
        pe.wait_ge(self.seen_ready, b + 1)
        router = g.router1 if self.layer else g.router0
        for t in range(KD):
            for c in range(KD):
                k = nc.tensor.matmul(self.small_ps[:, t * E:(t + 1) * E], self.xrt[:, c, t * P:(t + 1) * P],
                                     router[:, c, :], start=c == 0, stop=c == KD - 1)
        k.then_inc(self.logits_done, 1)

    def tensor_rank(self, nc, pe, b):
        g = self.g
        pe.wait_ge(self.mask_ready, b + 1)
        pe.wait_ge(self.seen_ready, b + 1)
        for t in range(KD):
            out = self.small_ps[:, 32 + t * E:32 + (t + 1) * E]
            nc.tensor.matmul(out, g.before[:], self.mask[:, t, :], start=True, stop=False)
            if t:
                nc.tensor.matmul(out, g.ones[:], self.mask[:, 0, :], start=False, stop=False)
            k = nc.tensor.matmul(out, g.ones[:], g.seen[:], start=False, stop=True)
        k.then_inc(self.rank_done, 1)


def mix(nc, io, g):
    with Memory(nc) as m:
        same = m.sb("same", [P, 2, D])
        other = m.sb("other", [P, 2, D])
        spec = [m.sb(f"out_spec{p}", [P, 2, D]) for p in range(2)]
        ot = m.sb("ot", [P, KD, S])
        one_row = m.sb("one_row", [1, P])
        ot_ps, y_ps, xr_ps, small_ps = m.bank("ot_ps"), m.bank("y_ps"), m.bank("xr_ps"), m.bank("small_ps")
        r = Routing(m, g, 0, xr_ps, small_ps)
        other_ready = m.sem("c_other_ready")
        spec_ready, ot_done, ot_copied = m.sem("c_spec_ready"), m.sem("c_ot_done"), m.sem("c_ot_copied")
        y_done, x_done, ones_ready = m.sem("c_y_done"), m.sem("c_x_done"), m.sem("c_ones_ready")
        block = m.stack.enter_context(nc.Block())

        def heads(ap):
            return ap.rearrange("p a (h c) -> p a h c", c=C)

        def per_head(w, b, a):
            return bc(w[:, a, ds(b * H, H)].rearrange("p (h c) -> p h c", c=1), 2, C)

        @block.gpsimd
        def _(pool):
            nc.gpsimd.memset(one_row[:], 1.0).then_inc(ones_ready, 1)

            def body(s, p):
                if active(s, 0):
                    pool.wait_ge(spec_ready, s + 1)
                    for a in range(2):
                        k = nc.gpsimd.tensor_tensor(
                            other[:, a, :].rearrange("p (h c) -> p h c", c=C),
                            g.v_spec[:, ds(s, 1), 1 - a, :].rearrange("p a (h c) -> p (a h) c", c=C),
                            per_head(g.w_other, s, a), ALU.mult)
                    k.then_inc(other_ready, 1)
                if active(s, 3):
                    r.gpsimd_scatter(nc, pool, s - 3, 1 - p)

            skewed(pool, 3, body)
            for p in range(2):
                pool.wait_ge(r.scattered[p], r.per_batch * (B // 2))

        @block.scalar
        def _(act):
            def body(s, p):
                if active(s, 1):
                    act.wait_ge(ot_done, s)
                    nc.scalar.copy(flat(ot), ot_ps[:]).then_inc(ot_copied, 1)
                if active(s, 2):
                    r.scalar(nc, act, s - 2)
                if active(s, 1):
                    r.scalar_deviation(nc, act, s - 1)

            act.preload_act_table(ACT.Sqrt)
            skewed(act, 3, body)

        @block.vector
        def _(dve):
            dve.sem_inc(spec_ready, 1)
            nc.vector.memset(g.seen[:], 0.0).then_inc(r.seen_ready, 1)

            def body(s, p):
                dve.drain()
                if active(s, 0):
                    for a in range(2):
                        nc.vector.tensor_tensor(
                            same[:, a, :].rearrange("p (h c) -> p h c", c=C),
                            g.v_spec[:, ds(s, 1), a, :].rearrange("p a (h c) -> p (a h) c", c=C),
                            per_head(g.w_same, s, a), ALU.mult)
                    dve.drain()
                if active(s, 3):
                    r.vector_place(nc, dve, s - 3, 1 - p)
                if active(s, 0):
                    dve.wait_ge(other_ready, s + 1)
                    nc.vector.tensor_tensor(spec[p][:], same[:], other[:], ALU.add).then_inc(spec_ready, 1)
                if active(s, 1):
                    b = s - 1
                    dve.wait_ge(y_done, b + 1)
                    xb = g.x[:, ds(b * KD, KD), :]
                    nc.vector.scalar_tensor_tensor(xb, y_ps[:].rearrange("p (t d) -> p t d", d=D),
                                                   g.gates[:, 0:1], xb, ALU.mult, ALU.add).then_inc(x_done, 1)
                    dve.drain()
                    r.vector_norm(nc, dve, b)
                if active(s, 2):
                    r.vector_pick(nc, dve, s - 2)
                if active(s, 1):
                    r.vector_rows(nc, dve, s - 1, 1 - p)

            skewed(dve, 3, body)

        @block.tensor
        def _(pe):
            pe.wait_ge(ones_ready, 1)

            def body(s, p):
                b = s - 1
                if active(s, 1):
                    pe.wait_ge(spec_ready, b + 2)
                    for c in range(KD):
                        for f in range(2):
                            k = nc.tensor.matmul(ot_ps[:, c * S:(c + 1) * S], spec[1 - p][:, f, c * P:(c + 1) * P],
                                                 g.iout[:, f, :], start=f == 0, stop=f == 1)
                    k.then_inc(ot_done, 1)
                if active(s, 3):
                    r.tensor_rank(nc, pe, s - 3)
                if active(s, 2):
                    r.tensor_turn(nc, pe, s - 2, p)
                if active(s, 1):
                    pe.wait_ge(ot_copied, b + 1)
                    wait_past_zero(pe, x_done, b)
                    for t in range(KD):
                        out = y_ps[:, t * D:(t + 1) * D]
                        nc.tensor.matmul(out, one_row[:], g.bo[0:1, :], start=True, stop=False)
                        for c in range(KD):
                            k = nc.tensor.matmul(out, ot[:, c, t * P:(t + 1) * P], g.wo0[:, c, :],
                                                 start=False, stop=c == KD - 1)
                    k.then_inc(y_done, 1)
                if active(s, 2):
                    r.tensor_logits(nc, pe, s - 2)

            skewed(pe, 3, body)


def plan(nc, io, g, layer):
    with Memory(nc) as m:
        n = f"p{layer}_"
        count = m.sb(n + "count", [P, E])
        tiles_i = m.sb(n + "tiles_i", [P, E], i32)
        tiles = m.sb(n + "tiles", [P, E])
        ends = m.sb(n + "ends", [P, E])
        shift = m.sb(n + "shift", [P, E])
        one = m.sb(n + "one", [P, E])
        over = m.sb(n + "over", [P, NT, E])
        work = m.sb(n + "work", [P, NT, E])
        plan_f = m.sb(n + "plan_f", [P, 4, NT])
        count_i = m.sb(n + "count_i", [P, E], i32)
        pick = m.sb(n + "pick", [P, NTT * TOPK, E])
        packed = m.sb(n + "packed", [P, NTT * TOPK])
        expd = m.sb(n + "expd", [P, NTT])
        count_ps = m.bank(n + "count_ps")
        counted, counts_ready, done = m.sem(n + "counted"), m.sem(n + "counts_ready"), m.sem(n + "done")
        diff_ready, exp_done = m.sem(n + "diff_ready"), m.sem(n + "exp_done")
        block = m.stack.enter_context(nc.Block())

        @block.tensor
        def _(pe):
            nc.tensor.matmul(count_ps[:, 0:E], g.ones[:], g.seen[:], start=True, stop=True).then_inc(counted, 1)

        @block.gpsimd
        def _(pool):
            if layer:
                nc.gpsimd.memset(g.plan[:, 0, NT:NT + NTT], E)
                nc.gpsimd.iota(g.plan[:, 1, NT:NT + NTT], pattern=[[P, NTT]], base=E * REGION,
                               channel_multiplier=0)

        @block.scalar
        def _(act):
            act.wait_ge(diff_ready, 1)
            nc.scalar.activation(expd[:], expd[:], ACT.Exp).then_inc(exp_done, 1)

        @block.sync
        def _(sp):
            sp.wait_ge(counts_ready, 1)
            for e in range(E):
                c = sp.value_load(count_i[0:1, e:e + 1], min_val=0, max_val=TOK)
                sp.dma_start(g.routed[ds(c + e * REGION, P), :], g.zeros[:]).then_inc(done, 16)
            sp.wait_ge(done, 16 * E)

        @block.vector
        def _(dve):
            v = nc.vector
            v.memset(one[:], 1.0)
            v.tensor_tensor(expd[:], g.top_v[:, :, 1], g.top_v[:, :, 0], ALU.subtract).then_inc(diff_ready, 1)
            dve.wait_ge(counted, 1)
            v.tensor_copy(count[:], count_ps[:, 0:E])
            dve.drain()
            v.tensor_copy(count_i[:], count[:]).then_inc(counts_ready, 1)
            v.tensor_scalar(tiles_i[:], count[:], float(P - 1), None, ALU.add)
            dve.drain()
            v.tensor_scalar(tiles_i[:], tiles_i[:], 7, None, ALU.arith_shift_right)
            dve.drain()
            v.tensor_copy(tiles[:], tiles_i[:])
            dve.drain()
            v.tensor_tensor_scan(ends[:], one[:], tiles[:], 0.0, ALU.mult, ALU.add)
            dve.drain()
            v.tensor_tensor(over[:], bc(g.tile_no[:].rearrange("p (n a) -> p n a", a=1), 2, E),
                            bc(ends[:].rearrange("p (a e) -> p a e", a=1), 1, NT), ALU.is_ge)
            v.tensor_tensor(shift[:], ends[:], tiles[:], ALU.subtract)
            dve.drain()
            v.tensor_reduce(plan_f[:, 0, :], over[:], AX, ALU.add)
            v.tensor_tensor(work[:], over[:], bc(tiles[:].rearrange("p (a e) -> p a e", a=1), 1, NT), ALU.mult)
            v.scalar_tensor_tensor(shift[:], shift[:], float(P), g.region_of[:], ALU.mult, ALU.subtract)
            dve.drain()
            v.tensor_reduce(plan_f[:, 1, :], work[:], AX, ALU.add)
            v.tensor_scalar(plan_f[:, 2, :], plan_f[:, 0, :], float(E), None, ALU.is_lt)
            v.tensor_scalar(plan_f[:, 3, :], plan_f[:, 0, :], float(E - 1), None, ALU.min)
            dve.drain()
            v.tensor_tensor(plan_f[:, 1, :], g.tile_no[:], plan_f[:, 1, :], ALU.subtract)
            dve.drain()
            v.scalar_tensor_tensor(plan_f[:, 1, :], plan_f[:, 1, :], float(P), plan_f[:, 2, :], ALU.mult, ALU.mult)
            dve.drain()
            v.scalar_tensor_tensor(plan_f[:, 1, :], plan_f[:, 3, :], float(REGION), plan_f[:, 1, :],
                                   ALU.mult, ALU.add)
            v.tensor_copy(g.plan[:, 0, 0:NT], plan_f[:, 3, :])
            dve.drain()
            v.tensor_copy(g.plan[:, 1, 0:NT], plan_f[:, 1, :])
            v.tensor_tensor(pick[:], bc(g.top_f[:].rearrange("p t (k a) -> p (t k) a", a=1), 2, E),
                            bc(g.expert_of[:].rearrange("p (a e) -> p a e", a=1), 1, NTT * TOPK), ALU.is_equal)
            dve.drain()
            v.tensor_tensor(pick[:], pick[:], bc(shift[:].rearrange("p (a e) -> p a e", a=1), 1, NTT * TOPK),
                            ALU.mult)
            dve.drain()
            v.tensor_reduce(packed[:], pick[:], AX, ALU.add)
            dve.drain()
            v.tensor_tensor(g.packed_i[:], packed[:], g.pos[:].rearrange("p t k -> p (t k)"), ALU.add)
            dve.drain()
            dve.wait_ge(exp_done, 1)
            v.tensor_scalar(packed[:, 0:NTT], expd[:], 1.0, None, ALU.add)
            dve.drain()
            v.reciprocal(packed[:, 0:NTT], packed[:, 0:NTT])
            dve.drain()
            v.tensor_scalar(g.share[:, 0, :], packed[:, 0:NTT], g.gates[:, 2 + layer:3 + layer], None, ALU.mult)
            dve.drain()
            v.tensor_tensor(g.share[:, 1, :], g.share[:, 0, :], expd[:], ALU.mult)


def experts(nc, io, g, layer):
    tiles = NT + (NTT if layer else 0)
    ups = 1 if layer else 2
    slots = E + layer
    width = (ups * KD * F) + KF * D
    w = g.ffn_flat[:, 0:slots * width].rearrange("p (e n) -> p e n", n=width)
    up_bias = g.v_flat[:, 0:slots * ups * F].rearrange("p (e n) -> p e n", n=ups * F)
    with Memory(nc) as m:
        n = f"e{layer}_"
        xg = [m.sb(n + f"xg{p}", [P, D]) for p in range(2)]
        xt = [m.sb(n + f"xt{p}", [P, KD, P]) for p in range(2)]
        pre = m.sb(n + "pre", [P, F])
        lin = m.sb(n + "lin", [P, F])
        act_out = m.sb(n + "act_out", [P, F])
        h = m.sb(n + "h", [P, F])
        ht = [m.sb(n + f"ht{p}", [P, KF, P]) for p in range(2)]
        out = [m.sb(n + f"out{p}", [P, D]) for p in range(2)]
        down_bias = m.sb(n + "down_bias", [P, slots, D])
        up_ps = [[m.bank(n + f"up_ps{u}{p}") for p in range(2)] for u in range(ups)]
        xt_ps = m.bank(n + "xt_ps")
        ht_ps, out_ps = m.bank(n + "ht_ps"), m.bank(n + "out_ps")
        bias_in = m.sem(n + "bias_in")
        xg_loaded = [m.sem(n + f"xg_loaded{p}") for p in range(2)]
        stored = [m.sem(n + f"stored{p}") for p in range(2)]
        xt_done, xt_copied, up_done, pre_ready, act_done, h_ready, ht_done, ht_copied, out_done, out_ready = (
            m.sem(n + s) for s in ("xt_done", "xt_copied", "up_done", "pre_ready", "act_done", "h_ready",
                                   "ht_done", "ht_copied", "out_done", "out_ready"))
        block = m.stack.enter_context(nc.Block())

        @block.sync
        def _(sp):
            def body(s, p):
                if active(s, 0, tiles):
                    row = sp.value_load(g.plan[0:1, 1, ds(s, 1)], min_val=0, max_val=(E + 1) * REGION - P)
                    if not isinstance(s, int) or s >= 2:
                        sp.wait_ge(xt_done, s - 1)
                    sp.dma_start(xg[p][:], g.routed[ds(row, P), :]).then_inc(xg_loaded[p], 16)

            skewed(sp, 3, body, tiles)

        @block.gpsimd
        def _(pool):
            def body(s, p):
                if active(s, 3, tiles):
                    pool.wait_ge(out_ready, s - 2)
                    pool.dma_start(g.expert_out[layer][ds((s - 3) * P, P), :], out[1 - p][:])\
                        .then_inc(stored[1 - p], 16)

            skewed(pool, 3, body, tiles)
            for p in range(2):
                pool.wait_ge(stored[p], 16 * (tiles // 2))

        @block.scalar
        def _(act):
            for e in range(slots):
                if e == E:
                    names = ("L1_ffn_sb1", "L1_ffn_sb2")
                else:
                    names = ("L1_ffn_eb1", "L1_ffn_eb2") if layer else ("L0_ffn_b1", "L0_ffn_b2", "L0_ffn_b3")
                for u, name in enumerate(names):
                    dst = down_bias[:, e, :] if u == ups else up_bias[:, e, u * F:(u + 1) * F]
                    act.dma_start(dst, over_partitions(io[name] if e == E else io[name][e], D if u == ups else F))\
                        .then_inc(bias_in, 16)
            act.preload_act_table(ACT.Gelu if layer else ACT.Silu)

            def body(s, p):
                if active(s, 2, tiles):
                    i = s - 2
                    act.wait_ge(ht_done, i + 1)
                    if not isinstance(i, int) or i >= 2:
                        act.wait_ge(out_done, i - 1)
                    nc.scalar.copy(flat(ht[p]), ht_ps[:]).then_inc(ht_copied, 1)
                if active(s, 0, tiles):
                    act.wait_ge(xt_done, s + 1)
                    nc.scalar.copy(flat(xt[p]), xt_ps[:, 0:D]).then_inc(xt_copied, 1)
                if active(s, 1, tiles):
                    i = s - 1
                    act.wait_ge(pre_ready, i + 1)
                    wait_past_zero(act, ht_done if layer else h_ready, i)
                    dst, func = (h, ACT.Gelu) if layer else (act_out, ACT.Silu)
                    nc.scalar.activation(dst[:], pre[:], func).then_inc(act_done, 1)

            skewed(act, 3, body, tiles)

        @block.vector
        def _(dve):
            dve.wait_ge(bias_in, 16 * slots * (ups + 1))

            def body(s, p):
                if active(s, 1, tiles):
                    i = s - 1
                    e = dve.value_load(g.plan[0:1, 0, ds(i, 1)], min_val=0, max_val=slots - 1)
                    dve.wait_ge(up_done, i * ups + 1)
                    wait_past_zero(dve, act_done, i)
                    nc.vector.tensor_tensor(pre[:], up_ps[0][1 - p][:], up_bias[:, ds(e, 1), 0:F], ALU.add)\
                        .then_inc(pre_ready, 1)
                    if not layer:
                        dve.drain()
                        dve.wait_ge(up_done, i * ups + 2)
                        nc.vector.tensor_tensor(lin[:], up_ps[1][1 - p][:], up_bias[:, ds(e, 1), F:2 * F], ALU.add)
                        dve.drain()
                        dve.wait_ge(act_done, i + 1)
                        wait_past_zero(dve, ht_done, i)
                        nc.vector.tensor_tensor(h[:], act_out[:], lin[:], ALU.mult).then_inc(h_ready, 1)
                if active(s, 3, tiles):
                    i = s - 3
                    e = dve.value_load(g.plan[0:1, 0, ds(i, 1)], min_val=0, max_val=slots - 1)
                    dve.wait_ge(out_done, i + 1)
                    if not isinstance(i, int) or i >= 2:
                        dve.wait_ge(stored[1 - p], filled(i - 2, 1 - p, 16))
                    nc.vector.tensor_tensor(out[1 - p][:], out_ps[:, 0:D], down_bias[:, ds(e, 1), :], ALU.add)\
                        .then_inc(out_ready, 1)

            skewed(dve, 3, body, tiles)

        @block.tensor
        def _(pe):
            pe.wait_ge(g.ffn_in if not layer else g.ffn1_in, 16 * (E * 3 if not layer else 2 * slots))

            def body(s, p):
                if active(s, 1, tiles):
                    i = s - 1
                    e = pe.value_load(g.plan[0:1, 0, ds(i, 1)], min_val=0, max_val=slots - 1)
                    pe.wait_ge(xt_copied, i + 1)
                    for u in range(ups):
                        for c in range(KD):
                            at = (u * KD + c) * F
                            k = nc.tensor.matmul(up_ps[u][1 - p][:], xt[1 - p][:, c, :], w[:, ds(e, 1), at:at + F],
                                                 start=c == 0, stop=c == KD - 1)
                        k.then_inc(up_done, 1)
                if active(s, 2, tiles):
                    i = s - 2
                    pe.wait_ge(act_done if layer else h_ready, i + 1)
                    wait_past_zero(pe, ht_copied, i)
                    for f in range(KF):
                        k = nc.tensor.transpose(ht_ps[:, f * P:(f + 1) * P], h[:, f * P:(f + 1) * P], g.ident[:])
                    k.then_inc(ht_done, 1)
                if active(s, 0, tiles):
                    pe.wait_ge(xg_loaded[p], filled(s, p, 16))
                    wait_past_zero(pe, xt_copied, s)
                    for c in range(KD):
                        k = nc.tensor.transpose(xt_ps[:, c * P:(c + 1) * P], xg[p][:, c * P:(c + 1) * P],
                                                g.ident[:])
                    k.then_inc(xt_done, 1)
                if active(s, 3, tiles):
                    i = s - 3
                    e = pe.value_load(g.plan[0:1, 0, ds(i, 1)], min_val=0, max_val=slots - 1)
                    pe.wait_ge(ht_copied, i + 1)
                    wait_past_zero(pe, out_ready, i)
                    for f in range(KF):
                        at = ups * KD * F + f * D
                        k = nc.tensor.matmul(out_ps[:, 0:D], ht[1 - p][:, f, :], w[:, ds(e, 1), at:at + D],
                                             start=f == 0, stop=f == KF - 1)
                    k.then_inc(out_done, 1)

            skewed(pe, 3, body, tiles)


def attention(nc, io, g, tail, room):
    QUAD = 4
    NQ = H // QUAD
    CV = 32
    bank_of = [h % 3 for h in range(H - 1)] + [1]
    RING = 2 * QUAD
    fr = mybir.dt.float32r
    with Memory(nc) as m:
        exps = [room.take(KD, S) for _ in range(RING)]
        eo = [room.take(KD * TOPK, D) for _ in range(2)]
        v = [room.take(KD, D) for _ in range(2)]
        out_t = room.take(NQ, S)
        ctx_in = [tail.take(KD, D) for _ in range(2)]
        xn, xnt, ctxt = tail.take(KD, D), tail.take(KD, S), tail.take(KD, S)
        on, ont = tail.take(KD, D), tail.take(KD, S)
        idx = [m.sb(f"d_idx{p}", [P, KD * TOPK], i32) for p in range(2)]
        stats = m.sb("d_stats", [P, KD, 6])
        moments = m.sb("d_moments", [P, KD, 2])
        rstd = m.sb("d_rstd", [P, KD])
        q_hi = [m.sb(f"d_q_hi{p}", [P, KD, S], fr) for p in range(2)]
        q_lo = [m.sb(f"d_q_lo{p}", [P, KD, S], fr) for p in range(2)]
        k_hi = [[m.sb(f"d_k_hi{p}{par}", [P, KD, S], fr) for par in range(2)] for p in range(2)]
        k_lo = [[m.sb(f"d_k_lo{p}{par}", [P, KD, S], fr) for par in range(2)] for p in range(2)]
        neg_max = m.sb("d_neg_max", [P, RING, KD])
        sums = m.sb("d_sums", [P, 2, KD, QUAD])
        vp = [m.sb(f"d_vp{q}", [P, KD, QUAD, CV]) for q in range(2)]
        rden = m.sb("d_rden", [P, KD, H])
        t_ps = [m.bank(f"d_t_ps{i}") for i in range(2)]
        s_ps = [m.bank(f"d_s_ps{i}") for i in range(3)]
        o_ps = [m.bank(f"d_o_ps{i}") for i in range(2)]
        small_ps = m.bank("d_small_ps")
        r = Routing(m, g, 1, t_ps[1], small_ps)
        (moments_ready, rstd_ready, xn_ready, rows_used, scores_done, max_ready, exp_done, vp_ready,
         weighed, out_copied) = (
            m.sem("d_" + n) for n in ("moments_ready", "rstd_ready", "xn_ready", "rows_used", "scores_done",
                                      "max_ready", "exp_done", "vp_ready", "weighed", "out_copied"))
        ctx_loaded = [m.sem(f"d_ctx_loaded{p}") for p in range(2)]
        gathered = [m.sem(f"d_gathered{p}") for p in range(2)]
        uses = [("values", 3, (0, 1)), ("norm_t", 3, (1,)), ("ctx_t", 1, (1,)), ("y", 3, (0,)),
                ("xn_t", 1, (0,)), ("route_t", 3, (1,)), ("q", 1, (0,)), ("k", 1, (1,)), ("v", 1, (0,))]
        made = {n: m.sem(f"d_{n}_made") for n, _, _ in uses if n != "route_t"}
        taken = {n: m.sem(f"d_{n}_taken") for n, _, _ in uses if n != "route_t"}
        made["route_t"], taken["route_t"] = r.xrt_done, r.xrt_copied
        hi_ready = m.sem("d_hi_ready")
        block = m.stack.enter_context(nc.Block())

        def wait_bank_free(pe, name, step):
            at = next(i for i, u in enumerate(uses) if u[0] == name)
            for bank in uses[at][2]:
                for back in range(len(uses) * B):
                    i = at - 1 - back
                    past, i = -(i // len(uses)), i % len(uses)
                    st = step - past if past else step
                    if isinstance(st, int) and st < 0:
                        break
                    if bank in uses[i][2] and active(st, uses[i][1]):
                        pe.wait_ge(taken[uses[i][0]], st - uses[i][1] + 1)
                        break

        @block.sync
        def _(sp):
            def body(s, p):
                if active(s, 0):
                    if not isinstance(s, int) or s >= 2:
                        sp.wait_ge(made["ctx_t"], s - 1)
                    sp.dma_start(ctx_in[p], io["ctx"][:, ds(s * KD, KD), :]).then_inc(ctx_loaded[p], 16)

            skewed(sp, 3, body)

        @block.gpsimd
        def _(pool):
            for q in range(2):
                nc.gpsimd.memset(vp[q][:], 0.0).then_inc(vp_ready, 1)
            pool.drain()

            def body(s, p):
                if active(s, 1):
                    pool.wait_ge(moments_ready, s)
                    nc.gpsimd.tensor_tensor(rstd[:], moments[:, :, 1], bc(g.eps[:], 1, KD), ALU.add)
                    pool.drain()
                    nc.gpsimd.tensor_tensor(rstd[:], rstd[:], bc(g.neg_half[:], 1, KD), ALU.pow)\
                        .then_inc(rstd_ready, 1)
                if active(s, 0):
                    pool.wait_ge(rows_used, s + 1)
                    nc.gpsimd.tensor_copy(idx[p][:], g.packed_i[:, ds(s * (KD * TOPK), KD * TOPK)])
                    pool.drain()
                    for at in range(KD * TOPK):
                        pool.indirect_dma_start(
                            eo[p][:, at, :], None, g.expert_out[0],
                            bass.IndirectOffsetOnAxis(ap=idx[p][:, at:at + 1], axis=0)).then_inc(gathered[p], 16)
                if active(s, 3):
                    r.gpsimd_rstd(nc, pool, s - 3)
                    r.gpsimd_scatter(nc, pool, s - 3, 1 - p)

            skewed(pool, 3, body)
            for p in range(2):
                pool.wait_ge(r.scattered[p], r.per_batch * (B // 2))

        @block.scalar
        def _(act):
            act.preload_act_table(ACT.Exp)

            def leave(name, n, dst, bank, scale=None):
                act.wait_ge(made[name], n + 1)
                dst = dst.rearrange("p a b -> p (a b)")
                if scale is None:
                    return nc.scalar.copy(dst, t_ps[bank][:])
                return nc.scalar.mul(dst, t_ps[bank][:], scale)

            def body(s, p):
                a, b, c = s - 1, s - 2, s - 3
                on1, on2, on3 = active(s, 1), active(s, 2), active(s, 3)
                for h in range(H):
                    if on2:
                        i, q = h % RING, h // QUAD % 2
                        act.wait_ge(max_ready, b * H + h + 1)
                        if not isinstance(b, int) or b > 0 or h >= RING:
                            act.wait_ge(weighed, b * NQ + h // QUAD - 1)
                        for t in range(KD):
                            k = nc.scalar.activation(exps[i][:, t, :], s_ps[bank_of[h]][:, t * S:(t + 1) * S],
                                                     ACT.Exp, bias=neg_max[:, i, t:t + 1],
                                                     accum_out=sums[:, q, t, h % QUAD:h % QUAD + 1])
                        k.then_inc(exp_done, 1)
                    if h == 2 and on3:
                        act.wait_ge(weighed, c * NQ + NQ)
                        for half in range(2):
                            k = nc.scalar.copy(out_t[:, half * 2:half * 2 + 2, :].rearrange("p a b -> p (a b)"),
                                               o_ps[half][:])
                        k.then_inc(out_copied, 1)
                    if h == 6 and on3:
                        leave("norm_t", c, ont, 1).then_inc(taken["norm_t"], 1)
                    if h == 7 and on1:
                        leave("ctx_t", a, ctxt, 1).then_inc(taken["ctx_t"], 1)
                    if h == 9 and on1:
                        leave("xn_t", a, xnt, 0).then_inc(taken["xn_t"], 1)
                    if h == 11 and on3:
                        r.scalar(nc, act, c)
                    if h == 12 and on1:
                        leave("q", a, q_hi[1 - p][:], 0, float(D) ** -0.5).then_inc(hi_ready, 1)
                    if h == 13 and on1:
                        leave("k", a, k_hi[1 - p][0][:], 1, g.parity[:, 0:1])
                        leave("k", a, k_hi[1 - p][1][:], 1, g.parity[:, 1:2]).then_inc(hi_ready, 1)
                    if h == 15 and on1:
                        leave("v", a, v[1 - p], 0).then_inc(taken["v"], 1)

            skewed(act, 3, body)

        @block.vector
        def _(dve):
            dve.sem_inc(rows_used, 2)
            nc.vector.memset(g.seen[:], 0.0).then_inc(r.seen_ready, 1)

            def scale_values(n, par, quad):
                q = quad % 2
                dve.wait_ge(exp_done, n * H + (quad + 1) * QUAD)
                if quad == 0:
                    dve.wait_ge(taken["v"], n + 1)
                nc.vector.reciprocal(sums[:, q, :, :], sums[:, q, :, :])
                dve.drain()
                by = sums[:, q, :, :].rearrange("p t (h a) -> p t h a", a=1)
                nc.vector.tensor_tensor(
                    vp[q][:, :, :, 0:C],
                    v[par][:, :, quad * QUAD * C:(quad + 1) * QUAD * C].rearrange("p t (h c) -> p t h c", c=C),
                    bc(by, 3, C), ALU.mult)
                nc.vector.tensor_copy(vp[q][:, :, :, C:C + 1], by).then_inc(vp_ready, 1)

            def combine(n, par):
                dve.wait_ge(gathered[par], filled(n, par, 16 * KD * TOPK))
                for k in range(TOPK):
                    for t in range(KD):
                        xb = g.x[:, ds(n * KD + t, 1), :]
                        last = nc.vector.scalar_tensor_tensor(
                            xb, eo[par][:, t * TOPK + k, :], g.share[:, k, ds(n * KD + t, 1)], xb,
                            ALU.mult, ALU.add)
                    if k == TOPK - 1:
                        last.then_inc(rows_used, 1)
                    dve.drain()
                for t in range(KD):
                    nc.vector.bn_stats(stats[:, t, :], g.x[:, ds(n * KD + t, 1), :])
                dve.drain()
                for t in range(KD):
                    k = nc.vector.bn_aggr(moments[:, t, :], stats[:, t, :])
                k.then_inc(moments_ready, 1)

            def body(s, p):
                a, b, c = s - 1, s - 2, s - 3
                on1, on2, on3 = active(s, 1), active(s, 2), active(s, 3)
                for h in range(H):
                    if on2:
                        dve.wait_ge(scores_done, b * H + h + 1)
                        nc.vector.tensor_reduce(neg_max[:, h % RING, :],
                                                s_ps[bank_of[h]][:].rearrange("p (t n) -> p t n", n=S),
                                                AX, ALU.max, negate=True).then_inc(max_ready, 1)
                    if h == 0 and on3:
                        scale_values(c, 1 - p, NQ - 1)
                    if h == 1 and on1:
                        combine(a, 1 - p)
                    if h == 4 and on3:
                        dve.wait_ge(made["values"], c + 1)
                        for t in range(KD):
                            o = t_ps[t][:].rearrange("p (h c) -> p h c", c=CV)
                            nc.vector.reciprocal(rden[:, t, :], o[:, :, C])
                        dve.drain()
                        for t in range(KD):
                            o = t_ps[t][:].rearrange("p (h c) -> p h c", c=CV)
                            k = nc.vector.tensor_tensor(on[:, t, :].rearrange("p (h c) -> p h c", c=C), o[:, :, 0:C],
                                                        bc(rden[:, t, :].rearrange("p (h a) -> p h a", a=1), 2, C),
                                                        ALU.mult)
                        k.then_inc(taken["values"], 1)
                    if h in (5, 9, 13) and on2:
                        scale_values(b, p, h // QUAD - 1)
                    if h == 6 and on1:
                        dve.wait_ge(rstd_ready, a + 1)
                        for t in range(KD):
                            k = nc.vector.tensor_scalar(xn[:, t, :], g.x[:, ds(a * KD + t, 1), :],
                                                        moments[:, t, 0:1], rstd[:, t:t + 1],
                                                        ALU.subtract, ALU.mult)
                        k.then_inc(xn_ready, 1)
                    if h == 8 and on3:
                        dve.wait_ge(made["y"], c + 1)
                        xb = g.x[:, ds(c * KD, KD), :]
                        nc.vector.scalar_tensor_tensor(xb, t_ps[0][:].rearrange("p (t d) -> p t d", d=D),
                                                       g.gates[:, 1:2], xb, ALU.mult, ALU.add)\
                            .then_inc(taken["y"], 1)
                        dve.drain()
                        r.vector_norm(nc, dve, c)
                    if h == 9 and on3:
                        r.vector_rows(nc, dve, c, 1 - p)
                    if h == 12 and on1:
                        dve.wait_ge(hi_ready, a * 2 + 1)
                        nc.vector.scalar_tensor_tensor(flat(q_lo[1 - p]), t_ps[0][:], float(D) ** -0.5,
                                                       flat(q_hi[1 - p]).bitcast(f32), ALU.mult, ALU.subtract)\
                            .then_inc(taken["q"], 1)
                    if h == 13 and on1:
                        dve.wait_ge(hi_ready, a * 2 + 2)
                        for par in range(2):
                            k = nc.vector.scalar_tensor_tensor(
                                flat(k_lo[1 - p][par]), t_ps[1][:], g.parity[:, par:par + 1],
                                flat(k_hi[1 - p][par]).bitcast(f32), ALU.mult, ALU.subtract)
                        k.then_inc(taken["k"], 1)
                    if h == 14 and on3:
                        r.vector_pick(nc, dve, c)
                    if h == 15 and on3:
                        r.vector_place(nc, dve, c, 1 - p)

            skewed(dve, 3, body)

        @block.tensor
        def _(pe):
            pe.wait_ge(g.attn1_in, 16 * 6)

            def product(name, s, out, lhs, rhs):
                wait_bank_free(pe, name, s)
                for i in range(KD):
                    for c in range(KD):
                        k = nc.tensor.matmul(out[:, i * 256:(i + 1) * 256], lhs[:, c, i * P:(i + 1) * P],
                                             rhs[:, c, :], start=c == 0, stop=c == KD - 1)
                k.then_inc(made[name], 1)

            def turn_over(name, s, out, src):
                wait_bank_free(pe, name, s)
                for t in range(KD):
                    for c in range(KD):
                        k = nc.tensor.transpose(out[:, c * S + t * P:c * S + (t + 1) * P],
                                                src[:, t, c * P:(c + 1) * P], g.ident[:])
                k.then_inc(made[name], 1)

            def scores(n, par, h):
                r0 = h % 8 // 2 * 32
                if h == 0:
                    pe.wait_ge(taken["q"], n + 1)
                    pe.wait_ge(taken["k"], n + 1)
                before = [b for b in range(-H, h) if bank_of[b % H] == bank_of[h]][-1]
                if not isinstance(n, int) or n > 0 or before >= 0:
                    pe.wait_ge(exp_done, n * H + before + 1)
                for t in range(KD):
                    out = s_ps[bank_of[h]][:, t * S:(t + 1) * S]
                    parts = ((k_hi, q_hi), (k_hi, q_lo), (k_lo, q_hi))
                    for i, (kk, qq) in enumerate(parts):
                        k = nc.tensor.matmul(out, kk[par][h % 2][r0:r0 + 32, h // 8, t * P:(t + 1) * P],
                                             qq[par][r0:r0 + 32, h // 8, :], start=i == 0, stop=i == 2)
                k.then_inc(scores_done, 1)

            def weigh(n, q):
                pe.wait_ge(vp_ready, n * NQ + q + 3)
                if q == 0 and (not isinstance(n, int) or n > 0):
                    pe.wait_ge(out_copied, n)
                for t in range(KD):
                    for i in range(QUAD):
                        k = nc.tensor.matmul(
                            o_ps[q // 2][i * CV:(i + 1) * CV, q % 2 * S:(q % 2 + 1) * S],
                            vp[q % 2][:, t, i, :], exps[(q % 2) * QUAD + i][:, t, :],
                            start=t == 0, stop=t == KD - 1)
                k.then_inc(weighed, 1)

            def body(s, p):
                a, b, c = s - 1, s - 2, s - 3
                on1, on2, on3 = active(s, 1), active(s, 2), active(s, 3)
                for h in range(H):
                    if on2:
                        scores(b, p, h)
                    if h == 1 and on3:
                        weigh(c, NQ - 1)
                    if h == 3 and on3:
                        wait_bank_free(pe, "values", s)
                        pe.wait_ge(out_copied, c + 1)
                        for t in range(KD):
                            for q in range(NQ):
                                k = nc.tensor.transpose(t_ps[t][:, q * P:(q + 1) * P],
                                                        out_t[:, q, t * P:(t + 1) * P], g.ident[:])
                        k.then_inc(made["values"], 1)
                    if h == 5 and on3:
                        pe.wait_ge(taken["values"], c + 1)
                        turn_over("norm_t", s, t_ps[1], on)
                    if h in (6, 10, 14) and on2:
                        weigh(b, h // QUAD - 1)
                    if h == 6 and on1:
                        pe.wait_ge(ctx_loaded[1 - p], filled(a, 1 - p, 16))
                        turn_over("ctx_t", s, t_ps[1], ctx_in[1 - p])
                    if h == 7 and on3:
                        pe.wait_ge(taken["norm_t"], c + 1)
                        product("y", s, t_ps[0], ont, g.wo1)
                    if h == 8 and on1:
                        pe.wait_ge(xn_ready, a + 1)
                        turn_over("xn_t", s, t_ps[0], xn)
                    if h == 10 and on3:
                        wait_bank_free(pe, "route_t", s)
                        r.tensor_turn(nc, pe, c, 1 - p)
                    if h == 11 and on1:
                        pe.wait_ge(taken["xn_t"], a + 1)
                        product("q", s, t_ps[0], g.wq1, xnt)
                    if h == 12 and on1:
                        pe.wait_ge(taken["ctx_t"], a + 1)
                        product("k", s, t_ps[1], g.wk1, ctxt)
                    if h == 13 and on3:
                        r.tensor_logits(nc, pe, c)
                    if h == 14 and on1:
                        product("v", s, t_ps[0], ctxt, g.wv1)
                    if h == 15 and on3:
                        r.tensor_rank(nc, pe, c)

            skewed(pe, 3, body)


def finish(nc, io, g):
    with Memory(nc) as m:
        idx = [m.sb(f"f_idx{p}", [P, KD * TOPK], i32) for p in range(2)]
        eo = [m.sb(f"f_eo{p}", [P, KD * TOPK, D]) for p in range(2)]
        shared = [m.sb(f"f_shared{p}", [P, KD, D]) for p in range(2)]
        rows_used = m.sem("f_rows_used")
        gathered = [m.sem(f"f_gathered{p}") for p in range(2)]
        shared_in = [m.sem(f"f_shared_in{p}") for p in range(2)]
        ready, stored = m.sem("f_ready"), m.sem("f_stored")
        block = m.stack.enter_context(nc.Block())

        @block.gpsimd
        def _(pool):
            with pool.Fori(0, B // 2) as j:
                for p in range(2):
                    b = j * 2 + p
                    pool.wait_ge(rows_used, b + 1)
                    nc.gpsimd.tensor_copy(idx[p][:], g.packed_i[:, ds(b * KD * TOPK, KD * TOPK)])
                    pool.drain()
                    for at in range(KD * TOPK):
                        pool.indirect_dma_start(
                            eo[p][:, at, :], None, g.expert_out[1],
                            bass.IndirectOffsetOnAxis(ap=idx[p][:, at:at + 1], axis=0)).then_inc(gathered[p], 16)

        @block.sync
        def _(sp):
            with sp.Fori(0, B // 2) as j:
                for p in range(2):
                    b = j * 2 + p
                    sp.wait_ge(rows_used, b + 1)
                    sp.dma_start(shared[p][:], g.expert_out[1][ds(b * S + NT * P, S), :]
                                 .rearrange("(t p) d -> p t d", p=P)).then_inc(shared_in[p], 16)

        @block.scalar
        def _(act):
            with act.Fori(0, B) as b:
                act.wait_ge(ready, b + 1)
                act.dma_start(io["out"][:, ds(b * KD, KD), :], g.x[:, ds(b * KD, KD), :]).then_inc(stored, 16)
            act.wait_ge(stored, 16 * B)

        @block.vector
        def _(dve):
            dve.sem_inc(rows_used, 2)
            with dve.Fori(0, B // 2) as j:
                for p in range(2):
                    b = j * 2 + p
                    dve.wait_ge(shared_in[p], (j + 1) * 16)
                    xb = g.x[:, ds(b * KD, KD), :]
                    nc.vector.scalar_tensor_tensor(xb, shared[p][:], g.gates[:, 3:4], xb, ALU.mult, ALU.add)
                    dve.drain()
                    dve.wait_ge(gathered[p], (j + 1) * (16 * KD * TOPK))
                    for k in range(TOPK):
                        for t in range(KD):
                            xb = g.x[:, ds(b * KD + t, 1), :]
                            last = nc.vector.scalar_tensor_tensor(
                                xb, eo[p][:, t * TOPK + k, :], g.share[:, k, ds(b * KD + t, 1)], xb,
                                ALU.mult, ALU.add)
                        dve.drain()
                    dve.sem_inc(rows_used, 1)
                    dve.sem_inc(ready, 1)


def build(nc, io, upto=99):
    with Memory(nc) as g:
        g.routed = nc.dram_tensor("routed_rows", [(E + 1) * REGION, D], f32, kind="Internal").ap()
        g.expert_out = [nc.dram_tensor(f"expert_rows{n}", [(NT + n * NTT) * P, D], f32, kind="Internal").ap()
                        for n in range(2)]
        g.x = g.sb("x", [P, NTT, D])
        g.ffn = g.sb("ffn", [P, E, 2 * KD * F + KF * D])
        g.ffn_flat = g.ffn[:].rearrange("p e n -> p (e n)")
        g.v_spec = g.sb("v_spec", [P, B, 2, D])
        g.v_flat = g.v_spec[:].rearrange("p b a d -> p (b a d)")
        g.ident = g.sb("ident", [P, P])
        g.ones = g.sb("ones", [P, P], bf16)
        g.before = g.sb("before", [P, P], bf16)
        g.zeros = g.sb("zeros", [P, D])
        g.neg_half, g.eps = g.sb("neg_half", [P, 1]), g.sb("eps", [P, 1])
        g.zero_i = g.sb("zero_i", [P, KD * TOPK], i32)
        g.not_dc, g.only_dc = g.sb("not_dc", [P, 1]), g.sb("only_dc", [P, 1])
        g.parity = g.sb("parity", [P, 2])
        g.parity_rows = g.sb("parity_rows", [P, 2, 4])
        g.expert_of, g.region_of = g.sb("expert_of", [P, E]), g.sb("region_of", [P, E])
        g.tile_no = g.sb("tile_no", [P, NT])
        g.gates = g.sb("gates", [P, 4])
        g.bo = g.sb("bo", [P, D])
        g.router0, g.router1 = g.sb("router0", [P, KD, E]), g.sb("router1", [P, KD, E])
        g.router_b = g.sb("router_b", [P, 1, E])
        g.seen = g.sb("seen", [P, E], bf16)
        g.top_v, g.top_f = g.sb("top_v", [P, NTT, TOPK]), g.sb("top_f", [P, NTT, TOPK])
        g.pos = g.sb("pos", [P, NTT, TOPK])
        g.packed_i = g.sb("packed_i", [P, NTT * TOPK], i32)
        g.share = g.sb("share", [P, TOPK, NTT])
        g.plan = g.sb("plan", [P, 2, NT + NTT], i32)
        g.consts_made, g.later_in, g.ffn_in = g.sem("consts_made"), g.sem("later_in"), g.sem("ffn_in")
        g.gates_ready, g.attn1_in, g.ffn1_in = g.sem("gates_ready"), g.sem("attn1_in"), g.sem("ffn1_in")

        with Memory(nc) as m0:
            g.dft, g.icorr = m0.sb("dft", [P, KD, S]), m0.sb("icorr", [P, 2, S])
            g.iout, g.wo0 = m0.sb("iout", [P, 2, S]), m0.sb("wo0", [P, KD, D])
            g.cross = m0.sb("cross", [P, 2, B * H])
            g.w_same, g.w_other = m0.sb("w_same", [P, 2, B * H]), m0.sb("w_other", [P, 2, B * H])
            spectra(nc, io, g)
            if upto > 1: lags(nc, io, g)
            if upto > 2: mix(nc, io, g)
        if upto > 3: plan(nc, io, g, 0)
        if upto > 4: experts(nc, io, g, 0)
        tail = Carved(g.ffn_flat, (E + 1) * (KD * F + KF * D))
        g.wq1, g.wk1, g.wv1, g.wo1 = (tail.take(KD, D) for _ in range(4))
        if upto > 5: load_layer1(nc, io, g)
        if upto > 5: attention(nc, io, g, tail, Carved(g.v_flat, 0))
        if upto > 6: plan(nc, io, g, 1)
        if upto > 7: experts(nc, io, g, 1)
        if upto > 8: finish(nc, io, g)


def load_layer1(nc, io, g):
    width = KD * F + KF * D
    w = g.ffn_flat[:, 0:(E + 1) * width].rearrange("p (e n) -> p e n", n=width)
    with nc.Block() as block:
        @block.sync
        def _(sp):
            for dst, name in ((g.wq1, "L1_xattn_Wq"), (g.wk1, "L1_xattn_Wk"), (g.wv1, "L1_xattn_Wv"),
                              (g.wo1, "L1_xattn_Wo")):
                sp.dma_start(dst[:], rows(io[name])).then_inc(g.attn1_in, 16)
            sp.dma_start(g.router1[:], rows(io["L1_ffn_router_w"])).then_inc(g.attn1_in, 16)
            sp.dma_start(g.router_b[:, 0, :], over_partitions(io["L1_ffn_router_b"], E)).then_inc(g.attn1_in, 16)
            for e in range(E + 1):
                up = io["L1_ffn_ew1"][e] if e < E else io["L1_ffn_sw1"]
                down = io["L1_ffn_ew2"][e] if e < E else io["L1_ffn_sw2"]
                sp.dma_start(w[:, e, 0:KD * F].rearrange("p (k n) -> p k n", k=KD), rows(up)).then_inc(g.ffn1_in, 16)
                sp.dma_start(w[:, e, KD * F:].rearrange("p (k n) -> p k n", k=KF), rows(down)).then_inc(g.ffn1_in, 16)


TRANSPOSED = ("L0_xattn_Wq", "L0_xattn_Wk", "L0_xattn_Wv", "L0_xattn_Wo", "L0_ffn_Wg", "L0_ffn_W1", "L0_ffn_W2",
              "L0_ffn_W3", "L1_xattn_Wq", "L1_xattn_Wk", "L1_xattn_Wv", "L1_xattn_Wo")


def transforms():
    t = np.arange(S)
    w = 2 * np.pi * np.outer(t, np.arange(S // 2)) / S
    cos, sin = np.cos(w), np.sin(w)
    sin[:, 0] = np.cos(np.pi * t)
    two = np.full(S // 2, 2.0 / S)
    two[0] = 1.0 / S
    sign = np.full(S // 2, -1.0)
    sign[0] = 1.0
    forward = np.concatenate([cos, sin], 1)
    from_cross = np.concatenate([cos * two, sin * two * sign], 1).T / C
    from_spectrum = np.concatenate([cos * two, sin * two], 1).T
    return {n: np.ascontiguousarray(a, np.float32)
            for n, a in (("dft", forward), ("icorr", from_cross), ("iout", from_spectrum))}


def kernel(**inputs):
    import concourse.bacc as bacc
    from concourse.bass_utils import run_bass_kernel_spmd

    nc = bacc.Bacc("TRN2", target_bir_lowering=False, num_devices=1)
    arrays = {}
    for name, a in inputs.items():
        a = np.asarray(a)
        arrays[name] = np.ascontiguousarray(np.swapaxes(a, -1, -2) if name in TRANSPOSED else a)
    arrays.update(transforms())
    io = {n: nc.dram_tensor(n, a.shape, mybir.dt.from_np(a.dtype), kind="ExternalInput").ap()
          for n, a in arrays.items()}
    out = nc.dram_tensor("out", (B, S, D), f32, kind="ExternalOutput").ap()
    by_tile = "b (t p) d -> p (b t) d"
    io["x"] = io["x"].rearrange(by_tile, p=P)
    io["ctx"] = io["ctx_1024"].rearrange(by_tile, p=P)
    io["out"] = out.rearrange(by_tile, p=P)
    build(nc, io)
    r = run_bass_kernel_spmd(nc, [arrays], core_ids=[0])
    return r.results[0]["out"]
```

```python
from contextlib import ExitStack

import numpy as np
import concourse.bass as bass
from concourse import mybir

P = 128
B, S, D = 16, 256, 256
H, C = 16, 16
KD = D // P
TOK = B * S
NTT = TOK // P
E, F = 8, 512
KF = F // P
TOPK, LAGS = 2, 5
NT = 2 * TOK // P + E
REGION = TOK + P
EPS = 1e-5
GROUP = P // H
HALF = TOK // P // 2
LOWEST, TAKEN = -3.0e38, -3.2e38

f32 = mybir.dt.float32
bf16 = mybir.dt.bfloat16
i32 = mybir.dt.int32
u32 = mybir.dt.uint32
ALU = mybir.AluOpType
ACT = mybir.ActivationFunctionType
AX = mybir.AxisListType.X
ds = bass.ds


class Memory:

    def __init__(self, nc):
        self.nc, self.stack = nc, ExitStack()

    def __enter__(self):
        return self

    def __exit__(self, *_):
        self.stack.close()

    def sb(self, name, shape, dt=f32):
        return self.stack.enter_context(self.nc.sbuf_tensor("sb_" + name, shape, dt))

    def bank(self, name, shape=(P, 512), dt=f32):
        return self.stack.enter_context(self.nc.psum_tensor(name, list(shape), dt))

    def sem(self, name):
        return self.stack.enter_context(self.nc.semaphore(name))


class Carved:

    def __init__(self, flat_ap, start):
        self.ap, self.at = flat_ap, start

    def take(self, a, b):
        self.at += a * b
        assert self.at <= self.ap.shape[1]
        return self.ap[:, self.at - a * b:self.at].rearrange("p (a b) -> p a b", a=a)


def rows(ap):
    return ap.rearrange("(k p) n -> p k n", p=P)


def over_partitions(ap, n):
    return ap.rearrange("(a n) -> a n", a=1).broadcast_to([P, n])


def flat(t):
    return t[:].rearrange("p a b -> p (a b)")


def wait_past_zero(engine, sem, value):
    if not isinstance(value, int) or value > 0:
        engine.wait_ge(sem, value)


def active(step, stage, count=B):
    return not isinstance(step, int) or 0 <= step - stage < count


def skewed(engine, depth, body, count=B, peel=0):
    first = max(depth + depth % 2, peel)
    for step in range(first):
        body(step, step % 2)
    with engine.Fori(first // 2, count // 2) as j:
        for p in range(2):
            body(j * 2 + p, p)
    for step in range(count, count + depth):
        body(step, step % 2)


def filled(n, parity, inc):
    return n * (inc // 2) + inc - parity * (inc // 2)


def bc(ap, axis, n):
    shape = list(ap.shape)
    shape[axis] = n
    return ap.broadcast_to(shape)


def load_expert0(sp, io, g, e):
    for n, name in enumerate(("L0_ffn_W1", "L0_ffn_W2")):
        sp.dma_start(g.ffn[:, e, n * KD * F:(n + 1) * KD * F].rearrange("p (k n) -> p k n", k=KD),
                     rows(io[name][e])).then_inc(g.ffn_in, 16)
    sp.dma_start(g.ffn[:, e, 2 * KD * F:].rearrange("p (k n) -> p k n", k=KF),
                 rows(io["L0_ffn_W3"][e])).then_inc(g.ffn_in, 16)


def load_expert1(sp, io, g, twice_e, half):
    shared = isinstance(twice_e, int) and twice_e == 2 * E
    at = twice_e * ((KD * F + KF * D) // 2) + half * (KD * F)
    k, n = ((KD, F), (KF, D))[half]
    if shared:
        src = rows(io["L1_ffn_sw2" if half else "L1_ffn_sw1"])
    else:
        src = io["L1_ffn_ew2" if half else "L1_ffn_ew1"].rearrange("e (k p) n -> p (e k) n", p=P)
        src = src[:, ds(twice_e * (k // 2), k), :]
    sp.dma_start(g.ffn_flat[:, ds(at, k * n)].rearrange("p (k n) -> p k n", k=k), src).then_inc(g.ffn1_in, 16)


def spectra(nc, io, g):
    with Memory(nc) as m:
        ctx_in = [m.sb(f"ctx_in{p}", [P, KD, D]) for p in range(2)]
        xn = [m.sb(f"xn{p}", [P, KD, D]) for p in range(2)]
        stats = m.sb("ln0_stats", [P, KD, 6])
        moments = m.sb("ln0_moments", [P, 2, KD, 2])
        rstd = m.sb("ln0_rstd", [P, 2, KD])
        spare = g.ffn[:, E - 1, :]
        wq = spare[:, 0:KD * D].rearrange("p (k n) -> p k n", k=KD)
        wkv = spare[:, KD * D:3 * KD * D].rearrange("p (k n) -> p k n", k=KD)
        bias0 = spare[:, 3 * KD * D:3 * KD * D + 3 * D]
        xf = [m.sb(f"xf{p}", [P, KD, S]) for p in range(2)]
        cf = [m.sb(f"cf{p}", [P, KD, S]) for p in range(2)]
        qs = m.sb("q_spec", [P, 2, D])
        ks = m.sb("k_spec", [P, 2, D])
        prod = m.sb("prod", [P, 4, D])
        summed = m.sb("prod_sum", [P, 4, H])
        edge = m.sb("edge", [P, 2, H])
        xf_ps, cf_ps = m.bank("xf_ps"), m.bank("cf_ps")
        q_ps = [m.bank(f"q_ps{t}") for t in range(2)]
        kv_ps = [m.bank(f"kv_ps{t}") for t in range(2)]

        consts_in = m.sem("a_consts_in")
        zeroed = m.sem("a_zeroed")
        in_loaded = [m.sem(f"a_in_loaded{p}") for p in range(2)]
        moments_ready, rstd_ready = m.sem("a_moments_ready"), m.sem("a_rstd_ready")
        xn_ready = m.sem("a_xn_ready")
        xf_done, cf_done = m.sem("a_xf_done"), m.sem("a_cf_done")
        xf_copied, cf_copied = m.sem("a_xf_copied"), m.sem("a_cf_copied")
        q_done, kv_done = m.sem("a_q_done"), m.sem("a_kv_done")
        act_copied, dve_copied = m.sem("a_sin_copied"), m.sem("a_cos_copied")
        spec_used = m.sem("a_spec_used")
        bias_ready = m.sem("a_bias_ready")
        block = m.stack.enter_context(nc.Block())

        @block.sync
        def _(sp):
            sp.dma_start(g.dft[:], rows(io["dft"])).then_inc(consts_in, 16)
            sp.dma_start(wq[:], rows(io["L0_xattn_Wq"])).then_inc(consts_in, 16)
            sp.dma_start(wkv[:, :, 0:D], rows(io["L0_xattn_Wk"])).then_inc(consts_in, 16)
            sp.dma_start(wkv[:, :, D:2 * D], rows(io["L0_xattn_Wv"])).then_inc(consts_in, 16)
            sp.wait_ge(zeroed, 1)
            for n, name in enumerate(("L0_xattn_bq", "L0_xattn_bk", "L0_xattn_bv")):
                sp.dma_start(bias0[0:1, n * D:(n + 1) * D],
                             io[name].rearrange("(a n) -> a n", a=1)).then_inc(consts_in, 16)
            with sp.Fori(0, B // 2) as j:
                for p in range(2):
                    b = j * 2 + p
                    sp.wait_ge(cf_done, b + 1)
                    sp.dma_start(ctx_in[p][:], io["ctx"][:, ds(b * KD, KD), :]).then_inc(in_loaded[p], 16)
                    sp.dma_start(g.x[:, ds(b * KD, KD), :], io["x"][:, ds(b * KD, KD), :])\
                        .then_inc(in_loaded[p], 16)
            sp.dma_start(g.icorr[:], rows(io["icorr"])).then_inc(g.later_in, 16)
            sp.dma_start(g.iout[:], rows(io["iout"])).then_inc(g.later_in, 16)
            sp.dma_start(g.wo0[:], rows(io["L0_xattn_Wo"])).then_inc(g.later_in, 16)
            sp.dma_start(g.router0[:], rows(io["L0_ffn_Wg"])).then_inc(g.later_in, 16)
            sp.dma_start(g.bo[:], over_partitions(io["L0_xattn_bo"], D)).then_inc(g.later_in, 16)
            sp.dma_start(g.gates[:, 0:2], over_partitions(io["g_xattn"], 2)).then_inc(g.later_in, 16)
            sp.dma_start(g.gates[:, 2:4], over_partitions(io["g_ffn"], 2)).then_inc(g.later_in, 16)
            for e in range(E - 1):
                load_expert0(sp, io, g, e)

        @block.gpsimd
        def _(pool):
            nc.gpsimd.memset(bias0, 0.0).then_inc(zeroed, 1)
            nc.gpsimd.memset(g.neg_half[:], -0.5)
            nc.gpsimd.memset(g.eps[:], EPS)
            nc.gpsimd.memset(g.zero_i[:], 0)
            nc.gpsimd.memset(g.ones[:], 1.0)
            nc.gpsimd.memset(g.before[:], 1.0)
            nc.gpsimd.memset(g.ident[:], 0.0)
            nc.gpsimd.memset(g.not_dc[:], 1.0)
            nc.gpsimd.memset(g.only_dc[:], 0.0)
            nc.gpsimd.memset(g.low_rows[:], 0.0)
            nc.gpsimd.memset(g.zeros[:], 0.0)
            nc.gpsimd.iota(g.expert_of[:], pattern=[[1, E]], base=0, channel_multiplier=0, allow_small_or_imprecise_dtypes=True)
            nc.gpsimd.iota(g.region_of[:], pattern=[[REGION, E]], base=0, channel_multiplier=0, allow_small_or_imprecise_dtypes=True)
            nc.gpsimd.iota(g.tile_no[:], pattern=[[1, NT]], base=0, channel_multiplier=0, allow_small_or_imprecise_dtypes=True)
            pool.drain()
            nc.gpsimd.memset(g.not_dc[0:1, :], 0.0)
            nc.gpsimd.memset(g.only_dc[0:1, :], 1.0)
            nc.gpsimd.affine_select(out=g.before[:], in_=g.before[:], compare_op=ALU.is_gt, fill=0.0,
                                    base=0, pattern=[[1, P]], channel_multiplier=-1)
            nc.gpsimd.affine_select(out=g.ident[:], in_=g.ident[:], compare_op=ALU.not_equal, fill=1.0,
                                    base=0, pattern=[[-1, P]], channel_multiplier=1)
            for i, scale in enumerate((float(D) ** -0.5, 1.0)):
                nc.gpsimd.memset(g.low_runs[:, i, :], scale)
            pool.drain()
            for i, width in enumerate((2 * C, C)):
                v = g.low_runs[:, i, :]
                nc.gpsimd.affine_select(out=v, in_=v, compare_op=ALU.is_ge, fill=0.0, base=-width,
                                        pattern=[[-2 * width, 4]], channel_multiplier=1)
            pool.drain()
            for i, width in enumerate((2 * C, C)):
                v = g.low_runs[:, i, :]
                nc.gpsimd.affine_select(out=v, in_=v, compare_op=ALU.is_ge, fill=0.0, base=2 * width - 1,
                                        pattern=[[2 * width, 4]], channel_multiplier=-1)\
                    .then_inc(g.consts_made, 1)

            def scale_of_rows(b, p):
                pool.wait_ge(moments_ready, b + 1)
                nc.gpsimd.tensor_tensor(rstd[:, p, :], moments[:, p, :, 1], bc(g.eps[:], 1, KD), ALU.add)
                pool.drain()
                nc.gpsimd.tensor_tensor(rstd[:, p, :], rstd[:, p, :], bc(g.neg_half[:], 1, KD), ALU.pow)\
                    .then_inc(rstd_ready, 1)

            pool.drain()
            with pool.Fori(0, B // 2) as j:
                for p in range(2):
                    scale_of_rows(j * 2 + p, p)

        @block.scalar
        def _(act):
            act.sem_inc(xf_copied, 1)
            act.sem_inc(cf_copied, 1)
            act.wait_ge(zeroed, 1)
            act.wait_ge(consts_in, 16 * 7)
            nc.scalar.mul(bias0, bias0, float(S)).then_inc(bias_ready, 1)

            def spectra_in(b, p):
                act.wait_ge(xf_done, b + 3)
                nc.scalar.copy(flat(xf[p]), xf_ps[:]).then_inc(xf_copied, 1)
                act.wait_ge(cf_done, b + 3)
                nc.scalar.copy(flat(cf[p]), cf_ps[:]).then_inc(cf_copied, 1)

            def sines(b, p):
                act.wait_ge(q_done, b + 1)
                act.wait_ge(spec_used, b + 1)
                nc.scalar.copy(qs[:, 1, :], q_ps[1][:, 0:D])
                act.wait_ge(kv_done, b * 2 + 2)
                nc.scalar.copy(ks[:, 1, :], kv_ps[1][:, 0:D])
                nc.scalar.copy(g.v_spec[:, ds(b, 1), 1, :], kv_ps[1][:, D:2 * D]).then_inc(act_copied, 1)

            spectra_in(0, 0)
            with act.Fori(0, B // 2 - 1) as j:
                for p in range(2):
                    spectra_in(j * 2 + p + 1, 1 - p)
                    sines(j * 2 + p, p)
            spectra_in(B - 1, 1)
            sines(B - 2, 0)
            sines(B - 1, 1)

        @block.vector
        def _(dve):
            dve.sem_inc(spec_used, 1)

            def normalise(b, p):
                dve.wait_ge(in_loaded[p], b * 16 + (32 - 16 * p))
                for t in range(KD):
                    nc.vector.bn_stats(stats[:, t, :], g.x[:, ds(b * KD + t, 1), :])
                dve.drain()
                for t in range(KD):
                    k = nc.vector.bn_aggr(moments[:, p, t, :], stats[:, t, :])
                k.then_inc(moments_ready, 1)
                dve.drain()
                dve.wait_ge(rstd_ready, b + 1)
                dve.wait_ge(xf_done, b + 1)
                for t in range(KD):
                    k = nc.vector.tensor_scalar(xn[p][:, t, :], g.x[:, ds(b * KD + t, 1), :],
                                                moments[:, p, t, 0:1], rstd[:, p, t:t + 1],
                                                ALU.subtract, ALU.mult)
                k.then_inc(xn_ready, 1)

            def cross_spectrum(b, p):
                dve.wait_ge(q_done, b + 1)
                nc.vector.tensor_tensor(qs[:, 0, :], q_ps[0][:, 0:D], bias0[:, 0:D], ALU.add)
                dve.wait_ge(kv_done, b * 2 + 1)
                nc.vector.tensor_tensor(ks[:, 0, :], kv_ps[0][:, 0:D], bias0[:, D:2 * D], ALU.add)
                nc.vector.tensor_tensor(g.v_spec[:, ds(b, 1), 0, :], kv_ps[0][:, D:2 * D],
                                        bias0[:, 2 * D:3 * D], ALU.add).then_inc(dve_copied, 1)
                dve.drain()
                dve.wait_ge(act_copied, b + 1)
                nc.vector.tensor_tensor(prod[:, 0:2, :], qs[:], ks[:], ALU.mult)
                nc.vector.tensor_tensor(prod[:, 2, :], qs[:, 0, :], ks[:, 1, :], ALU.mult)
                nc.vector.tensor_tensor(prod[:, 3, :], qs[:, 1, :], ks[:, 0, :], ALU.mult)\
                    .then_inc(spec_used, 1)
                dve.drain()
                nc.vector.tensor_reduce(summed[:], prod[:].rearrange("p a (h c) -> p a h c", c=C), AX, ALU.add)
                dve.drain()
                nc.vector.scalar_tensor_tensor(g.cross[:, 0, ds(b * H, H)], summed[:, 1, :], g.not_dc[:],
                                               summed[:, 0, :], ALU.mult, ALU.add)
                nc.vector.tensor_tensor(edge[:, 0, :], summed[:, 2, :], summed[:, 3, :], ALU.subtract)
                nc.vector.tensor_scalar(edge[:, 1, :], summed[:, 1, :], g.only_dc[:], None, ALU.mult)
                dve.drain()
                nc.vector.scalar_tensor_tensor(g.cross[:, 1, ds(b * H, H)], edge[:, 0, :], g.not_dc[:],
                                               edge[:, 1, :], ALU.mult, ALU.add)

            normalise(0, 0)
            normalise(1, 1)
            dve.wait_ge(bias_ready, 1)
            dve.wait_ge(g.consts_made, 2)
            nc.vector.tensor_reduce(g.low_rows[:], g.low_runs[:], AX, ALU.add)
            with dve.Fori(0, B // 2 - 1) as j:
                for p in range(2):
                    b = j * 2 + p
                    normalise(b + 2, p)
                    cross_spectrum(b, p)
            cross_spectrum(B - 2, 0)
            cross_spectrum(B - 1, 1)

        @block.tensor
        def _(pe):
            pe.sem_inc(xf_done, 2)
            pe.sem_inc(cf_done, 2)

            def forward(b, p):
                pe.wait_ge(xn_ready, b + 1)
                pe.wait_ge(xf_copied, b + 1)
                for c in range(KD):
                    for t in range(KD):
                        k = nc.tensor.matmul(xf_ps[:, c * S:(c + 1) * S], xn[p][:, t, c * P:(c + 1) * P],
                                             g.dft[:, t, :], start=t == 0, stop=t == KD - 1)
                k.then_inc(xf_done, 1)
                pe.wait_ge(in_loaded[p], b * 16 + (32 - 16 * p))
                pe.wait_ge(cf_copied, b + 1)
                for c in range(KD):
                    for t in range(KD):
                        k = nc.tensor.matmul(cf_ps[:, c * S:(c + 1) * S], ctx_in[p][:, t, c * P:(c + 1) * P],
                                             g.dft[:, t, :], start=t == 0, stop=t == KD - 1)
                k.then_inc(cf_done, 1)

            def project(b, p):
                pe.wait_ge(xf_copied, b + 2)
                wait_past_zero(pe, act_copied, b)
                wait_past_zero(pe, dve_copied, b)
                for f in range(2):
                    for c in range(KD):
                        k = nc.tensor.matmul(q_ps[f][:, 0:D], xf[p][:, c, f * P:(f + 1) * P],
                                             wq[:, c, :], start=c == 0, stop=c == KD - 1)
                k.then_inc(q_done, 1)
                pe.wait_ge(cf_copied, b + 2)
                for f in range(2):
                    for c in range(KD):
                        k = nc.tensor.matmul(kv_ps[f][:], cf[p][:, c, f * P:(f + 1) * P],
                                             wkv[:, c, :], start=c == 0, stop=c == KD - 1)
                    k.then_inc(kv_done, 1)

            pe.wait_ge(consts_in, 16 * 7)
            forward(0, 0)
            forward(1, 1)
            project(0, 0)
            with pe.Fori(1, B // 2) as j:
                for p in range(2):
                    b = j * 2 + p
                    forward(b, p)
                    project(b - 1, 1 - p)
            project(B - 1, 1)


def lags(nc, io, g):
    G2 = B // GROUP
    with Memory(nc) as m:
        corr = m.sb("corr", [P, G2, S + 8])
        left = m.sb("corr_left", [P, G2, S + 8])
        top8 = m.sb("top8", [P, G2, 8])
        best = m.sb("best", [P, G2, 8])
        neg_max = m.sb("neg_max", [P, G2])
        expd = m.sb("lag_exp", [P, G2, S])
        weight = m.sb("lag_weight", [P, G2, S])
        total = m.sb("lag_total", [P, G2])
        weight_t = m.sb("lag_weight_t", [P, KD, G2 * P])
        corr_ps = [m.bank(f"corr_ps{i}") for i in range(G2)]
        wt_ps, ws_ps = m.bank("wt_ps"), m.bank("ws_ps")
        corr_done, exp_in, exp_done = m.sem("b_corr_done"), m.sem("b_exp_in"), m.sem("b_exp_done")
        weight_ready, wt_done, wt_copied = m.sem("b_weight_ready"), m.sem("b_wt_done"), m.sem("b_wt_copied")
        ws_done = m.sem("b_ws_done")
        block = m.stack.enter_context(nc.Block())

        @block.sync
        def _(sp):
            load_expert0(sp, io, g, E - 1)

        @block.tensor
        def _(pe):
            pe.wait_ge(g.later_in, 16 * 7)
            for i in range(G2):
                for f in range(2):
                    k = nc.tensor.matmul(corr_ps[i][:, 0:S], g.cross[:, f, i * P:(i + 1) * P],
                                         g.icorr[:, f, :], start=f == 0, stop=f == 1)
                k.then_inc(corr_done, 1)
            for i in range(G2):
                pe.wait_ge(weight_ready, i + 1)
                for t in range(KD):
                    k = nc.tensor.transpose(wt_ps[:, t * G2 * P + i * P:t * G2 * P + (i + 1) * P],
                                            weight[:, i, t * P:(t + 1) * P], g.ident[:])
            k.then_inc(wt_done, 1)
            pe.wait_ge(wt_copied, 1)
            for f in range(2):
                for t in range(KD):
                    k = nc.tensor.matmul(ws_ps[:, f * B * H:(f + 1) * B * H], g.dft[:, t, f * P:(f + 1) * P],
                                         weight_t[:, t, :], start=t == 0, stop=t == KD - 1)
            k.then_inc(ws_done, 1)

        @block.scalar
        def _(act):
            act.wait_ge(g.later_in, 16 * 7)
            nc.scalar.activation(g.gates[:], g.gates[:], ACT.Tanh).then_inc(g.gates_ready, 1)
            for i in range(G2):
                act.wait_ge(exp_in, i + 1)
                nc.scalar.activation(expd[:, i, :], corr[:, i, 0:S], ACT.Exp, bias=neg_max[:, i:i + 1])\
                    .then_inc(exp_done, 1)
            act.wait_ge(wt_done, 1)
            nc.scalar.copy(flat(weight_t), wt_ps[:]).then_inc(wt_copied, 1)

        @block.vector
        def _(dve):
            nc.vector.memset(corr[:], LOWEST)
            nc.vector.memset(best[:], LOWEST)
            dve.drain()
            for i in range(G2):
                dve.wait_ge(corr_done, i + 1)
                nc.vector.tensor_copy(corr[:, i, 0:S], corr_ps[i][:, 0:S])
                dve.drain()
                nc.vector.max(top8[:, i, :], corr[:, i, 0:S])
                dve.drain()
                nc.vector.tensor_scalar(neg_max[:, i:i + 1], top8[:, i, 0:1], -1.0, None, ALU.mult)\
                    .then_inc(exp_in, 1)
                nc.vector.tensor_copy(best[:, i, 0:LAGS], top8[:, i, 0:LAGS])
                dve.drain()
                nc.vector.match_replace(left[:, i, :], best[:, i, :], corr[:, i, :], TAKEN)
            dve.drain()
            for i in range(G2):
                dve.wait_ge(exp_done, i + 1)
                nc.vector.scalar_tensor_tensor(weight[:, i, :], left[:, i, 0:S], (LOWEST + TAKEN) / 2,
                                               expd[:, i, :], ALU.is_lt, ALU.mult,
                                               accum_out=total[:, i:i + 1])
                dve.drain()
                nc.vector.reciprocal(total[:, i:i + 1], total[:, i:i + 1])
                dve.drain()
                nc.vector.tensor_scalar(weight[:, i, :], weight[:, i, :], total[:, i:i + 1], None, ALU.mult)\
                    .then_inc(weight_ready, 1)
            dve.wait_ge(ws_done, 1)
            nc.vector.tensor_copy(g.w_same[:, 0, :], ws_ps[:, 0:B * H])
            nc.vector.tensor_scalar(g.w_other[:, 1, :], ws_ps[:, B * H:2 * B * H], g.not_dc[:], None, ALU.mult)
            nc.vector.tensor_scalar(g.w_other[:, 0, :], ws_ps[:, B * H:2 * B * H], g.not_dc[:], -1.0,
                                    ALU.mult, ALU.mult)
            nc.vector.tensor_scalar(g.w_same[:, 1, :], ws_ps[:, B * H:2 * B * H], g.only_dc[:], None, ALU.mult)
            dve.drain()
            nc.vector.scalar_tensor_tensor(g.w_same[:, 1, :], g.w_same[:, 0, :], g.not_dc[:],
                                           g.w_same[:, 1, :], ALU.mult, ALU.add)


class Routing:

    def __init__(self, m, g, layer, xr_ps, small_ps):
        self.g, self.layer, self.xr_ps, self.small_ps = g, layer, xr_ps, small_ps
        n = f"r{layer}_"
        self.stats = m.sb(n + "stats", [P, KD, 6])
        self.moments = m.sb(n + "moments", [P, KD, 2])
        self.rstd = m.sb(n + "rstd", [P, KD])
        self.xr = [m.sb(n + f"xr{p}", [P, KD, D]) for p in range(2)]
        self.xrt = m.sb(n + "xrt", [P, KD, S])
        self.logits = m.sb(n + "logits", [P, KD, E])
        self.top_v = m.sb(n + "top_v", [P, KD, 8])
        self.top_f = m.sb(n + "top_f", [P, KD, TOPK])
        self.top_i = m.sb(n + "top_i", [P, KD, 8], u32)
        self.onehot = m.sb(n + "onehot", [P, KD, TOPK, E])
        self.mask = m.sb(n + "mask", [P, KD, E], bf16)
        self.rank = m.sb(n + "rank", [P, KD, E])
        self.pos_f = m.sb(n + "pos_f", [P, KD, TOPK, E])
        self.to = [m.sb(n + f"to{p}", [P, KD * TOPK], i32) for p in range(2)]
        self.pos_i = [m.sb(n + f"pos_i{p}", [P, KD * TOPK], i32) for p in range(2)]
        (self.moments_ready, self.rstd_ready, self.xr_ready, self.xrt_done, self.xrt_copied,
         self.logits_done, self.mask_ready, self.rank_done, self.pos_ready, self.seen_ready) = (
            m.sem(n + s) for s in ("moments_ready", "rstd_ready", "xr_ready", "xrt_done", "xrt_copied",
                                   "logits_done", "mask_ready", "rank_done", "pos_ready", "seen_ready"))
        self.scattered = [m.sem(n + f"scattered{p}") for p in range(2)]
        self.per_batch = 16 * (KD * TOPK + (1 if layer else 0))

    def vector_norm(self, nc, dve, b):
        for t in range(KD):
            nc.vector.bn_stats(self.stats[:, t, :], self.g.x[:, ds(b * KD + t, 1), :])
        dve.drain()
        for t in range(KD):
            k = nc.vector.bn_aggr(self.moments[:, t, :], self.stats[:, t, :])
        k.then_inc(self.moments_ready, 1)

    def vector_rows(self, nc, dve, b, p):
        dve.wait_ge(self.rstd_ready, b + 1)
        if not self.layer:
            nc.vector.reciprocal(self.rstd[:], self.rstd[:])
            dve.drain()
        if not isinstance(b, int) or b >= 2:
            dve.wait_ge(self.scattered[p], filled(b - 2, p, self.per_batch))
        for t in range(KD):
            k = nc.vector.tensor_scalar(self.xr[p][:, t, :], self.g.x[:, ds(b * KD + t, 1), :],
                                        self.moments[:, t, 0:1], self.rstd[:, t:t + 1],
                                        ALU.subtract, ALU.mult)
        k.then_inc(self.xr_ready, 1)

    def vector_pick(self, nc, dve, b):
        g = self.g
        dve.wait_ge(self.logits_done, b + 1)
        logits_ps = self.small_ps[:, 0:KD * E].rearrange("p (t e) -> p t e", e=E)
        if self.layer:
            nc.vector.tensor_tensor(self.logits[:], logits_ps, bc(g.router_b[:], 1, KD), ALU.add)
        else:
            nc.vector.tensor_copy(self.logits[:], logits_ps)
        dve.drain()
        for t in range(KD):
            nc.vector.max(self.top_v[:, t, :], self.logits[:, t, :])
        dve.drain()
        for t in range(KD):
            nc.vector.max_index(self.top_i[:, t, :], self.top_v[:, t, :], self.logits[:, t, :])
        nc.vector.tensor_copy(g.top_v[:, ds(b * KD, KD), :], self.top_v[:, :, 0:TOPK])
        dve.drain()
        nc.vector.tensor_copy(self.top_f[:], self.top_i[:, :, 0:TOPK])
        dve.drain()
        nc.vector.tensor_copy(g.top_f[:, ds(b * KD, KD), :], self.top_f[:])
        nc.vector.tensor_tensor(self.onehot[:].rearrange("p t k e -> p (t k) e"),
                                bc(g.expert_of[:].rearrange("p (a e) -> p a e", a=1), 1, KD * TOPK),
                                bc(self.top_f[:].rearrange("p t (k c) -> p (t k) c", c=1), 2, E), ALU.is_equal)
        dve.drain()
        nc.vector.tensor_tensor(self.mask[:], self.onehot[:, :, 0, :], self.onehot[:, :, 1, :], ALU.add)\
            .then_inc(self.mask_ready, 1)

    def vector_place(self, nc, dve, b, p):
        g = self.g
        dve.wait_ge(self.rank_done, b + 1)
        rank_ps = self.small_ps[:, 32:32 + KD * E].rearrange("p (t e) -> p t e", e=E)
        nc.vector.tensor_tensor(self.rank[:], rank_ps, bc(g.region_of[:].rearrange("p (a e) -> p a e", a=1), 1, KD),
                                ALU.add)
        nc.vector.tensor_tensor(g.seen[:], g.seen[:], self.mask[:, 0, :], ALU.add)
        dve.drain()
        nc.vector.tensor_tensor(g.seen[:], g.seen[:], self.mask[:, 1, :], ALU.add).then_inc(self.seen_ready, 1)
        for t in range(KD):
            nc.vector.tensor_tensor(self.pos_f[:, t, :, :], self.onehot[:, t, :, :],
                                    bc(self.rank[:, t:t + 1, :], 1, TOPK), ALU.mult)
        dve.drain()
        pos = g.pos[:, ds(b * KD, KD), :]
        nc.vector.tensor_reduce(pos, self.pos_f[:], AX, ALU.add)
        dve.drain()
        nc.vector.tensor_copy(self.pos_i[p][:].rearrange("p (t k) -> p t k", k=TOPK), pos)\
            .then_inc(self.pos_ready, 1)

    def gpsimd_rstd(self, nc, pool, b):
        pool.wait_ge(self.moments_ready, b + 1)
        nc.gpsimd.tensor_tensor(self.rstd[:], self.moments[:, :, 1], bc(self.g.eps[:], 1, KD), ALU.add)
        pool.drain()
        nc.gpsimd.tensor_tensor(self.rstd[:], self.rstd[:], bc(self.g.neg_half[:], 1, KD), ALU.pow)\
            .then_inc(self.rstd_ready, 1)

    def scalar_deviation(self, nc, act, b):
        act.wait_ge(self.moments_ready, b + 1)
        nc.scalar.activation(self.rstd[:], self.moments[:, :, 1], ACT.Sqrt, bias=self.g.eps[:])\
            .then_inc(self.rstd_ready, 1)

    def gpsimd_scatter(self, nc, pool, b, p):
        pool.wait_ge(self.pos_ready, b + 1)
        nc.gpsimd.tensor_tensor(self.to[p][:], self.pos_i[p][:], self.g.zero_i[:], ALU.add)
        pool.drain()
        for t in range(KD):
            for k in range(TOPK):
                at = t * TOPK + k
                pool.indirect_dma_start(
                    self.g.routed, bass.IndirectOffsetOnAxis(ap=self.to[p][:, at:at + 1], axis=0),
                    self.xr[p][:, t, :], None).then_inc(self.scattered[p], 16)
        if self.layer:
            pool.dma_start(
                self.g.routed[ds(b * S + E * REGION, S), :].rearrange("(t p) d -> p t d", p=P),
                self.xr[p][:]).then_inc(self.scattered[p], 16)

    def scalar(self, nc, act, b):
        act.wait_ge(self.xrt_done, b + 1)
        nc.scalar.copy(flat(self.xrt), self.xr_ps[:]).then_inc(self.xrt_copied, 1)

    def tensor_turn(self, nc, pe, b, p):
        g = self.g
        pe.wait_ge(self.xr_ready, b + 1)
        for t in range(KD):
            for c in range(KD):
                k = nc.tensor.transpose(self.xr_ps[:, c * S + t * P:c * S + (t + 1) * P],
                                        self.xr[p][:, t, c * P:(c + 1) * P], g.ident[:])
        k.then_inc(self.xrt_done, 1)

    def tensor_logits(self, nc, pe, b):
        g = self.g
        pe.wait_ge(self.xrt_copied, b + 1)
        pe.wait_ge(self.seen_ready, b + 1)
        router = g.router1 if self.layer else g.router0
        for t in range(KD):
            for c in range(KD):
                k = nc.tensor.matmul(self.small_ps[:, t * E:(t + 1) * E], self.xrt[:, c, t * P:(t + 1) * P],
                                     router[:, c, :], start=c == 0, stop=c == KD - 1)
        k.then_inc(self.logits_done, 1)

    def tensor_rank(self, nc, pe, b):
        g = self.g
        pe.wait_ge(self.mask_ready, b + 1)
        pe.wait_ge(self.seen_ready, b + 1)
        for t in range(KD):
            out = self.small_ps[:, 32 + t * E:32 + (t + 1) * E]
            nc.tensor.matmul(out, g.before[:], self.mask[:, t, :], start=True, stop=False)
            if t:
                nc.tensor.matmul(out, g.ones[:], self.mask[:, 0, :], start=False, stop=False)
            k = nc.tensor.matmul(out, g.ones[:], g.seen[:], start=False, stop=True)
        k.then_inc(self.rank_done, 1)


def mix(nc, io, g):
    with Memory(nc) as m:
        same = m.sb("same", [P, 2, D])
        other = m.sb("other", [P, 2, D])
        spec = [m.sb(f"out_spec{p}", [P, 2, D]) for p in range(2)]
        ot = m.sb("ot", [P, KD, S])
        one_row = m.sb("one_row", [1, P])
        ot_ps, y_ps, xr_ps, small_ps = m.bank("ot_ps"), m.bank("y_ps"), m.bank("xr_ps"), m.bank("small_ps")
        r = Routing(m, g, 0, xr_ps, small_ps)
        other_ready = m.sem("c_other_ready")
        spec_ready, ot_done, ot_copied = m.sem("c_spec_ready"), m.sem("c_ot_done"), m.sem("c_ot_copied")
        y_done, x_done, ones_ready = m.sem("c_y_done"), m.sem("c_x_done"), m.sem("c_ones_ready")
        block = m.stack.enter_context(nc.Block())

        def heads(ap):
            return ap.rearrange("p a (h c) -> p a h c", c=C)

        def per_head(w, b, a):
            return bc(w[:, a, ds(b * H, H)].rearrange("p (h c) -> p h c", c=1), 2, C)

        @block.gpsimd
        def _(pool):
            nc.gpsimd.memset(one_row[:], 1.0).then_inc(ones_ready, 1)

            def body(s, p):
                if active(s, 0):
                    pool.wait_ge(spec_ready, s + 1)
                    for a in range(2):
                        k = nc.gpsimd.tensor_tensor(
                            other[:, a, :].rearrange("p (h c) -> p h c", c=C),
                            g.v_spec[:, ds(s, 1), 1 - a, :].rearrange("p a (h c) -> p (a h) c", c=C),
                            per_head(g.w_other, s, a), ALU.mult)
                    k.then_inc(other_ready, 1)
                if active(s, 3):
                    r.gpsimd_scatter(nc, pool, s - 3, 1 - p)

            skewed(pool, 3, body)
            for p in range(2):
                pool.wait_ge(r.scattered[p], r.per_batch * (B // 2))

        @block.scalar
        def _(act):
            def body(s, p):
                if active(s, 1):
                    act.wait_ge(ot_done, s)
                    nc.scalar.copy(flat(ot), ot_ps[:]).then_inc(ot_copied, 1)
                if active(s, 2):
                    r.scalar(nc, act, s - 2)
                if active(s, 1):
                    r.scalar_deviation(nc, act, s - 1)

            act.preload_act_table(ACT.Sqrt)
            skewed(act, 3, body)

        @block.vector
        def _(dve):
            dve.sem_inc(spec_ready, 1)
            nc.vector.memset(g.seen[:], 0.0).then_inc(r.seen_ready, 1)

            def body(s, p):
                dve.drain()
                if active(s, 0):
                    for a in range(2):
                        nc.vector.tensor_tensor(
                            same[:, a, :].rearrange("p (h c) -> p h c", c=C),
                            g.v_spec[:, ds(s, 1), a, :].rearrange("p a (h c) -> p (a h) c", c=C),
                            per_head(g.w_same, s, a), ALU.mult)
                    dve.drain()
                if active(s, 3):
                    r.vector_place(nc, dve, s - 3, 1 - p)
                if active(s, 0):
                    dve.wait_ge(other_ready, s + 1)
                    nc.vector.tensor_tensor(spec[p][:], same[:], other[:], ALU.add).then_inc(spec_ready, 1)
                if active(s, 1):
                    b = s - 1
                    dve.wait_ge(y_done, b + 1)
                    xb = g.x[:, ds(b * KD, KD), :]
                    nc.vector.scalar_tensor_tensor(xb, y_ps[:].rearrange("p (t d) -> p t d", d=D),
                                                   g.gates[:, 0:1], xb, ALU.mult, ALU.add).then_inc(x_done, 1)
                    dve.drain()
                    r.vector_norm(nc, dve, b)
                if active(s, 2):
                    r.vector_pick(nc, dve, s - 2)
                if active(s, 1):
                    r.vector_rows(nc, dve, s - 1, 1 - p)

            skewed(dve, 3, body)

        @block.tensor
        def _(pe):
            pe.wait_ge(ones_ready, 1)

            def body(s, p):
                b = s - 1
                if active(s, 1):
                    pe.wait_ge(spec_ready, b + 2)
                    for c in range(KD):
                        for f in range(2):
                            k = nc.tensor.matmul(ot_ps[:, c * S:(c + 1) * S], spec[1 - p][:, f, c * P:(c + 1) * P],
                                                 g.iout[:, f, :], start=f == 0, stop=f == 1)
                    k.then_inc(ot_done, 1)
                if active(s, 3):
                    r.tensor_rank(nc, pe, s - 3)
                if active(s, 2):
                    r.tensor_turn(nc, pe, s - 2, p)
                if active(s, 1):
                    pe.wait_ge(ot_copied, b + 1)
                    wait_past_zero(pe, x_done, b)
                    for t in range(KD):
                        out = y_ps[:, t * D:(t + 1) * D]
                        nc.tensor.matmul(out, one_row[:], g.bo[0:1, :], start=True, stop=False)
                        for c in range(KD):
                            k = nc.tensor.matmul(out, ot[:, c, t * P:(t + 1) * P], g.wo0[:, c, :],
                                                 start=False, stop=c == KD - 1)
                    k.then_inc(y_done, 1)
                if active(s, 2):
                    r.tensor_logits(nc, pe, s - 2)

            skewed(pe, 3, body)


def load_biases(act, io, g, layer):
    names = ("L1_ffn_eb1", "L1_ffn_eb2") if layer else ("L0_ffn_b1", "L0_ffn_b2", "L0_ffn_b3")
    ups = len(names) - 1
    for e in range(E):
        for u, name in enumerate(names):
            at = (e * ups + u) * F
            dst, n = (g.down_bias[:, e, :], D) if u == ups else (g.v_flat[:, at:at + F], F)
            act.dma_start(dst, over_partitions(io[name][e], n)).then_inc(g.bias_in[layer], 16)


def plan(nc, io, g, layer):
    with Memory(nc) as m:
        n = f"p{layer}_"
        count = m.sb(n + "count", [P, E])
        tiles_i = m.sb(n + "tiles_i", [P, E], i32)
        tiles = m.sb(n + "tiles", [P, E])
        ends = m.sb(n + "ends", [P, E])
        shift = m.sb(n + "shift", [P, E])
        one = m.sb(n + "one", [P, E])
        over = m.sb(n + "over", [P, NT, E])
        work = m.sb(n + "work", [P, NT, E])
        plan_f = m.sb(n + "plan_f", [P, 4, NT])
        count_i = m.sb(n + "count_i", [P, E], i32)
        pick = m.sb(n + "pick", [P, NTT * TOPK, E])
        packed = m.sb(n + "packed", [P, NTT * TOPK])
        expd = m.sb(n + "expd", [P, NTT])
        count_ps = m.bank(n + "count_ps")
        counted, counts_ready, done = m.sem(n + "counted"), m.sem(n + "counts_ready"), m.sem(n + "done")
        diff_ready, exp_done = m.sem(n + "diff_ready"), m.sem(n + "exp_done")
        block = m.stack.enter_context(nc.Block())

        @block.tensor
        def _(pe):
            nc.tensor.matmul(count_ps[:, 0:E], g.ones[:], g.seen[:], start=True, stop=True).then_inc(counted, 1)

        @block.scalar
        def _(act):
            load_biases(act, io, g, layer)
            act.wait_ge(diff_ready, 1)
            nc.scalar.activation(expd[:], expd[:], ACT.Exp).then_inc(exp_done, 1)

        @block.sync
        def _(sp):
            sp.wait_ge(counts_ready, 1)
            for e in range(E):
                c = sp.value_load(count_i[0:1, e:e + 1], min_val=0, max_val=TOK)
                sp.dma_start(g.routed[ds(c + e * REGION, P), :], g.zeros[:]).then_inc(done, 16)
            sp.wait_ge(done, 16 * E)

        @block.vector
        def _(dve):
            v = nc.vector
            v.memset(one[:], 1.0)
            v.tensor_tensor(expd[:], g.top_v[:, :, 1], g.top_v[:, :, 0], ALU.subtract).then_inc(diff_ready, 1)
            dve.wait_ge(counted, 1)
            v.tensor_copy(count[:], count_ps[:, 0:E])
            dve.drain()
            v.tensor_copy(count_i[:], count[:]).then_inc(counts_ready, 1)
            v.tensor_scalar(tiles_i[:], count[:], float(P - 1), None, ALU.add)
            dve.drain()
            v.tensor_scalar(tiles_i[:], tiles_i[:], 7, None, ALU.arith_shift_right)
            dve.drain()
            v.tensor_copy(tiles[:], tiles_i[:])
            dve.drain()
            v.tensor_tensor_scan(ends[:], one[:], tiles[:], 0.0, ALU.mult, ALU.add)
            dve.drain()
            v.tensor_tensor(over[:], bc(g.tile_no[:].rearrange("p (n a) -> p n a", a=1), 2, E),
                            bc(ends[:].rearrange("p (a e) -> p a e", a=1), 1, NT), ALU.is_ge)
            v.tensor_tensor(shift[:], ends[:], tiles[:], ALU.subtract)
            dve.drain()
            v.tensor_reduce(plan_f[:, 0, :], over[:], AX, ALU.add)
            v.tensor_tensor(work[:], over[:], bc(tiles[:].rearrange("p (a e) -> p a e", a=1), 1, NT), ALU.mult)
            v.scalar_tensor_tensor(shift[:], shift[:], float(P), g.region_of[:], ALU.mult, ALU.subtract)
            dve.drain()
            v.tensor_reduce(plan_f[:, 1, :], work[:], AX, ALU.add)
            v.tensor_scalar(plan_f[:, 2, :], plan_f[:, 0, :], float(E), None, ALU.is_lt)
            v.tensor_scalar(plan_f[:, 3, :], plan_f[:, 0, :], float(E - 1), None, ALU.min)
            dve.drain()
            v.tensor_tensor(plan_f[:, 1, :], g.tile_no[:], plan_f[:, 1, :], ALU.subtract)
            dve.drain()
            v.scalar_tensor_tensor(plan_f[:, 1, :], plan_f[:, 1, :], float(P), plan_f[:, 2, :], ALU.mult, ALU.mult)
            dve.drain()
            v.scalar_tensor_tensor(plan_f[:, 1, :], plan_f[:, 3, :], float(REGION), plan_f[:, 1, :],
                                   ALU.mult, ALU.add)
            v.tensor_copy(g.plan[:, 0, 0:NT], plan_f[:, 3, :])
            dve.drain()
            v.tensor_copy(g.plan[:, 1, 0:NT], plan_f[:, 1, :])
            v.tensor_tensor(pick[:], bc(g.top_f[:].rearrange("p t (k a) -> p (t k) a", a=1), 2, E),
                            bc(g.expert_of[:].rearrange("p (a e) -> p a e", a=1), 1, NTT * TOPK), ALU.is_equal)
            dve.drain()
            v.tensor_tensor(pick[:], pick[:], bc(shift[:].rearrange("p (a e) -> p a e", a=1), 1, NTT * TOPK),
                            ALU.mult)
            dve.drain()
            v.tensor_reduce(packed[:], pick[:], AX, ALU.add)
            dve.drain()
            v.tensor_tensor(g.packed_i[:], packed[:], g.pos[:].rearrange("p t k -> p (t k)"), ALU.add)
            dve.drain()
            dve.wait_ge(exp_done, 1)
            v.tensor_scalar(packed[:, 0:NTT], expd[:], 1.0, None, ALU.add)
            dve.drain()
            v.reciprocal(packed[:, 0:NTT], packed[:, 0:NTT])
            dve.drain()
            v.tensor_scalar(g.share[:, 0, :], packed[:, 0:NTT], g.gates[:, 2 + layer:3 + layer], None, ALU.mult)
            dve.drain()
            v.tensor_tensor(g.share[:, 1, :], g.share[:, 0, :], expd[:], ALU.mult)


def experts(nc, io, g, layer):
    tiles = NT
    ups = 1 if layer else 2
    width = (ups * KD * F) + KF * D
    w = g.ffn_flat[:, 0:E * width].rearrange("p (e n) -> p e n", n=width)
    up_bias = g.v_flat[:, 0:E * ups * F].rearrange("p (e n) -> p e n", n=ups * F)
    with Memory(nc) as m:
        n = f"e{layer}_"
        xg = [m.sb(n + f"xg{p}", [P, D]) for p in range(2)]
        xt = [m.sb(n + f"xt{p}", [P, KD, P]) for p in range(2)]
        pre = m.sb(n + "pre", [P, F])
        lin = m.sb(n + "lin", [P, F])
        act_out = m.sb(n + "act_out", [P, F])
        h = m.sb(n + "h", [P, F])
        ht = [m.sb(n + f"ht{p}", [P, KF, P]) for p in range(2)]
        out = [m.sb(n + f"out{p}", [P, D]) for p in range(2)]
        up_ps = [[m.bank(n + f"up_ps{u}{p}") for p in range(2)] for u in range(ups)]
        xt_ps = m.bank(n + "xt_ps")
        ht_ps, out_ps = m.bank(n + "ht_ps"), m.bank(n + "out_ps")
        xg_loaded = [m.sem(n + f"xg_loaded{p}") for p in range(2)]
        stored = [m.sem(n + f"stored{p}") for p in range(2)]
        xt_done, xt_copied, up_done, pre_ready, act_done, h_ready, ht_done, ht_copied, out_done, out_ready = (
            m.sem(n + s) for s in ("xt_done", "xt_copied", "up_done", "pre_ready", "act_done", "h_ready",
                                   "ht_done", "ht_copied", "out_done", "out_ready"))
        block = m.stack.enter_context(nc.Block())

        @block.sync
        def _(sp):
            def body(s, p):
                if active(s, 0, tiles):
                    row = sp.value_load(g.plan[0:1, 1, ds(s, 1)], min_val=0, max_val=E * REGION - P)
                    if not isinstance(s, int) or s >= 2:
                        sp.wait_ge(xt_done, s - 1)
                    sp.dma_start(xg[p][:], g.routed[ds(row, P), :]).then_inc(xg_loaded[p], 16)

            if layer:
                for half in range(2):
                    load_expert1(sp, io, g, 2 * E, half)
            skewed(sp, 3, body, tiles)

        @block.gpsimd
        def _(pool):
            def body(s, p):
                if active(s, 3, tiles):
                    pool.wait_ge(out_ready, s - 2)
                    pool.dma_start(g.expert_out[layer][ds((s - 3) * P, P), :], out[1 - p][:])\
                        .then_inc(stored[1 - p], 16)

            skewed(pool, 3, body, tiles)
            for p in range(2):
                pool.wait_ge(stored[p], 16 * (tiles // 2))

        @block.scalar
        def _(act):
            act.preload_act_table(ACT.Gelu if layer else ACT.Silu)

            def body(s, p):
                if active(s, 2, tiles):
                    i = s - 2
                    act.wait_ge(ht_done, i + 1)
                    if not isinstance(i, int) or i >= 2:
                        act.wait_ge(out_done, i - 1)
                    nc.scalar.copy(flat(ht[p]), ht_ps[:]).then_inc(ht_copied, 1)
                if active(s, 0, tiles):
                    act.wait_ge(xt_done, s + 1)
                    nc.scalar.copy(flat(xt[p]), xt_ps[:, 0:D]).then_inc(xt_copied, 1)
                if active(s, 1, tiles):
                    i = s - 1
                    act.wait_ge(pre_ready, i + 1)
                    wait_past_zero(act, ht_done if layer else h_ready, i)
                    dst, func = (h, ACT.Gelu) if layer else (act_out, ACT.Silu)
                    nc.scalar.activation(dst[:], pre[:], func).then_inc(act_done, 1)

            skewed(act, 3, body, tiles)

        @block.vector
        def _(dve):
            dve.wait_ge(g.bias_in[layer], 16 * E * (ups + 1))

            def body(s, p):
                if active(s, 1, tiles):
                    i = s - 1
                    e = dve.value_load(g.plan[0:1, 0, ds(i, 1)], min_val=0, max_val=E - 1)
                    dve.wait_ge(up_done, i * ups + 1)
                    wait_past_zero(dve, act_done, i)
                    nc.vector.tensor_tensor(pre[:], up_ps[0][1 - p][:], up_bias[:, ds(e, 1), 0:F], ALU.add)\
                        .then_inc(pre_ready, 1)
                    if not layer:
                        dve.drain()
                        dve.wait_ge(up_done, i * ups + 2)
                        nc.vector.tensor_tensor(lin[:], up_ps[1][1 - p][:], up_bias[:, ds(e, 1), F:2 * F], ALU.add)
                        dve.drain()
                        dve.wait_ge(act_done, i + 1)
                        wait_past_zero(dve, ht_done, i)
                        nc.vector.tensor_tensor(h[:], act_out[:], lin[:], ALU.mult).then_inc(h_ready, 1)
                if active(s, 3, tiles):
                    i = s - 3
                    e = dve.value_load(g.plan[0:1, 0, ds(i, 1)], min_val=0, max_val=E - 1)
                    dve.wait_ge(out_done, i + 1)
                    if not isinstance(i, int) or i >= 2:
                        dve.wait_ge(stored[1 - p], filled(i - 2, 1 - p, 16))
                    nc.vector.tensor_tensor(out[1 - p][:], out_ps[:, 0:D], g.down_bias[:, ds(e, 1), :], ALU.add)\
                        .then_inc(out_ready, 1)

            skewed(dve, 3, body, tiles)

        @block.tensor
        def _(pe):
            pe.wait_ge(g.ffn1_in if layer else g.ffn_in, 16 * E * (ups + 1))

            def body(s, p):
                if active(s, 1, tiles):
                    i = s - 1
                    e = pe.value_load(g.plan[0:1, 0, ds(i, 1)], min_val=0, max_val=E - 1)
                    pe.wait_ge(xt_copied, i + 1)
                    for u in range(ups):
                        for c in range(KD):
                            at = (u * KD + c) * F
                            k = nc.tensor.matmul(up_ps[u][1 - p][:], xt[1 - p][:, c, :], w[:, ds(e, 1), at:at + F],
                                                 start=c == 0, stop=c == KD - 1)
                        k.then_inc(up_done, 1)
                if active(s, 2, tiles):
                    i = s - 2
                    pe.wait_ge(act_done if layer else h_ready, i + 1)
                    wait_past_zero(pe, ht_copied, i)
                    for f in range(KF):
                        k = nc.tensor.transpose(ht_ps[:, f * P:(f + 1) * P], h[:, f * P:(f + 1) * P], g.ident[:])
                    k.then_inc(ht_done, 1)
                if active(s, 0, tiles):
                    pe.wait_ge(xg_loaded[p], filled(s, p, 16))
                    wait_past_zero(pe, xt_copied, s)
                    for c in range(KD):
                        k = nc.tensor.transpose(xt_ps[:, c * P:(c + 1) * P], xg[p][:, c * P:(c + 1) * P],
                                                g.ident[:])
                    k.then_inc(xt_done, 1)
                if active(s, 3, tiles):
                    i = s - 3
                    e = pe.value_load(g.plan[0:1, 0, ds(i, 1)], min_val=0, max_val=E - 1)
                    pe.wait_ge(ht_copied, i + 1)
                    wait_past_zero(pe, out_ready, i)
                    for f in range(KF):
                        at = ups * KD * F + f * D
                        k = nc.tensor.matmul(out_ps[:, 0:D], ht[1 - p][:, f, :], w[:, ds(e, 1), at:at + D],
                                             start=f == 0, stop=f == KF - 1)
                    k.then_inc(out_done, 1)

            skewed(pe, 3, body, tiles)


def attention(nc, io, g, tail, room):
    QUAD = 4
    NQ = H // QUAD
    CV = 32
    bank_of = [h % 3 for h in range(H - 1)] + [1]
    RING = 2 * QUAD
    fr = mybir.dt.float32r
    k_slots, q_slots = (2, 3, 4, 12), (9, 11, 13, 15)
    with Memory(nc) as m:
        exps = [room.take(KD, S) for _ in range(RING)]
        eo = room.take(KD * TOPK, D)
        low = [room.take(2, S) for _ in range(2)]
        v = [room.take(KD, D) for _ in range(2)]
        out_t = g.wq_wk1
        wq4, wk4 = tail.take(KD, QUAD * D), tail.take(KD, QUAD * D)
        ctx_in = tail.take(KD, D)
        xn, xnt, ctxt = tail.take(KD, D), tail.take(KD, S), tail.take(KD, S)
        on, ont = tail.take(KD, D), tail.take(KD, S)
        idx = [m.sb(f"d_idx{p}", [P, KD * TOPK], i32) for p in range(2)]
        stats = m.sb("d_stats", [P, KD, 6])
        moments = m.sb("d_moments", [P, KD, 2])
        rstd = m.sb("d_rstd", [P, KD])
        q4 = [[m.sb(f"d_q4_{p}{j}", [P, 2, S], fr) for j in range(NQ)] for p in range(2)]
        k4 = [[m.sb(f"d_k4_{p}{j}", [P, 2, S], fr) for j in range(NQ)] for p in range(2)]
        neg_max = m.sb("d_neg_max", [P, RING, KD])
        sums = m.sb("d_sums", [P, 2, KD, QUAD])
        vp = [m.sb(f"d_vp{q}", [P, KD, QUAD, CV]) for q in range(2)]
        rden = m.sb("d_rden", [P, KD, H])
        t_ps = [m.bank(f"d_t_ps{i}") for i in range(2)]
        s_ps = [m.bank(f"d_s_ps{i}") for i in range(3)]
        o_ps = [m.bank(f"d_o_ps{i}") for i in range(2)]
        small_ps = m.bank("d_small_ps")
        r = Routing(m, g, 1, t_ps[1], small_ps)
        (moments_ready, rstd_ready, xn_ready, rows_used, scores_done, max_ready, exp_done, vp_ready,
         weighed, out_copied) = (
            m.sem("d_" + n) for n in ("moments_ready", "rstd_ready", "xn_ready", "rows_used", "scores_done",
                                      "max_ready", "exp_done", "vp_ready", "weighed", "out_copied"))
        ctx_loaded, gathered = m.sem("d_ctx_loaded"), m.sem("d_gathered")
        uses = [("ctx_t", 1, (1,), 0, 1), ("k", 1, (0,), 0, NQ), ("k", 1, (1,), 1, NQ), ("k", 1, (0,), 2, NQ),
                ("v", 1, (1,), 0, 1), ("values", 3, (0, 1), 0, 1), ("xn_t", 1, (0,), 0, 1),
                ("norm_t", 3, (1,), 0, 1), ("q", 1, (0,), 0, NQ), ("y", 3, (1,), 0, 1), ("q", 1, (0,), 1, NQ),
                ("k", 1, (1,), 3, NQ), ("q", 1, (0,), 2, NQ), ("route_t", 3, (1,), 0, 1),
                ("q", 1, (0,), 3, NQ)]
        names = sorted({u[0] for u in uses} - {"route_t"})
        made, taken = {n: m.sem(f"d_{n}_made") for n in names}, {n: m.sem(f"d_{n}_taken") for n in names}
        made["route_t"], taken["route_t"] = r.xrt_done, r.xrt_copied
        quads = [(u[0], u[3]) for u in uses if u[0] in "qk"]
        high_ready, weights_ready = m.sem("d_high_ready"), m.sem("d_weights_ready")
        block = m.stack.enter_context(nc.Block())

        def bank_for(name, j):
            return next(u[2][0] for u in uses if u[0] == name and u[3] == j)

        def wait_bank_free(pe, name, step, j=0):
            at = next(i for i, u in enumerate(uses) if u[0] == name and u[3] == j)
            for bank in uses[at][2]:
                for back in range(len(uses) * B):
                    i = at - 1 - back
                    past, i = -(i // len(uses)), i % len(uses)
                    before, stage, banks, which, of = uses[i]
                    st = step - past if past else step
                    if isinstance(st, int) and st < 0:
                        break
                    if bank in banks and active(st, stage):
                        pe.wait_ge(taken[before], (st - stage) * of + which + 1)
                        break

        @block.sync
        def _(sp):
            def body(s, p):
                if active(s, 0):
                    wait_past_zero(sp, made["ctx_t"], s)
                    sp.dma_start(ctx_in, io["ctx"][:, ds(s * KD, KD), :]).then_inc(ctx_loaded, 16)
                    load_expert1(sp, io, g, s - p, p)

            skewed(sp, 4, body)

        @block.gpsimd
        def _(pool):
            for q in range(2):
                nc.gpsimd.memset(vp[q][:], 0.0).then_inc(vp_ready, 1)
            pool.drain()

            def body(s, p):
                if active(s, 1):
                    pool.wait_ge(moments_ready, s)
                    nc.gpsimd.tensor_tensor(rstd[:], moments[:, :, 1], bc(g.eps[:], 1, KD), ALU.add)
                    pool.drain()
                    nc.gpsimd.tensor_tensor(rstd[:], rstd[:], bc(g.neg_half[:], 1, KD), ALU.pow)\
                        .then_inc(rstd_ready, 1)
                if active(s, 0):
                    pool.wait_ge(rows_used, s + 1)
                    nc.gpsimd.tensor_copy(idx[p][:], g.packed_i[:, ds(s * (KD * TOPK), KD * TOPK)])
                    pool.drain()
                    for at in range(KD * TOPK):
                        pool.indirect_dma_start(
                            eo[:, at, :], None, g.expert_out[0],
                            bass.IndirectOffsetOnAxis(ap=idx[p][:, at:at + 1], axis=0)).then_inc(gathered, 16)
                if active(s, 4):
                    r.gpsimd_scatter(nc, pool, s - 4, p)
                if active(s, 3):
                    r.gpsimd_rstd(nc, pool, s - 3)

            skewed(pool, 4, body)
            for p in range(2):
                pool.wait_ge(r.scattered[p], r.per_batch * (B // 2))

        @block.scalar
        def _(act):
            act.preload_act_table(ACT.Exp)

            def leave(name, n, dst, bank):
                act.wait_ge(made[name], n + 1)
                nc.scalar.copy(dst.rearrange("p a b -> p (a b)"), t_ps[bank][:]).then_inc(taken[name], 1)

            def high_parts(name, n, j):
                bank = bank_for(name, j)
                act.wait_ge(made[name], n * NQ + j + 1)
                mask = g.low_rows[:, 0:1] if name == "k" else g.low_rows[:, 1:2]
                nc.scalar.mul(low[bank].rearrange("p a b -> p (a b)").bitcast(fr), t_ps[bank][:], mask)\
                    .then_inc(high_ready, 1)

            def body(s, p):
                a, b, c = s - 1, s - 2, s - 3
                on1, on2, on3 = (active(s, stage) for stage in range(1, 4))
                for h in range(H):
                    if on2:
                        i, q = h % RING, h // QUAD % 2
                        act.wait_ge(max_ready, b * H + h + 1)
                        if not isinstance(b, int) or b > 0 or h >= RING:
                            act.wait_ge(weighed, b * NQ + h // QUAD - 1)
                        for t in range(KD):
                            k = nc.scalar.activation(exps[i][:, t, :], s_ps[bank_of[h]][:, t * S:(t + 1) * S],
                                                     ACT.Exp, bias=neg_max[:, i, t:t + 1],
                                                     accum_out=sums[:, q, t, h % QUAD:h % QUAD + 1])
                        k.then_inc(exp_done, 1)
                    if h == 0 and on1:
                        leave("ctx_t", a, ctxt, 1)
                    if h == 2 and on3:
                        act.wait_ge(weighed, c * NQ + NQ)
                        for half in range(2):
                            k = nc.scalar.copy(out_t[:, half * 2:half * 2 + 2, :].rearrange("p a b -> p (a b)"),
                                               o_ps[half][:])
                        k.then_inc(out_copied, 1)
                    if h in k_slots and on1:
                        high_parts("k", a, k_slots.index(h))
                    if h in q_slots and on1:
                        high_parts("q", a, q_slots.index(h))
                    if h == 5 and on1:
                        leave("v", a, v[1 - p], 1)
                    if h == 7 and on1:
                        leave("xn_t", a, xnt, 0)
                    if h == 8 and on3:
                        leave("norm_t", c, ont, 1)
                    if h == 14 and on3:
                        r.scalar(nc, act, c)

            skewed(act, 4, body)

        @block.vector
        def _(dve):
            dve.sem_inc(rows_used, 1)
            dve.wait_ge(g.attn1_in, 16 * 6)
            for n, dst in enumerate((wq4, wk4)):
                for c in range(KD):
                    k = nc.vector.tensor_copy(
                        dst[:, c, :].rearrange("p (h a c) -> p h a c", a=QUAD, c=C),
                        bc(g.wq_wk1[:, n * KD + c, :].rearrange("p (h a c) -> p h a c", a=1, c=C), 2, QUAD))
                k.then_inc(weights_ready, 1)
            nc.vector.memset(g.seen[:], 0.0).then_inc(r.seen_ready, 1)

            def scale_values(n, par, quad):
                q = quad % 2
                dve.wait_ge(exp_done, n * H + (quad + 1) * QUAD)
                if quad == 0:
                    dve.wait_ge(taken["v"], n + 1)
                nc.vector.reciprocal(sums[:, q, :, :], sums[:, q, :, :])
                dve.drain()
                by = sums[:, q, :, :].rearrange("p t (h a) -> p t h a", a=1)
                nc.vector.tensor_tensor(
                    vp[q][:, :, :, 0:C],
                    v[par][:, :, quad * QUAD * C:(quad + 1) * QUAD * C].rearrange("p t (h c) -> p t h c", c=C),
                    bc(by, 3, C), ALU.mult)
                nc.vector.tensor_copy(vp[q][:, :, :, C:C + 1], by).then_inc(vp_ready, 1)

            def combine(n):
                dve.wait_ge(gathered, (n + 1) * (16 * KD * TOPK))
                for k in range(TOPK):
                    for t in range(KD):
                        xb = g.x[:, ds(n * KD + t, 1), :]
                        last = nc.vector.scalar_tensor_tensor(
                            xb, eo[:, t * TOPK + k, :], g.share[:, k, ds(n * KD + t, 1)], xb,
                            ALU.mult, ALU.add)
                    if k == TOPK - 1:
                        last.then_inc(rows_used, 1)
                    dve.drain()
                for t in range(KD):
                    nc.vector.bn_stats(stats[:, t, :], g.x[:, ds(n * KD + t, 1), :])
                dve.drain()
                for t in range(KD):
                    k = nc.vector.bn_aggr(moments[:, t, :], stats[:, t, :])
                k.then_inc(moments_ready, 1)

            def low_parts(name, n, par, j):
                bank = bank_for(name, j)
                dve.wait_ge(high_ready, n * len(quads) + quads.index((name, j)) + 1)
                dst = (k4 if name == "k" else q4)[par][j]
                nc.vector.scalar_tensor_tensor(
                    flat(dst), t_ps[bank][:], float(D) ** -0.5 if name == "k" else 1.0,
                    low[bank].rearrange("p a b -> p (a b)"), ALU.mult, ALU.subtract).then_inc(taken[name], 1)

            def body(s, p):
                a, b, c, d = (s - stage for stage in range(1, 5))
                on1, on2, on3, on4 = (active(s, stage) for stage in range(1, 5))
                for h in range(H):
                    if on2:
                        dve.wait_ge(scores_done, b * H + h + 1)
                        nc.vector.tensor_reduce(neg_max[:, h % RING, :],
                                                s_ps[bank_of[h]][:].rearrange("p (t n) -> p t n", n=S),
                                                AX, ALU.max, negate=True).then_inc(max_ready, 1)
                    if h == 0 and on3:
                        scale_values(c, 1 - p, NQ - 1)
                    if h == 0 and on2:
                        low_parts("q", b, p, NQ - 1)
                    if h == 1 and on4:
                        r.vector_pick(nc, dve, d)
                    if h == 2 and on1:
                        combine(a)
                    if h == 4 and on4:
                        r.vector_place(nc, dve, d, p)
                    if h - 1 in k_slots and on1:
                        low_parts("k", a, 1 - p, k_slots.index(h - 1))
                    if h - 1 in q_slots and on1:
                        low_parts("q", a, 1 - p, q_slots.index(h - 1))
                    if h == 7 and on3:
                        dve.wait_ge(made["values"], c + 1)
                        for t in range(KD):
                            o = t_ps[t][:].rearrange("p (h c) -> p h c", c=CV)
                            nc.vector.reciprocal(rden[:, t, :], o[:, :, C])
                        dve.drain()
                        for t in range(KD):
                            o = t_ps[t][:].rearrange("p (h c) -> p h c", c=CV)
                            k = nc.vector.tensor_tensor(on[:, t, :].rearrange("p (h c) -> p h c", c=C), o[:, :, 0:C],
                                                        bc(rden[:, t, :].rearrange("p (h a) -> p h a", a=1), 2, C),
                                                        ALU.mult)
                        k.then_inc(taken["values"], 1)
                    if h in (5, 9, 13) and on2:
                        scale_values(b, p, h // QUAD - 1)
                    if h == 6 and on1:
                        dve.wait_ge(rstd_ready, a + 1)
                        for t in range(KD):
                            k = nc.vector.tensor_scalar(xn[:, t, :], g.x[:, ds(a * KD + t, 1), :],
                                                        moments[:, t, 0:1], rstd[:, t:t + 1],
                                                        ALU.subtract, ALU.mult)
                        k.then_inc(xn_ready, 1)
                    if h == 11 and on3:
                        dve.wait_ge(made["y"], c + 1)
                        xb = g.x[:, ds(c * KD, KD), :]
                        nc.vector.scalar_tensor_tensor(xb, t_ps[1][:].rearrange("p (t d) -> p t d", d=D),
                                                       g.gates[:, 1:2], xb, ALU.mult, ALU.add)\
                            .then_inc(taken["y"], 1)
                        dve.drain()
                        r.vector_norm(nc, dve, c)
                    if h == 13 and on3:
                        r.vector_rows(nc, dve, c, 1 - p)

            skewed(dve, 4, body)

        @block.tensor
        def _(pe):
            pe.wait_ge(g.attn1_in, 16 * 6)

            pe.wait_ge(weights_ready, 2)

            def product(name, s, out, lhs, rhs):
                wait_bank_free(pe, name, s)
                for i in range(KD):
                    for c in range(KD):
                        k = nc.tensor.matmul(out[:, i * 256:(i + 1) * 256], lhs[:, c, i * P:(i + 1) * P],
                                             rhs[:, c, :], start=c == 0, stop=c == KD - 1)
                k.then_inc(made[name], 1)

            def project(name, s, n, j, w, rhs):
                wait_bank_free(pe, name, s, j)
                bank = bank_for(name, j)
                for i in range(2):
                    at = (j * 2 + i) * P
                    for c in range(KD):
                        k = nc.tensor.matmul(t_ps[bank][:, i * S:(i + 1) * S], w[:, c, at:at + P],
                                             rhs[:, c, :], start=c == 0, stop=c == KD - 1)
                k.then_inc(made[name], 1)

            def turn_over(name, s, out, src):
                wait_bank_free(pe, name, s)
                for t in range(KD):
                    for c in range(KD):
                        k = nc.tensor.transpose(out[:, c * S + t * P:c * S + (t + 1) * P],
                                                src[:, t, c * P:(c + 1) * P], g.ident[:])
                k.then_inc(made[name], 1)

            def scores(n, par, h):
                r0 = h % 2 * 64
                if h % QUAD == 0:
                    pe.wait_ge(taken["q"], n * NQ + h // QUAD + 1)
                    pe.wait_ge(taken["k"], n * NQ + h // QUAD + 1)
                before = [b for b in range(-H, h) if bank_of[b % H] == bank_of[h]][-1]
                if not isinstance(n, int) or n > 0 or before >= 0:
                    pe.wait_ge(exp_done, n * H + before + 1)
                for t in range(KD):
                    k = nc.tensor.matmul(s_ps[bank_of[h]][:, t * S:(t + 1) * S],
                                         k4[par][h // QUAD][r0:r0 + 64, h % QUAD // 2, t * P:(t + 1) * P],
                                         q4[par][h // QUAD][r0:r0 + 64, h % QUAD // 2, :], start=True, stop=True)
                k.then_inc(scores_done, 1)

            def weigh(n, q):
                pe.wait_ge(vp_ready, n * NQ + q + 3)
                if q == 0 and (not isinstance(n, int) or n > 0):
                    pe.wait_ge(out_copied, n)
                for t in range(KD):
                    for i in range(QUAD):
                        k = nc.tensor.matmul(
                            o_ps[q // 2][i * CV:(i + 1) * CV, q % 2 * S:(q % 2 + 1) * S],
                            vp[q % 2][:, t, i, :], exps[(q % 2) * QUAD + i][:, t, :],
                            start=t == 0, stop=t == KD - 1)
                k.then_inc(weighed, 1)

            def body(s, p):
                a, b, c, d = (s - stage for stage in range(1, 5))
                on1, on2, on3, on4 = (active(s, stage) for stage in range(1, 5))
                for h in range(H):
                    if on2:
                        scores(b, p, h)
                    if h == 0 and on1:
                        pe.wait_ge(ctx_loaded, (a + 1) * 16)
                        turn_over("ctx_t", s, t_ps[1], ctx_in)
                    if h == 1 and on3:
                        weigh(c, NQ - 1)
                    if h in k_slots and on1:
                        if h == k_slots[0]:
                            pe.wait_ge(taken["ctx_t"], a + 1)
                        project("k", s, a, k_slots.index(h), wk4, ctxt)
                    if h == 3 and on4:
                        r.tensor_rank(nc, pe, d)
                    if h == 5 and on1:
                        product("v", s, t_ps[1], ctxt, g.wv1)
                    if h in (6, 10, 14) and on2:
                        weigh(b, h // QUAD - 1)
                    if h == 6 and on3:
                        wait_bank_free(pe, "values", s)
                        pe.wait_ge(out_copied, c + 1)
                        for t in range(KD):
                            for q in range(NQ):
                                k = nc.tensor.transpose(t_ps[t][:, q * P:(q + 1) * P],
                                                        out_t[:, q, t * P:(t + 1) * P], g.ident[:])
                        k.then_inc(made["values"], 1)
                    if h == 7 and on1:
                        pe.wait_ge(xn_ready, a + 1)
                        turn_over("xn_t", s, t_ps[0], xn)
                    if h == 8 and on3:
                        pe.wait_ge(taken["values"], c + 1)
                        turn_over("norm_t", s, t_ps[1], on)
                    if h in q_slots and on1:
                        if h == q_slots[0]:
                            pe.wait_ge(taken["xn_t"], a + 1)
                        project("q", s, a, q_slots.index(h), wq4, xnt)
                    if h == 10 and on3:
                        pe.wait_ge(taken["norm_t"], c + 1)
                        product("y", s, t_ps[1], ont, g.wo1)
                    if h == 14 and on3:
                        wait_bank_free(pe, "route_t", s)
                        r.tensor_turn(nc, pe, c, 1 - p)
                    if h == 15 and on3:
                        r.tensor_logits(nc, pe, c)

            skewed(pe, 4, body)


def shared_expert(nc, io, g):
    at = E * (KD * F + KF * D)
    w1 = g.ffn_flat[:, at:at + KD * F].rearrange("p (k n) -> p k n", k=KD)
    w2 = g.ffn_flat[:, at + KD * F:at + KD * F + KF * D].rearrange("p (k n) -> p k n", k=KF)
    with Memory(nc) as m:
        xg = [m.sb(f"s_xg{p}", [P, KD, D]) for p in range(2)]
        xt = [m.sb(f"s_xt{p}", [P, KD, S]) for p in range(2)]
        h = [m.sb(f"s_h{p}", [P, KF, S]) for p in range(2)]
        bias_rows = m.sb("s_bias_rows", [KF, P])
        up_bias, down_bias = m.sb("s_up_bias", [P, KF]), m.sb("s_down_bias", [P, 1, D])
        out = m.sb("s_out", [P, KD, D])
        idx = [m.sb(f"s_idx{p}", [P, KD * TOPK], i32) for p in range(2)]
        eo = [m.sb(f"s_eo{p}", [P, KD * TOPK, D]) for p in range(2)]
        up_ps = [[m.bank(f"s_up_ps{p}{i}") for i in range(2)] for p in range(2)]
        xt_ps, out_ps = m.bank("s_xt_ps"), [m.bank(f"s_out_ps{p}") for p in range(2)]
        bias_in, bias_turned, bias_ready = m.sem("s_bias_in"), m.sem("s_bias_turned"), m.sem("s_bias_ready")
        xg_loaded = [m.sem(f"s_xg_loaded{p}") for p in range(2)]
        gathered = [m.sem(f"s_gathered{p}") for p in range(2)]
        xt_done, xt_copied, up_done, h_ready, out_done, rows_used, x_ready, stored = (
            m.sem("s_" + n) for n in ("xt_done", "xt_copied", "up_done", "h_ready", "out_done", "rows_used",
                                      "x_ready", "stored"))
        block = m.stack.enter_context(nc.Block())

        @block.sync
        def _(sp):
            def body(s, p):
                if active(s, 0):
                    if not isinstance(s, int) or s >= 2:
                        sp.wait_ge(xt_done, s - 1)
                    sp.dma_start(xg[p][:], g.routed[ds(s * S + E * REGION, S), :]
                                 .rearrange("(t p) d -> p t d", p=P)).then_inc(xg_loaded[p], 16)

            skewed(sp, 2, body)

        @block.gpsimd
        def _(pool):
            def body(s, p):
                if active(s, 0):
                    if not isinstance(s, int) or s >= 2:
                        pool.wait_ge(rows_used, s - 1)
                    nc.gpsimd.tensor_copy(idx[p][:], g.packed_i[:, ds(s * (KD * TOPK), KD * TOPK)])
                    pool.drain()
                    for i in range(KD * TOPK):
                        pool.indirect_dma_start(
                            eo[p][:, i, :], None, g.expert_out[1],
                            bass.IndirectOffsetOnAxis(ap=idx[p][:, i:i + 1], axis=0)).then_inc(gathered[p], 16)

            skewed(pool, 2, body)

        @block.scalar
        def _(act):
            act.dma_start(bias_rows[:], io["L1_ffn_sb1"].rearrange("(k p) -> k p", p=P)).then_inc(bias_in, 16)
            act.dma_start(down_bias[:, 0, :], over_partitions(io["L1_ffn_sb2"], D)).then_inc(bias_in, 16)
            act.preload_act_table(ACT.Gelu)
            act.wait_ge(bias_ready, 1)

            def body(s, p):
                if active(s, 1):
                    b = s - 1
                    if not isinstance(b, int) or b >= 2:
                        act.wait_ge(out_done, b - 1)
                    for f in range(KF):
                        if f % 2 == 0:
                            act.wait_ge(up_done, b * 2 + f // 2 + 1)
                        k = nc.scalar.activation(h[1 - p][:, f, :],
                                                 up_ps[1 - p][f // 2][:, f % 2 * S:(f % 2 + 1) * S],
                                                 ACT.Gelu, bias=up_bias[:, f:f + 1])
                    k.then_inc(h_ready, 1)
                if active(s, 0):
                    act.wait_ge(xt_done, s + 1)
                    nc.scalar.copy(flat(xt[p]), xt_ps[:]).then_inc(xt_copied, 1)
                if active(s, 2):
                    b = s - 2
                    act.wait_ge(x_ready, b + 1)
                    act.dma_start(io["out"][:, ds(b * KD, KD), :], g.x[:, ds(b * KD, KD), :]).then_inc(stored, 16)

            skewed(act, 2, body, peel=4)
            act.wait_ge(stored, 16 * B)

        @block.vector
        def _(dve):
            dve.wait_ge(bias_turned, 1)
            nc.vector.tensor_copy(up_bias[:], xt_ps[:, 0:KF]).then_inc(bias_ready, 1)
            dve.wait_ge(bias_in, 16 * 2)

            def body(s, p):
                if active(s, 2):
                    b = s - 2
                    dve.wait_ge(gathered[p], filled(b, p, 16 * KD * TOPK))
                    for k in range(TOPK):
                        for t in range(KD):
                            xb = g.x[:, ds(b * KD + t, 1), :]
                            last = nc.vector.scalar_tensor_tensor(
                                xb, eo[p][:, t * TOPK + k, :], g.share[:, k, ds(b * KD + t, 1)], xb,
                                ALU.mult, ALU.add)
                        if k == TOPK - 1:
                            last.then_inc(rows_used, 1)
                        dve.drain()
                    dve.wait_ge(out_done, b + 1)
                    nc.vector.tensor_tensor(out[:], out_ps[p][:].rearrange("p (t d) -> p t d", d=D),
                                            bc(down_bias[:], 1, KD), ALU.add)
                    dve.drain()
                    xb = g.x[:, ds(b * KD, KD), :]
                    nc.vector.scalar_tensor_tensor(xb, out[:], g.gates[:, 3:4], xb, ALU.mult, ALU.add)\
                        .then_inc(x_ready, 1)

            skewed(dve, 2, body, peel=4)

        @block.tensor
        def _(pe):
            pe.wait_ge(bias_in, 16 * 2)
            nc.tensor.transpose(xt_ps[:, 0:KF], bias_rows[:], g.ident[0:KF, 0:KF]).then_inc(bias_turned, 1)
            pe.wait_ge(bias_ready, 1)
            pe.wait_ge(g.ffn1_in, 16 * 2 * (E + 1))

            def body(s, p):
                if active(s, 1):
                    b = s - 1
                    pe.wait_ge(xt_copied, b + 1)
                    for f in range(KF):
                        for c in range(KD):
                            k = nc.tensor.matmul(up_ps[1 - p][f // 2][:, f % 2 * S:(f % 2 + 1) * S],
                                                 w1[:, c, f * P:(f + 1) * P], xt[1 - p][:, c, :],
                                                 start=c == 0, stop=c == KD - 1)
                        if f % 2:
                            k.then_inc(up_done, 1)
                if active(s, 0):
                    pe.wait_ge(xg_loaded[p], filled(s, p, 16))
                    wait_past_zero(pe, xt_copied, s)
                    for t in range(KD):
                        for c in range(KD):
                            k = nc.tensor.transpose(xt_ps[:, c * S + t * P:c * S + (t + 1) * P],
                                                    xg[p][:, t, c * P:(c + 1) * P], g.ident[:])
                    k.then_inc(xt_done, 1)
                if active(s, 2):
                    b = s - 2
                    pe.wait_ge(h_ready, b + 1)
                    if not isinstance(b, int) or b >= 2:
                        pe.wait_ge(x_ready, b - 1)
                    for t in range(KD):
                        for f in range(KF):
                            k = nc.tensor.matmul(out_ps[p][:, t * D:(t + 1) * D], h[p][:, f, t * P:(t + 1) * P],
                                                 w2[:, f, :], start=f == 0, stop=f == KF - 1)
                    k.then_inc(out_done, 1)

            skewed(pe, 2, body, peel=4)


def build(nc, io, upto=99):
    with Memory(nc) as g:
        g.routed = nc.dram_tensor("routed_rows", [(E + 1) * REGION, D], f32, kind="Internal").ap()
        g.expert_out = [nc.dram_tensor(f"expert_rows{n}", [NT * P, D], f32, kind="Internal").ap()
                        for n in range(2)]
        g.x = g.sb("x", [P, NTT, D])
        g.ffn = g.sb("ffn", [P, E, 2 * KD * F + KF * D])
        g.ffn_flat = g.ffn[:].rearrange("p e n -> p (e n)")
        g.v_spec = g.sb("v_spec", [P, B, 2, D])
        g.v_flat = g.v_spec[:].rearrange("p b a d -> p (b a d)")
        g.ident = g.sb("ident", [P, P])
        g.ones = g.sb("ones", [P, P], bf16)
        g.before = g.sb("before", [P, P], bf16)
        g.zeros = g.sb("zeros", [P, D])
        g.neg_half, g.eps = g.sb("neg_half", [P, 1]), g.sb("eps", [P, 1])
        g.zero_i = g.sb("zero_i", [P, KD * TOPK], i32)
        g.not_dc, g.only_dc = g.sb("not_dc", [P, 1]), g.sb("only_dc", [P, 1])
        g.low_rows = g.sb("low_rows", [P, 2])
        g.low_runs = g.sb("low_runs", [P, 2, 4])
        g.expert_of, g.region_of = g.sb("expert_of", [P, E]), g.sb("region_of", [P, E])
        g.tile_no = g.sb("tile_no", [P, NT])
        g.gates = g.sb("gates", [P, 4])
        g.bo = g.sb("bo", [P, D])
        g.router0, g.router1 = g.sb("router0", [P, KD, E]), g.sb("router1", [P, KD, E])
        g.router_b = g.sb("router_b", [P, 1, E])
        g.seen = g.sb("seen", [P, E], bf16)
        g.top_v, g.top_f = g.sb("top_v", [P, NTT, TOPK]), g.sb("top_f", [P, NTT, TOPK])
        g.pos = g.sb("pos", [P, NTT, TOPK])
        g.packed_i = g.sb("packed_i", [P, NTT * TOPK], i32)
        g.share = g.sb("share", [P, TOPK, NTT])
        g.plan = g.sb("plan", [P, 2, NT], i32)
        g.consts_made, g.later_in, g.ffn_in = g.sem("consts_made"), g.sem("later_in"), g.sem("ffn_in")
        g.bias_in = [g.sem(f"bias_in{n}") for n in range(2)]
        g.gates_ready, g.attn1_in, g.ffn1_in = g.sem("gates_ready"), g.sem("attn1_in"), g.sem("ffn1_in")

        with Memory(nc) as m0:
            g.dft, g.icorr = m0.sb("dft", [P, KD, S]), m0.sb("icorr", [P, 2, S])
            g.iout, g.wo0 = m0.sb("iout", [P, 2, S]), m0.sb("wo0", [P, KD, D])
            g.cross = m0.sb("cross", [P, 2, B * H])
            g.w_same, g.w_other = m0.sb("w_same", [P, 2, B * H]), m0.sb("w_other", [P, 2, B * H])
            spectra(nc, io, g)
            if upto > 1: lags(nc, io, g)
            if upto > 2: mix(nc, io, g)
        with Memory(nc) as m0:
            g.down_bias = m0.sb("down_bias0", [P, E, D])
            if upto > 3: plan(nc, io, g, 0)
            if upto > 4: experts(nc, io, g, 0)
        tail, room = Carved(g.ffn_flat, E * (KD * F + KF * D)), Carved(g.v_flat, 0)
        g.wv1, g.wo1 = tail.take(KD, D), tail.take(KD, D)
        g.wq_wk1 = room.take(2 * KD, D)
        if upto > 5: load_layer1(nc, io, g)
        if upto > 5: attention(nc, io, g, tail, room)
        with Memory(nc) as m1:
            g.down_bias = m1.sb("down_bias1", [P, E, D])
            if upto > 6: plan(nc, io, g, 1)
            if upto > 7: experts(nc, io, g, 1)
        if upto > 8: shared_expert(nc, io, g)


def load_layer1(nc, io, g):
    with nc.Block() as block:
        @block.sync
        def _(sp):
            for dst, name in ((g.wq_wk1[:, 0:KD, :], "L1_xattn_Wq"), (g.wq_wk1[:, KD:, :], "L1_xattn_Wk"),
                              (g.wv1, "L1_xattn_Wv"), (g.wo1, "L1_xattn_Wo")):
                sp.dma_start(dst[:], rows(io[name])).then_inc(g.attn1_in, 16)
            sp.dma_start(g.router1[:], rows(io["L1_ffn_router_w"])).then_inc(g.attn1_in, 16)
            sp.dma_start(g.router_b[:, 0, :], over_partitions(io["L1_ffn_router_b"], E)).then_inc(g.attn1_in, 16)


TRANSPOSED = ("L0_xattn_Wq", "L0_xattn_Wk", "L0_xattn_Wv", "L0_xattn_Wo", "L0_ffn_Wg", "L0_ffn_W1", "L0_ffn_W2",
              "L0_ffn_W3", "L1_xattn_Wq", "L1_xattn_Wk", "L1_xattn_Wv", "L1_xattn_Wo")


def transforms():
    t = np.arange(S)
    w = 2 * np.pi * np.outer(t, np.arange(S // 2)) / S
    cos, sin = np.cos(w), np.sin(w)
    sin[:, 0] = np.cos(np.pi * t)
    two = np.full(S // 2, 2.0 / S)
    two[0] = 1.0 / S
    sign = np.full(S // 2, -1.0)
    sign[0] = 1.0
    forward = np.concatenate([cos, sin], 1)
    from_cross = np.concatenate([cos * two, sin * two * sign], 1).T / C
    from_spectrum = np.concatenate([cos * two, sin * two], 1).T
    return {n: np.ascontiguousarray(a, np.float32)
            for n, a in (("dft", forward), ("icorr", from_cross), ("iout", from_spectrum))}


def kernel(**inputs):
    import concourse.bacc as bacc
    from concourse.bass_utils import run_bass_kernel_spmd

    nc = bacc.Bacc("TRN2", target_bir_lowering=False, num_devices=1)
    arrays = {}
    for name, a in inputs.items():
        a = np.asarray(a)
        arrays[name] = np.ascontiguousarray(np.swapaxes(a, -1, -2) if name in TRANSPOSED else a)
    arrays.update(transforms())
    io = {n: nc.dram_tensor(n, a.shape, mybir.dt.from_np(a.dtype), kind="ExternalInput").ap()
          for n, a in arrays.items()}
    out = nc.dram_tensor("out", (B, S, D), f32, kind="ExternalOutput").ap()
    by_tile = "b (t p) d -> p (b t) d"
    io["x"] = io["x"].rearrange(by_tile, p=P)
    io["ctx"] = io["ctx_1024"].rearrange(by_tile, p=P)
    io["out"] = out.rearrange(by_tile, p=P)
    build(nc, io)
    r = run_bass_kernel_spmd(nc, [arrays], core_ids=[0])
    return r.results[0]["out"]
```
